# Optimizing a Trainium2 kernel written in Bass

```python
import numpy as np
import jax
import jax.numpy as jnp

def _softmax(x, axis=-1):
    return jax.nn.softmax(x, axis=axis)

def _gelu(x):
    return jax.nn.gelu(x, approximate=True)

def _silu(x):
    return jax.nn.silu(x)

def _sigmoid(x):
    return jax.nn.sigmoid(x)

def _layernorm(x, axis=-1, eps=1e-05):
    m = jnp.mean(x, axis=axis, keepdims=True)
    v = jnp.var(x, axis=axis, keepdims=True)
    return (x - m) / jnp.sqrt(v + eps)

def _scatter_add(tgt, idx, src, axis=0):
    return tgt.at[idx].add(src)

def _segment_sum(src, seg, n):
    return jax.ops.segment_sum(src, seg, n)
kernel_name = 'mk_xattn_ffn_d1_seqx_r4_ee4aad'

def setup_inputs(seed: int=0):
    np.random.seed(seed)
    _w = jnp.asarray

    def _rec_inputs():
        import jax
        import jax.numpy as jnp
        _rk = jax.random.key(seed)
        x = 6.313e-05 + 0.9998 * jax.random.normal(jax.random.fold_in(_rk, 1), (4, 1024, 256), jnp.float32)
        _lenS = 1024 - jax.random.randint(jax.random.fold_in(_rk, 7), (4,), 0, max(1, 1024 // 4) + 1, jnp.int32)
        _lenS2 = 77 - jax.random.randint(jax.random.fold_in(_rk, 8), (4,), 0, max(1, 77 // 4) + 1, jnp.int32)
        _ctx_1024P = jax.random.normal(jax.random.fold_in(_rk, 11), (4, 16, 256), jnp.float32)
        _ctx_1024c = jax.random.dirichlet(jax.random.fold_in(_rk, 511), 0.3 * jnp.ones((16,), jnp.float32), (4, 77))
        _ctx_1024t = jnp.einsum('bsk,bkd->bsd', _ctx_1024c, _ctx_1024P)
        _ctx_1024t = _ctx_1024t * jax.lax.rsqrt(jnp.mean(jnp.square(_ctx_1024t)) + 1e-12) * 0.953939
        ctx_1024 = -0.000214406 + 1.00034 * (_ctx_1024t + 0.3 * jax.random.normal(jax.random.fold_in(_rk, 611), (4, 77, 256), jnp.float32))
        return (x, ctx_1024)
    x, ctx_1024 = _rec_inputs()

    def _L0_xattn_setup():
        import jax, jax.numpy as jnp
        import numpy as np
        from jax import lax
        BIG = jnp.float32(1e+30)

        def _pairwise_euclidean(a, b):
            aa = jnp.sum(a * a, axis=-1)[:, None]
            bb = jnp.sum(b * b, axis=-1)[None, :]
            ab = a @ b.T
            return jnp.sqrt(jnp.maximum(aa + bb - 2.0 * ab, 0.0))

        def _dtw_cost(D):
            row0 = jnp.cumsum(D[0])

            def row_step(prev_row, d_row):
                first = d_row[0] + prev_row[0]

                def col_step(left, inp):
                    d_ij, up, diag = inp
                    r = d_ij + jnp.minimum(jnp.minimum(up, left), diag)
                    return (r, r)
                _, rest = lax.scan(col_step, first, (d_row[1:], prev_row[1:], prev_row[:-1]))
                row = jnp.concatenate([first[None], rest])
                return (row, row)
            _, rows = lax.scan(row_step, row0, D[1:])
            return jnp.concatenate([row0[None], rows], axis=0)

        def _backtrack(R, T1, T2):
            L = T1 + T2 - 1

            def step(carry, _):
                i, j, done = carry
                valid = jnp.logical_not(done)
                cd = jnp.where((i > 0) & (j > 0), R[jnp.maximum(i - 1, 0), jnp.maximum(j - 1, 0)], BIG)
                cu = jnp.where(i > 0, R[jnp.maximum(i - 1, 0), j], BIG)
                cl = jnp.where(j > 0, R[i, jnp.maximum(j - 1, 0)], BIG)
                choice = jnp.argmin(jnp.stack([cd, cu, cl]))
                ni = jnp.where(choice <= 1, i - 1, i)
                nj = jnp.where((choice == 0) | (choice == 2), j - 1, j)
                at_origin = (i == 0) & (j == 0)
                ni = jnp.where(at_origin, 0, ni)
                nj = jnp.where(at_origin, 0, nj)
                return ((ni, nj, done | at_origin), (i, j, valid))
            init = (jnp.int32(T1 - 1), jnp.int32(T2 - 1), jnp.bool_(False))
            _, (i_idx, j_idx, valid) = lax.scan(step, init, None, length=L)
            return (i_idx, j_idx, valid)

        def _align_one(small, large):
            T_small, d = small.shape
            T_large = large.shape[0]
            D = _pairwise_euclidean(small, large)
            R = _dtw_cost(D)
            i_idx, j_idx, valid = _backtrack(R, T_small, T_large)
            contrib = small[i_idx] * valid[:, None].astype(small.dtype)
            expanded = jnp.zeros((T_large, d), dtype=small.dtype).at[j_idx].add(contrib)
            return expanded
        key = jax.random.key(seed)
        k1, k2 = jax.random.split(key)
        teacher = jax.random.normal(k1, (16, 100, 256), dtype=jnp.float32)
        student = jax.random.normal(k2, (16, 150, 256), dtype=jnp.float32)
        return {'teacher_features': teacher, 'student_features': student}
    _L0_xattn_all = _L0_xattn_setup()
    _L0_xattn_in = {k: v for k, v in _L0_xattn_all.items() if k in ()}
    del _L0_xattn_all

    def _L0_ffn_setup():
        import jax, jax.numpy as jnp
        import numpy as np
        DIM = 256
        E = 16
        TOPK = 2
        G = 4
        TOPK_G = 2
        INTER = 128
        N_SHARED = 2
        ROUTE_SCALE = 1.0

        def _gate(xf, gate_w, gate_b):
            scores = xf @ gate_w.T
            scores = jax.nn.softmax(scores.astype(jnp.float32), axis=-1)
            orig = scores
            scores = scores + gate_b
            T = xf.shape[0]
            sg = scores.reshape(T, G, E // G)
            group_scores = jax.lax.top_k(sg, 2)[0].sum(-1)
            _, gidx = jax.lax.top_k(group_scores, TOPK_G)
            keep = jax.nn.one_hot(gidx, G).sum(axis=1) > 0
            sg = jnp.where(keep[:, :, None], sg, -jnp.inf)
            scores = sg.reshape(T, E)
            _, idx = jax.lax.top_k(scores, TOPK)
            weights = jnp.take_along_axis(orig, idx, axis=1)
            weights = (weights * ROUTE_SCALE).astype(xf.dtype)
            return (weights, idx)
        key = jax.random.key(seed)
        ks = jax.random.split(key, 16)
        s = lambda fan_in: 1.0 / np.sqrt(fan_in)
        inp = {'x': jax.random.normal(ks[0], (4, 256, DIM), dtype=jnp.float32), 'gate_w': jax.random.normal(ks[1], (E, DIM), dtype=jnp.float32) * s(DIM), 'gate_b': jnp.zeros((E,), dtype=jnp.float32), 'We1': jax.random.normal(ks[2], (E, DIM, INTER), dtype=jnp.float32) * s(DIM), 'be1': jnp.zeros((E, INTER), dtype=jnp.float32), 'We2': jax.random.normal(ks[3], (E, INTER, DIM), dtype=jnp.float32) * s(INTER), 'be2': jnp.zeros((E, DIM), dtype=jnp.float32), 'We3': jax.random.normal(ks[4], (E, DIM, INTER), dtype=jnp.float32) * s(DIM), 'be3': jnp.zeros((E, INTER), dtype=jnp.float32), 'ws1': jax.random.normal(ks[5], (DIM, N_SHARED * INTER), dtype=jnp.float32) * s(DIM), 'bs1': jnp.zeros((N_SHARED * INTER,), dtype=jnp.float32), 'ws2': jax.random.normal(ks[6], (N_SHARED * INTER, DIM), dtype=jnp.float32) * s(N_SHARED * INTER), 'bs2': jnp.zeros((DIM,), dtype=jnp.float32), 'ws3': jax.random.normal(ks[7], (DIM, N_SHARED * INTER), dtype=jnp.float32) * s(DIM), 'bs3': jnp.zeros((N_SHARED * INTER,), dtype=jnp.float32)}
        return inp
    _L0_ffn_all = _L0_ffn_setup()
    _L0_ffn_in = {k: v for k, v in _L0_ffn_all.items() if k in ('gate_w', 'gate_b', 'We1', 'be1', 'We2', 'be2', 'We3', 'be3', 'ws1', 'bs1', 'ws2', 'bs2', 'ws3', 'bs3')}
    del _L0_ffn_all
    return {'x': x, 'ctx_1024': ctx_1024, 'L0_ffn_gate_w': _L0_ffn_in['gate_w'], 'L0_ffn_gate_b': _L0_ffn_in['gate_b'], 'L0_ffn_We1': _L0_ffn_in['We1'], 'L0_ffn_be1': _L0_ffn_in['be1'], 'L0_ffn_We2': _L0_ffn_in['We2'], 'L0_ffn_be2': _L0_ffn_in['be2'], 'L0_ffn_We3': _L0_ffn_in['We3'], 'L0_ffn_be3': _L0_ffn_in['be3'], 'L0_ffn_ws1': _L0_ffn_in['ws1'], 'L0_ffn_bs1': _L0_ffn_in['bs1'], 'L0_ffn_ws2': _L0_ffn_in['ws2'], 'L0_ffn_bs2': _L0_ffn_in['bs2'], 'L0_ffn_ws3': _L0_ffn_in['ws3'], 'L0_ffn_bs3': _L0_ffn_in['bs3']}

def reference(x, ctx_1024, L0_ffn_gate_w, L0_ffn_gate_b, L0_ffn_We1, L0_ffn_be1, L0_ffn_We2, L0_ffn_be2, L0_ffn_We3, L0_ffn_be3, L0_ffn_ws1, L0_ffn_bs1, L0_ffn_ws2, L0_ffn_bs2, L0_ffn_ws3, L0_ffn_bs3):
    import jax
    import jax.numpy as jnp

    def _L0_xattn_ref(teacher_features, student_features):
        import jax, jax.numpy as jnp
        import numpy as np
        from jax import lax
        BIG = jnp.float32(1e+30)

        def _pairwise_euclidean(a, b):
            aa = jnp.sum(a * a, axis=-1)[:, None]
            bb = jnp.sum(b * b, axis=-1)[None, :]
            ab = a @ b.T
            return jnp.sqrt(jnp.maximum(aa + bb - 2.0 * ab, 0.0))

        def _dtw_cost(D):
            row0 = jnp.cumsum(D[0])

            def row_step(prev_row, d_row):
                first = d_row[0] + prev_row[0]

                def col_step(left, inp):
                    d_ij, up, diag = inp
                    r = d_ij + jnp.minimum(jnp.minimum(up, left), diag)
                    return (r, r)
                _, rest = lax.scan(col_step, first, (d_row[1:], prev_row[1:], prev_row[:-1]))
                row = jnp.concatenate([first[None], rest])
                return (row, row)
            _, rows = lax.scan(row_step, row0, D[1:])
            return jnp.concatenate([row0[None], rows], axis=0)

        def _backtrack(R, T1, T2):
            L = T1 + T2 - 1

            def step(carry, _):
                i, j, done = carry
                valid = jnp.logical_not(done)
                cd = jnp.where((i > 0) & (j > 0), R[jnp.maximum(i - 1, 0), jnp.maximum(j - 1, 0)], BIG)
                cu = jnp.where(i > 0, R[jnp.maximum(i - 1, 0), j], BIG)
                cl = jnp.where(j > 0, R[i, jnp.maximum(j - 1, 0)], BIG)
                choice = jnp.argmin(jnp.stack([cd, cu, cl]))
                ni = jnp.where(choice <= 1, i - 1, i)
                nj = jnp.where((choice == 0) | (choice == 2), j - 1, j)
                at_origin = (i == 0) & (j == 0)
                ni = jnp.where(at_origin, 0, ni)
                nj = jnp.where(at_origin, 0, nj)
                return ((ni, nj, done | at_origin), (i, j, valid))
            init = (jnp.int32(T1 - 1), jnp.int32(T2 - 1), jnp.bool_(False))
            _, (i_idx, j_idx, valid) = lax.scan(step, init, None, length=L)
            return (i_idx, j_idx, valid)

        def _align_one(small, large):
            T_small, d = small.shape
            T_large = large.shape[0]
            D = _pairwise_euclidean(small, large)
            R = _dtw_cost(D)
            i_idx, j_idx, valid = _backtrack(R, T_small, T_large)
            contrib = small[i_idx] * valid[:, None].astype(small.dtype)
            expanded = jnp.zeros((T_large, d), dtype=small.dtype).at[j_idx].add(contrib)
            return expanded
        return jax.vmap(_align_one)(teacher_features, student_features)

    def _L0_ffn_ref(x, gate_w, gate_b, We1, be1, We2, be2, We3, be3, ws1, bs1, ws2, bs2, ws3, bs3):
        import jax, jax.numpy as jnp
        import numpy as np
        DIM = 256
        E = 16
        TOPK = 2
        G = 4
        TOPK_G = 2
        INTER = 128
        N_SHARED = 2
        ROUTE_SCALE = 1.0

        def _gate(xf, gate_w, gate_b):
            scores = xf @ gate_w.T
            scores = jax.nn.softmax(scores.astype(jnp.float32), axis=-1)
            orig = scores
            scores = scores + gate_b
            T = xf.shape[0]
            sg = scores.reshape(T, G, E // G)
            group_scores = jax.lax.top_k(sg, 2)[0].sum(-1)
            _, gidx = jax.lax.top_k(group_scores, TOPK_G)
            keep = jax.nn.one_hot(gidx, G).sum(axis=1) > 0
            sg = jnp.where(keep[:, :, None], sg, -jnp.inf)
            scores = sg.reshape(T, E)
            _, idx = jax.lax.top_k(scores, TOPK)
            weights = jnp.take_along_axis(orig, idx, axis=1)
            weights = (weights * ROUTE_SCALE).astype(xf.dtype)
            return (weights, idx)
        shape = x.shape
        xf = x.reshape(-1, DIM)
        weights, idx = _gate(xf, gate_w, gate_b)
        combine = (jax.nn.one_hot(idx, E, dtype=xf.dtype) * weights[..., None]).sum(1)
        h1 = jnp.einsum('td,edi->tei', xf, We1) + be1
        h3 = jnp.einsum('td,edi->tei', xf, We3) + be3
        h = jax.nn.silu(h1) * h3
        yo = jnp.einsum('tei,eid->ted', h, We2) + be2
        y = jnp.einsum('te,ted->td', combine, yo)
        z = jax.nn.silu(xf @ ws1 + bs1) * (xf @ ws3 + bs3) @ ws2 + bs2
        return (y + z).reshape(shape)
    x = x + _L0_xattn_ref(ctx_1024, _layernorm(x, axis=-1))
    x = x + _L0_ffn_ref(_layernorm(x, axis=-1), L0_ffn_gate_w, L0_ffn_gate_b, L0_ffn_We1, L0_ffn_be1, L0_ffn_We2, L0_ffn_be2, L0_ffn_We3, L0_ffn_be3, L0_ffn_ws1, L0_ffn_bs1, L0_ffn_ws2, L0_ffn_bs2, L0_ffn_ws3, L0_ffn_bs3)
    return x

_drawn_inputs = setup_inputs


def setup_inputs(seed=0):
    import zlib

    import numpy as np

    out = dict(_drawn_inputs(seed))
    spreads = {'L0_ffn_gate_b': (0.0, 0.1),
     'L0_ffn_be1': (0.0, 0.694),
     'L0_ffn_be2': (0.0, 0.431),
     'L0_ffn_be3': (0.0, 0.706),
     'L0_ffn_bs1': (0.0, 0.1),
     'L0_ffn_bs2': (0.0, 0.1),
     'L0_ffn_bs3': (0.0, 0.1)}
    factors = {}
    for name, (base, spread) in spreads.items():
        noise = np.random.default_rng([zlib.crc32(name.encode()), seed]).standard_normal(out[name].shape)
        drawn = base * np.exp(spread * noise) if base else spread * noise
        out[name] = jnp.asarray(drawn.astype(out[name].dtype))
    for name, factor in factors.items():
        out[name] = (out[name] * factor).astype(out[name].dtype)
    return out
```

```python
import concourse.bass as bass
from concourse import mybir

ALU = mybir.AluOpType
ACT = mybir.ActivationFunctionType
AX = mybir.AxisListType
F32 = mybir.dt.float32
BF16 = mybir.dt.bfloat16
I32 = mybir.dt.int32

P = 128
QUAD = 32
B, S, D = 4, 1024, 256
CTX = 77
KC = D // P
CH = S // QUAD
W = CH + 1
NT = CTX + QUAD - 1
TILES = B * S // P
TOK = B * S
E = 16
G = 4
I = 128
MS = 2
SLOT_TILES = 80
SLOTS = SLOT_TILES * P
ROW = D + 1
DUMP = 2 * TOK
BIG = 1e30
EPS = 1e-5


def build(nc, x, ctx, gate_w, gate_b, we1, be1, we2, be2, we3, be3, ws1, bs1, ws2, bs2, ws3, bs3, out):
    def sb(name, shape, dt=F32):
        return nc.alloc_sbuf_tensor(name, shape, dt)

    def ps(name, shape, dt=F32):
        return nc.alloc_psum_tensor(name, shape, dt)

    def sem(name):
        return nc.alloc_semaphore(name)

    cost_skew = nc.dram_tensor("cost_skew", (P, NT * W), F32, kind="Internal").ap()
    mask_skew = nc.dram_tensor("mask_skew", (P, NT * CH), BF16, kind="Internal").ap()

    slot_rows = nc.dram_tensor("slot_rows", (SLOTS, ROW), F32, kind="Internal").ap()
    results = nc.dram_tensor("results", (DUMP, D), F32, kind="Internal").ap()

    top = [(nc.sbuf_base + 63) // 64 * 64]

    def size(shape, dt):
        n = 2 if dt is BF16 else 4
        for k in shape[1:]:
            n *= k
        return (n + 31) // 32 * 32

    def place(name, shape, dt=F32, at=None):
        cursor = top if at is None else at
        off = cursor[0]
        cursor[0] = off + size(shape, dt)
        assert cursor[0] <= nc.sbuf_usable_end, (name, cursor[0])
        return nc.alloc_sbuf_tensor_at(name, shape, dt, offset=off)

    ident = place("ident", [P, P])
    identb = place("identb", [P, P], BF16)
    ones = place("ones", [P, QUAD])
    stats = place("stats", [P, CH, 6])
    sm = place("sm", [P, 10, CH])
    first_chunk = place("first_chunk", [P, 1])
    last_chunk = place("last_chunk", [P, 1])
    eps = place("eps", [P, 1])
    xk = place("xk", [P, CH, D])
    w13 = place("w13", [P, KC, E, 2 * I])
    w2 = place("w2", [P, E, D])
    sw1 = place("sw1", [P, KC, MS * I])
    sw3 = place("sw3", [P, KC, MS * I])
    sw2 = place("sw2", [P, MS, D])
    sb1 = place("sb1", [P, MS])
    sb3 = place("sb3", [P, MS])
    gwT = place("gwT", [P, KC, E])
    gb = place("gb", [P, E])
    fill = place("fill", [P, ROW])
    tri = place("tri", [P, P], BF16)
    onesb = place("onesb", [P, P], BF16)
    gw = place("gw", [E, D])
    ids = place("ids", [P, 2, TILES], I32)
    slot = place("slot", [P, 2, TILES], I32)
    wt = place("wt", [P, 2, TILES])
    etab = place("etab", [P, SLOT_TILES], I32)
    idx = place("idx", [P, 8], I32)
    low_e = place("low_e", [P, G, G])
    rev_e = place("rev_e", [P, E])
    full = place("full", [P, TILES])
    tile_no = place("tile_no", [P, SLOT_TILES])

    low = top[0]
    cost = place("cost", [P, CTX, W])
    r_at = top[0]
    R = place("R", [P, NT + 1, W])
    m_at = top[0]
    M = place("M", [P, NT, W])
    cst_at = top[0]
    cst = place("cst", [P, NT, W])
    f_at = top[0]
    F = place("F", [P, NT, W])
    v_at = top[0]
    V = place("V", [P, NT + 1, W])
    a_at = top[0]
    A = place("A", [P, NT + 1, W], BF16)
    xT = place("xT", [P, 2, KC, 4, P])
    ctx_sb = place("ctx_sb", [CTX, B, D])
    ctx_rest = place("ctx_rest", [CTX, B, D])
    ctxT = place("ctxT", [P, KC, B, CTX])
    aa_diag = place("aa_diag", [CTX, B, CTX])
    front_end = top[0]
    aa = place("aa", [CTX, B])
    aa_row = place("aa_row", [P, CTX])
    carry = place("carry", [P, NT + 1])
    ctx_parts = place("ctx_parts", [CTX, 3, B, D], BF16)
    root = place("root", [P, CTX, W], at=[v_at])
    half = place("half", [P, CTX, W], at=[f_at])
    zeros = place("zeros", [P, W * 16], at=[m_at])
    cursor = [r_at]
    mask = place("mask", [P, NT, CH], BF16, at=cursor)
    maskU = place("maskU", [P, CTX, CH], BF16, at=cursor)
    maskT = place("maskT", [CTX, P, CH], BF16, at=[m_at])
    cursor = [low]
    orig, score, t1, t2, t3, oh1, oh2 = (place(n, [P, TILES, E], at=cursor)
                                         for n in ("orig", "score", "t1", "t2", "t3", "oh1", "oh2"))
    ohb = place("ohb", [P, TILES, E], BF16, at=cursor)
    cnt = place("cnt", [P, E, TILES], at=cursor)
    keep_on = place("keep_on", [P, E, TILES], at=cursor)
    upto = place("upto", [P, E, TILES], at=cursor)
    r1, r2, r3 = (place(n, [P, TILES], at=cursor) for n in ("r1", "r2", "r3"))
    gs, gk, gp = (place(n, [P, TILES, G], at=cursor) for n in ("gs", "gk", "gp"))
    te, tend, tbase, one_e = (place(n, [P, E], at=cursor) for n in ("te", "tend", "tbase", "one_e"))
    big_e = place("big_e", [P, SLOT_TILES, E], at=cursor)
    assert cursor[0] <= cst_at
    cursor = [low]
    b13 = place("b13", [P, E, 2 * I], at=cursor)
    b2 = place("b2", [P, E, D], at=cursor)
    hb = place("hb", [P, 2, 2 * I], at=cursor)
    sg = place("sg", [P, 2, I], at=cursor)
    hg = place("hg", [P, 2, I], at=cursor)
    hgT = place("hgT", [P, 2, P], at=cursor)
    assert cursor[0] <= cst_at
    cursor = [cst_at]
    x2T = place("x2T", [P, KC, TOK], at=cursor)
    silu = place("silu", [P, 2, MS, 512], at=cursor)
    assert cursor[0] <= a_at
    cursor = [a_at]
    x2n = place("x2n", [P, 4, D], at=cursor)
    lin = place("lin", [P, 512], at=cursor)
    bs2b = place("bs2b", [P, D], at=cursor)
    stage = place("stage", [P, 2, 2, ROW], at=cursor)
    xs = place("xs", [P, 4, ROW], at=cursor)
    xsT = place("xsT", [P, 2, KC, P], at=cursor)
    ys = place("ys", [P, 8, D], at=cursor)
    assert cursor[0] <= front_end, (cursor[0], front_end)
    back = place("back", [P, 2, 4, 2, D], at=[m_at])

    psT = [[ps(f"psT{h}{c}", [P, 4, P]) for c in range(KC)] for h in range(2)]
    psD = [ps(f"psD{h}", [P, 4, P]) for h in range(2)]
    psC = [ps(f"psC{i}", [P, 512]) for i in range(2)]

    psL = psD[0][:, :, :].rearrange("p a b -> p (a b)").rearrange("p (t e) -> p t e", e=E)
    psX = [psD[h][:, 0:2, :].rearrange("p a b -> p (a b)") for h in range(2)]
    psG = [psC[h][:, 0:P] for h in range(2)]
    psH = [psT[0][h][:, 0:2, :].rearrange("p a b -> p (a b)") for h in range(2)]
    psY = [psT[1][h][:, 0:2, :].rearrange("p a b -> p (a b)") for h in range(2)]
    w13f = w13[:, :, :, :].rearrange("p c e i -> p (c e i)")
    w2f = w2[:, :, :].rearrange("p e d -> p (e d)")
    b13f = b13[:, :, :].rearrange("p e i -> p (e i)")
    b2f = b2[:, :, :].rearrange("p e d -> p (e d)")
    EARLY = 6

    def live(i, c):
        return not isinstance(i, int) or 0 <= 8 * i + c < SLOT_TILES

    def head(i, c):
        return isinstance(i, int) and 8 * i + c < 0

    def load_expert(eng, regs, i, c):
        eng.reg_load(regs[c % 4], etab[0:1, bass.ds(8 * i + c, 1)])

    def expert(eng, regs, c):
        return eng.snap(regs[c % 4], min_val=0, max_val=(E - 1) * D)

    def pipeline(eng, step):
        for c in range(-1, 15):
            step(0, c)
        with eng.Fori(1, SLOT_TILES // 8 - 1) as i:
            for c in range(7, 15):
                step(i, c)
        for c in range(SLOT_TILES - 1, SLOT_TILES + 3):
            step(0, c)

    x_loaded = [sem(f"x_loaded{g}") for g in range(4)]
    ctx_loaded = sem("ctx_loaded")
    pads_zeroed = sem("pads_zeroed")
    const_ready = sem("const_ready")
    pool_step = sem("pool_step")
    dve_step = sem("dve_step")
    act_step = sem("act_step")
    var_ready = sem("var_ready")
    std_ready = sem("std_ready")
    norm_ready = sem("norm_ready")
    xn_act = sem("xn_act")
    xn_pool = sem("xn_pool")
    ctx_turned = sem("ctx_turned")
    ctxT_ready = sem("ctxT_ready")
    aa_ready = sem("aa_ready")
    aa_spread = sem("aa_spread")
    aa_done = sem("aa_done")
    turned = sem("turned")
    xT_act = sem("xT_act")
    xT_dve = sem("xT_dve")
    dist_ready = sem("dist_ready")
    dist_used = sem("dist_used")
    clipped = sem("clipped")
    rooted = sem("rooted")
    cost_ready = sem("cost_ready")
    cost_out = sem("cost_out")
    cost_in = sem("cost_in")
    mask_ready = sem("mask_ready")
    mask_out = sem("mask_out")
    mask_in = sem("mask_in")
    mask_turned = sem("mask_turned")
    maskT_ready = sem("maskT_ready")
    parts_ready = sem("parts_ready")
    x_nat = sem("x_nat")
    gathered = sem("gathered")
    x2_ready = sem("x2_ready")
    out_done = sem("out_done")
    xn_read = sem("xn_read")
    names = ("weights_loaded gate_turned gate_ready biases_loaded biases1_loaded filled fill_ready var2_ready "
             "std2_ready norm2_ready xn2_ready x2_turned x2T_ready logits_ready shifted expd oh_ready counted "
             "routed staged h_ready silu_ready act_ready z_ready z_used x_turned xT_copied h_done hb_ready "
             "silu_done gated g_turned hgT_copied y_done y_read id_copied combined etab_ready shared_small tail_in0 "
             "tail_in1").split()
    globals_ = {n: sem(n) for n in names}
    (weights_loaded, gate_turned, gate_ready, biases_loaded, biases1_loaded, filled, fill_ready, var2_ready,
     std2_ready, norm2_ready, xn2_ready, x2_turned, x2T_ready, logits_ready, shifted, expd, oh_ready, counted,
     routed, staged, h_ready, silu_ready, act_ready, z_ready, z_used, x_turned, xT_copied, h_done, hb_ready,
     silu_done, gated, g_turned, hgT_copied, y_done, y_read, id_copied, combined, etab_ready, shared_small,
     tail_in0, tail_in1) = (globals_[n] for n in names)
    tail_in = [tail_in0, tail_in1]
    scattered = [sem(f"scattered{i}") for i in range(2)]
    xs_loaded = [sem(f"xs_loaded{i}") for i in range(4)]
    res_out = [sem(f"res_out{i}") for i in range(8)]
    zeros_ready = sem("zeros_ready")
    lin_ready = sem("lin_ready")
    passed = sem("passed")

    xk_dram = x.rearrange("b (c k) d -> (b c) k d", k=CH)
    xn_dram = x.rearrange("b (t p) d -> p (b t) d", p=P)
    out_nat = out.rearrange("b (t p) d -> p (b t) d", p=P)

    def skewed(base, row, n_rows, r0):
        return bass.AP(tensor=base.tensor, offset=r0 * row,
                       ap=[[QUAD * NT * row, B], [NT * row + row, QUAD], [1, n_rows * row]])

    with nc.Block() as block:

        @block.sync
        def _(sp):
            for g in range(4):
                sp.dma_start(xk[:, 8 * g:8 * g + 8, :], xk_dram[:, 8 * g:8 * g + 8, :]).then_inc(x_loaded[g], 16)
            sp.dma_start(gw[:, :], gate_w).then_inc(weights_loaded, 16)
            sp.wait_ge(zeros_ready, 1)
            for n in range(0, NT, 16):
                k = min(16, NT - n)
                sp.dma_start(cost_skew[:, n * W:(n + k) * W], zeros[:, 0:k * W]).then_inc(pads_zeroed, 16)
            sp.wait_ge(pads_zeroed, 16 * ((NT + 15) // 16))
            sp.wait_ge(cost_ready, 1)
            for b in range(B):
                dst = bass.AP(tensor=cost_skew.tensor, offset=b * QUAD * NT * W,
                              ap=[[(NT + 1) * W, QUAD], [1, CTX * W]])
                sp.dma_start(dst, cost[QUAD * b:QUAD * b + QUAD, :, :].rearrange("p i w -> p (i w)")
                             ).then_inc(cost_out, 16)
            sp.wait_ge(cost_out, 16 * B)
            sp.dma_start(cst[:, :, :].rearrange("p t w -> p (t w)"), cost_skew[:, :]).then_inc(cost_in, 16)
            for c in range(KC):
                for w, lo in ((we1, 0), (we3, I)):
                    sp.dma_start(w13[:, c, :, lo:lo + I], w[:, c * P:(c + 1) * P, :].rearrange("e p i -> p e i")
                                 ).then_inc(biases1_loaded, 16)
            sp.dma_start(w2[:, :, :], we2.rearrange("e p d -> p e d")).then_inc(biases1_loaded, 16)
            sp.dma_start(sw1[:, :, :], ws1.rearrange("(c p) i -> p c i", p=P)).then_inc(shared_small, 16)
            sp.dma_start(sw3[:, :, :], ws3.rearrange("(c p) i -> p c i", p=P)).then_inc(shared_small, 16)
            sp.dma_start(sw2[:, :, :], ws2.rearrange("(c p) d -> p c d", p=P)).then_inc(shared_small, 16)
            with nc.allow_non_contiguous_dma(reason="two columns of biases"):
                sp.dma_start(sb1[:, :], bs1.rearrange("(m p) -> p m", p=P)).then_inc(shared_small, 16)
                sp.dma_start(sb3[:, :], bs3.rearrange("(m p) -> p m", p=P)).then_inc(shared_small, 16)
            sp.dma_start(gb[:, :], gate_b.partition_broadcast(P)).then_inc(shared_small, 16)
            sp.wait_ge(fill_ready, 2)
            for n in range(SLOT_TILES):
                sp.dma_start(slot_rows[n * P:(n + 1) * P, :], fill[:, :]).then_inc(filled, 16)
            sp.wait_ge(turned, 8)
            for g in range(4):
                sp.dma_start(xk[:, 8 * g:8 * g + 8, :], xn_dram[:, 8 * g:8 * g + 8, :]).then_inc(x_nat, 16)
            sp.wait_ge(mask_ready, 1)
            sp.dma_start(mask_skew[:, :], mask[:, :, :].rearrange("p t w -> p (t w)")).then_inc(mask_out, 16)
            sp.wait_ge(mask_out, 16)
            for b in range(B):
                src = bass.AP(tensor=mask_skew.tensor, offset=b * QUAD * NT * CH,
                              ap=[[(NT + 1) * CH, QUAD], [1, CTX * CH]])
                sp.dma_start(maskU[QUAD * b:QUAD * b + QUAD, :, :].rearrange("p i w -> p (i w)"),
                             src).then_inc(mask_in, 16)
            sp.dma_start(bs2b[:, :], bs2.partition_broadcast(P)).then_inc(lin_ready, 16)
            sp.wait_ge(routed, 1)
            sp.wait_ge(etab_ready, 1)
            sp.dma_start(b13[:, :, 0:I], be1.partition_broadcast(P)).then_inc(biases_loaded, 16)
            sp.dma_start(b13[:, :, I:2 * I], be3.partition_broadcast(P)).then_inc(biases_loaded, 16)
            sp.dma_start(b2[:, :, :], be2.partition_broadcast(P)).then_inc(biases_loaded, 16)

            def load_slots(i, u):
                sp.dma_start(xs[:, u, :], slot_rows[bass.ds((4 * i + u) * P, P), :]).then_inc(xs_loaded[u], 16)

            for w in range(2):
                sp.wait_ge(scattered[w], 16 * TILES)
            for u in range(4):
                load_slots(0, u)
            with sp.Fori(1, SLOT_TILES // 4) as i:
                for u in range(4):
                    sp.wait_ge(x_turned, 4 * i + u - 3)
                    sp.wait_ge(id_copied, 4 * i + u - 3)
                    load_slots(i, u)
            for u in range(8):
                sp.wait_ge(res_out[u], 16 * (SLOT_TILES // 8))
            for g in range(8):
                if g >= 2:
                    sp.wait_ge(combined, 4 * (g - 1))
                for w in range(2):
                    src = results[w * TOK + g * 4 * P:w * TOK + (g + 1) * 4 * P, :].rearrange("(t p) d -> p t d", p=P)
                    sp.dma_start(back[:, g % 2, :, w, :], src).then_inc(tail_in[g % 2], 16)
                if g >= 1:
                    sp.wait_ge(combined, 4 * g)
                    sp.dma_start(out_nat[:, 4 * g - 4:4 * g, :], xk[:, 4 * g - 4:4 * g, :]).then_inc(out_done, 16)
            sp.wait_ge(combined, 32)
            sp.dma_start(out_nat[:, 28:32, :], xk[:, 28:32, :]).then_inc(out_done, 16)
            sp.wait_ge(out_done, 16 * 8)

        @block.gpsimd
        def _(pool):
            pool.memset(zeros[:, :], 0.0).then_inc(zeros_ready, 1)
            pool.memset(ident[:, :], 0.0).then_inc(pool_step, 1)
            pool.memset(ones[:, :], 1.0).then_inc(const_ready, 1)
            pool.wait_ge(pool_step, 1)
            pool.affine_select(out=ident[:, :], in_=ident[:, :], compare_op=ALU.not_equal, fill=1.0, base=0,
                               pattern=[[-1, P]], channel_multiplier=1).then_inc(const_ready, 1)
            pool.memset(onesb[:, :], 1.0).then_inc(pool_step, 1)
            pool.memset(tri[:, :], 1.0).then_inc(pool_step, 1)
            pool.memset(low_e[:, :, :], 1.0).then_inc(pool_step, 1)
            pool.wait_ge(pool_step, 4)
            pool.affine_select(out=tri[:, :], in_=tri[:, :], compare_op=ALU.is_gt, fill=0.0, base=0,
                               pattern=[[1, P]], channel_multiplier=-1).then_inc(const_ready, 1)
            pool.affine_select(out=low_e[:, :, :], in_=low_e[:, :, :], compare_op=ALU.is_gt, fill=0.0, base=0,
                               pattern=[[1, G], [-1, G]], channel_multiplier=0).then_inc(const_ready, 1)
            pool.iota(rev_e[:, :], [[-1, E]], base=E, channel_multiplier=0,
                      allow_small_or_imprecise_dtypes=True).then_inc(const_ready, 1)
            pool.iota(full[:, :], [[P, TILES]], base=0, channel_multiplier=0,
                      allow_small_or_imprecise_dtypes=True).then_inc(const_ready, 1)
            pool.iota(tile_no[:, :], [[1, SLOT_TILES]], base=0, channel_multiplier=0,
                      allow_small_or_imprecise_dtypes=True).then_inc(const_ready, 1)
            pool.iota(ids[:, :, :], [[TOK, 2], [P, TILES]], base=0, channel_multiplier=1).then_inc(const_ready, 1)
            pool.memset(fill[:, 0:D], 0.0).then_inc(fill_ready, 1)
            pool.iota(fill[:, D:ROW].bitcast(I32), [[1, 1]], base=DUMP, channel_multiplier=1).then_inc(fill_ready, 1)
            for g in range(4):
                pool.wait_ge(norm_ready, g + 1)
                for k in range(8 * g + 5, 8 * g + 8):
                    pool.tensor_scalar(xk[:, k, :], xk[:, k, :], sm[:, 0, k:k + 1], sm[:, 1, k:k + 1],
                                       ALU.add, ALU.mult).then_inc(xn_pool, 1)
            pool.wait_ge(routed, 1)
            pool.wait_ge(filled, 16 * SLOT_TILES)
            for T in range(TILES):
                pool.wait_ge(staged, T + 1)
                for w in range(2):
                    pool.indirect_dma_start(
                        out=slot_rows, out_offset=bass.IndirectOffsetOnAxis(ap=slot[:, w, T:T + 1], axis=0),
                        in_=stage[:, T % 2, w, :], in_offset=None).then_inc(scattered[T % 2], 16)
            with pool.Fori(0, SLOT_TILES // 8) as i:
                for u in range(8):
                    pool.wait_ge(y_read, 8 * i + u + 1)
                    pool.sem_inc(passed, 1)
                    pool.indirect_dma_start(
                        out=results, out_offset=bass.IndirectOffsetOnAxis(ap=idx[:, u:u + 1], axis=0),
                        in_=ys[:, u, :], in_offset=None, bounds_check=DUMP - 1,
                        oob_is_err=False).then_inc(res_out[u], 16)

        @block.scalar
        def _(act):
            act.dma_start(ctx_sb[:, :, :], ctx.rearrange("b i d -> i b d")).then_inc(ctx_loaded, 16)
            act.wait_ge(ctx_turned, 1)
            for c in range(KC):
                act.activation(ctxT[:, c, :, :].rearrange("p b i -> p (b i)"), psC[c][:, 0:B * CTX],
                               ACT.Copy, scale=-2.0).then_inc(ctxT_ready, 1)

            def std(g):
                act.wait_ge(var_ready, g + 1)
                act.activation(sm[:, 3, 8 * g:8 * g + 8], sm[:, 2, 8 * g:8 * g + 8], ACT.Sqrt).then_inc(std_ready, 1)

            def copy_turned(n):
                act.wait_ge(turned, n + 1)
                if n >= 2:
                    act.wait_ge(dist_ready, n - 1)
                act.activation(xT[:, n % 2, 0, :, :], psT[n % 2][0][:, :, :], ACT.Copy).then_inc(xT_act, 1)

            std(0)
            for g in range(4):
                if g < 3:
                    std(g + 1)
                act.wait_ge(norm_ready, g + 1)
                for k in range(8 * g, 8 * g + 5):
                    act.activation(xk[:, k, :], xk[:, k, :], ACT.Identity, scale=sm[:, 1, k:k + 1],
                                   bias=sm[:, 4, k:k + 1]).then_inc(xn_act, 1)
                copy_turned(2 * g)
                copy_turned(2 * g + 1)
            act.wait_ge(clipped, 1)
            act.activation(root[:, :, 1:W], cost[:, :, 1:W], ACT.Sqrt).then_inc(rooted, 1)

            for g in range(4):
                act.wait_ge(var2_ready, g + 1)
                act.activation(sm[:, 3, 8 * g:8 * g + 8], sm[:, 2, 8 * g:8 * g + 8], ACT.Sqrt).then_inc(std2_ready, 1)
                act.wait_ge(norm2_ready, g + 1)
                for T in range(8 * g, 8 * g + 8):
                    if T >= 4:
                        act.wait_ge(x2_turned, T // 2 - 1)
                    act.activation(x2n[:, T % 4, :], xk[:, T, :], ACT.Identity, scale=sm[:, 1, T:T + 1],
                                   bias=sm[:, 4, T:T + 1]).then_inc(xn2_ready, 1)
            act.wait_ge(shifted, 1)
            act.activation(orig[:, :, :], t1[:, :, :], ACT.Exp).then_inc(expd, 1)

            def shared_silu(g):
                for m in range(MS):
                    act.wait_ge(h_ready, 2 * g + m + 1)
                    if g >= 2:
                        act.wait_ge(z_ready, 2 * (g - 1))
                    act.activation(silu[:, g % 2, m, :], psT[m][0][:, :, :].rearrange("p a b -> p (a b)"), ACT.Silu,
                                   bias=sb1[:, m:m + 1]).then_inc(silu_ready, 1)

            act.wait_ge(shared_small, 96)
            for g in range(EARLY):
                shared_silu(g)

            def act_step_of(i, c):
                q = 8 * i + c
                if live(i, c - 1):
                    act.wait_ge(hb_ready, q)
                    if not head(i, c - 3):
                        act.wait_ge(gated, q - 2)
                    act.activation(sg[:, (c - 1) % 2, :], hb[:, (c - 1) % 2, 0:I], ACT.Silu).then_inc(silu_done, 1)
                if live(i, c + 1):
                    act.wait_ge(x_turned, q + 2)
                    if not head(i, c - 1):
                        act.wait_ge(h_done, q)
                    act.activation(xsT[:, (c + 1) % 2, :, :].rearrange("p c t -> p (c t)"),
                                   psX[(c + 1) % 2], ACT.Copy).then_inc(xT_copied, 1)
                if live(i, c - 2):
                    act.wait_ge(g_turned, q - 1)
                    if not head(i, c - 4):
                        act.wait_ge(y_done, q - 3)
                    act.activation(hgT[:, c % 2, :], psG[c % 2], ACT.Copy).then_inc(hgT_copied, 1)

            pipeline(act, act_step_of)
            for g in range(EARLY, 8):
                shared_silu(g)

        @block.tensor
        def _(pe):
            pe.wait_ge(const_ready, 2)
            pe.wait_ge(ctx_loaded, 16)
            for c in range(KC):
                for b in range(B):
                    mm = pe.transpose(psC[c][:, b * CTX:(b + 1) * CTX], ctx_sb[:, b, c * P:(c + 1) * P],
                                      ident[0:CTX, 0:CTX])
            mm.then_inc(ctx_turned, 1)
            pe.wait_ge(weights_loaded, 16)
            for c in range(KC):
                mm = pe.transpose(psD[0][:, c, 0:E], gw[:, c * P:(c + 1) * P], ident[0:E, 0:E])
            mm.then_inc(gate_turned, 1)
            pe.wait_ge(aa_ready, 1)
            pe.wait_ge(ctxT_ready, KC)
            for b in range(B):
                mm = pe.matmul(psC[0][QUAD * b:QUAD * b + QUAD, 0:CTX], ones[0:CTX, :], aa_diag[:, b, :],
                               start=True, stop=True)
            mm.then_inc(aa_spread, 1)

            def turn(n):
                g, h = n // 2, n % 2
                pe.wait_ge(xn_act, 5 * g + (4 if h == 0 else 5))
                if h == 1:
                    pe.wait_ge(xn_pool, 3 * g + 3)
                if n >= 2:
                    pe.wait_ge(xT_act, n - 1)
                    pe.wait_ge(xT_dve, n - 1)
                for c in range(KC):
                    for k in range(4):
                        mm = pe.transpose(psT[h][c][:, k, :], xk[:, 4 * n + k, c * P:(c + 1) * P], ident[:, :])
                mm.then_inc(turned, 1)

            def distances(n):
                h = n % 2
                pe.wait_ge(xT_act, n + 1)
                pe.wait_ge(xT_dve, n + 1)
                if n == 0:
                    pe.wait_ge(gate_ready, 1)
                if n >= 2:
                    pe.wait_ge(dist_used, n - 1)
                for k in range(4):
                    for b in range(B):
                        for c in range(KC):
                            mm = pe.matmul(psD[h][QUAD * b:QUAD * b + QUAD, k, 0:CTX],
                                           xT[:, h, c, k, QUAD * b:QUAD * b + QUAD], ctxT[:, c, b, :],
                                           start=(c == 0), stop=(c == KC - 1))
                mm.then_inc(dist_ready, 1)

            for n in range(8):
                turn(n)
                if n >= 1:
                    distances(n - 1)
            distances(7)

            for b in range(B):
                pass
            pe.wait_ge(mask_in, 16 * B)
            pe.wait_ge(dist_used, 8)
            pe.wait_ge(xT_act, 8)
            pe.wait_ge(xT_dve, 8)
            for q in range(4):
                dst = psT[q // 2][q % 2][0:CTX, :, :].rearrange("p a b -> p (a b)").bitcast(BF16)
                for k in range(8):
                    mm = pe.transpose(dst[:, k * P:(k + 1) * P], maskU[:, :, 8 * q + k], identb[:, :])
                mm.then_inc(mask_turned, 1)
            def gather(n):
                if n >= 2:
                    pe.wait_ge(x2_ready, n - 1)
                for u in range(2):
                    T = 2 * n + u
                    b, j = T // 8, T % 8
                    lhs = maskT[:, 32 * b + 4 * j:32 * b + 4 * j + 4, :].rearrange("i p k -> i (p k)")
                    for part in range(3):
                        mm = pe.matmul(psC[n % 2][:, u * D:(u + 1) * D], lhs, ctx_parts[:, part, b, :],
                                       start=(part == 0), stop=(part == 2))
                mm.then_inc(gathered, 1)

            def logits(n):
                pe.wait_ge(x2T_ready, n + 1)
                for T in range(2 * n, 2 * n + 2):
                    for c in range(KC):
                        mm = pe.matmul(psL[:, T, :], x2T[:, c, T * P:(T + 1) * P], gwT[:, c, :],
                                       start=(c == 0), stop=(c == KC - 1))
                mm.then_inc(logits_ready, 1)

            def turn2(n):
                pe.wait_ge(xn2_ready, 2 * n + 2)
                if n >= 2:
                    pe.wait_ge(x2T_ready, n - 1)
                for u in range(2):
                    for c in range(KC):
                        mm = pe.transpose(psT[0][n % 2][:, 2 * c + u, :], x2n[:, (2 * n + u) % 4, c * P:(c + 1) * P],
                                          ident[:, :])
                mm.then_inc(x2_turned, 1)

            pe.wait_ge(maskT_ready, 4)
            pe.wait_ge(parts_ready, 3)
            for g in range(TILES // 8 + 1):
                if g < TILES // 8:
                    for n in range(4 * g, 4 * g + 4):
                        gather(n)
                if g:
                    for n in range(4 * g - 4, 4 * g):
                        turn2(n)
                        if n:
                            logits(n - 1)
            logits(TILES // 2 - 1)
            pe.wait_ge(oh_ready, 1)
            pe.matmul(psD[1][:, :, :].rearrange("p a b -> p (a b)"), tri[:, :],
                      ohb[:, :, :].rearrange("p t e -> p (t e)"), start=True, stop=True)
            pe.matmul(psC[0][:, :], onesb[:, :], ohb[:, :, :].rearrange("p t e -> p (t e)"),
                      start=True, stop=True).then_inc(counted, 1)

            def shared_h(g):
                for m in range(MS):
                    if g >= 1:
                        pe.wait_ge(act_ready, 2 * g + m - 1)
                    for w, ps_ in ((sw1, psT[m][0]), (sw3, psT[m][1])):
                        for c in range(KC):
                            mm = pe.matmul(ps_[:, :, :].rearrange("p a b -> p (a b)"), w[:, c, m * P:(m + 1) * P],
                                           x2T[:, c, 512 * g:512 * g + 512], start=(c == 0), stop=(c == KC - 1))
                    mm.then_inc(h_ready, 1)

            def shared_z(g):
                pe.wait_ge(act_ready, 2 * g + 2)
                for j in range(2):
                    if g >= 1:
                        pe.wait_ge(z_used, 2 * (g - 1) + j + 1)
                    for u in range(2):
                        for m in range(MS):
                            mm = pe.matmul(psC[j][:, u * D:(u + 1) * D],
                                           silu[:, g % 2, m, (2 * j + u) * P:(2 * j + u + 1) * P], sw2[:, m, :],
                                           start=(m == 0), stop=(m == MS - 1))
                    mm.then_inc(z_ready, 1)

            pe.wait_ge(routed, 1)
            pe.wait_ge(shared_small, 96)
            for g in range(EARLY):
                shared_h(g)
                if g:
                    shared_z(g - 1)
            shared_z(EARLY - 1)

            pe_expert = [pe.alloc_register(f"pe_expert{u}") for u in range(4)]

            def pe_step_of(i, c):
                q = 8 * i + c
                if live(i, c + 1):
                    r = c + 1
                    pe.wait_ge(xs_loaded[r % 4], 16 * (2 * i + r // 4 + 1))
                    if not head(i, r - 2):
                        pe.wait_ge(xT_copied, q)
                    for k in range(KC):
                        mm = pe.transpose(psX[r % 2][:, k * P:(k + 1) * P], xs[:, r % 4, k * P:(k + 1) * P], ident[:, :])
                    mm.then_inc(x_turned, 1)
                if live(i, c - 2):
                    pe.wait_ge(gated, q - 1)
                    if not head(i, c - 4):
                        pe.wait_ge(hgT_copied, q - 3)
                    pe.transpose(psG[c % 2], hg[:, c % 2, :], ident[:, :]).then_inc(g_turned, 1)
                if live(i, c):
                    e = expert(pe, pe_expert, c)
                    pe.wait_ge(xT_copied, q + 1)
                    if not head(i, c - 2):
                        pe.wait_ge(hb_ready, q - 1)
                    for k in range(KC):
                        mm = pe.matmul(psH[c % 2], xsT[:, c % 2, k, :], w13f[:, bass.ds(k * E * 2 * I + e, 2 * I)],
                                       start=(k == 0), stop=(k == KC - 1))
                    mm.then_inc(h_done, 1)
                if live(i, c + 1):
                    load_expert(pe, pe_expert, i, c + 1)
                if live(i, c - 2):
                    e = expert(pe, pe_expert, c - 2)
                    pe.wait_ge(hgT_copied, q - 1)
                    if not head(i, c - 4):
                        pe.wait_ge(y_read, q - 3)
                    pe.matmul(psY[c % 2], hgT[:, c % 2, :], w2f[:, bass.ds(e, D)],
                              start=True, stop=True).then_inc(y_done, 1)

            pe.wait_ge(etab_ready, 1)
            pe.wait_ge(biases1_loaded, 80)
            pe.wait_ge(z_used, 2 * EARLY)
            pipeline(pe, pe_step_of)
            pe.wait_ge(y_read, SLOT_TILES)
            pe.wait_ge(hgT_copied, SLOT_TILES)
            for g in range(EARLY, 8):
                shared_h(g)
                if g > EARLY:
                    shared_z(g - 1)
            shared_z(7)

        @block.vector
        def _(dve):
            done = [0]

            def link(ins):
                done[0] += 1
                ins.then_inc(dve_step, 1)
                dve.wait_ge(dve_step, done[0])

            def moments(g, ready):
                s = slice(8 * g, 8 * g + 8)
                me, m2e, mo, m2o = (stats[:, s, i] for i in (1, 2, 4, 5))
                dve.tensor_tensor(sm[:, 5, s], me, mo, ALU.subtract)
                dve.tensor_tensor(sm[:, 6, s], m2e, m2o, ALU.add)
                link(dve.tensor_tensor(sm[:, 7, s], me, mo, ALU.add))
                dve.tensor_scalar(sm[:, 0, s], sm[:, 7, s], -0.5, None, ALU.mult)
                link(dve.tensor_tensor(sm[:, 5, s], sm[:, 5, s], sm[:, 5, s], ALU.mult))
                link(dve.scalar_tensor_tensor(out=sm[:, 6, s], in0=sm[:, 5, s], scalar=D / 4.0, in1=sm[:, 6, s],
                                              op0=ALU.mult, op1=ALU.add))
                dve.tensor_scalar(sm[:, 2, s], sm[:, 6, s], 1.0 / D, EPS, ALU.mult, ALU.add).then_inc(ready, 1)

            def statistics(g):
                dve.wait_ge(x_loaded[g], 16)
                for k in range(8 * g, 8 * g + 8):
                    ins = dve.bn_stats(stats[:, k, :], xk[:, k, :])
                link(ins)
                moments(g, var_ready)

            def inverse_root(g):
                s = slice(8 * g, 8 * g + 8)
                v, sd, r, t = sm[:, 2, s], sm[:, 3, s], sm[:, 1, s], sm[:, 8, s]
                link(dve.reciprocal(r, sd))
                link(dve.tensor_tensor(t, r, r, ALU.mult))
                link(dve.tensor_tensor(t, t, v, ALU.mult))
                link(dve.tensor_scalar(t, t, -0.5, 1.5, ALU.mult, ALU.add))
                link(dve.tensor_tensor(r, r, t, ALU.mult))

            def norms(g):
                s = slice(8 * g, 8 * g + 8)
                r, t = sm[:, 1, s], sm[:, 8, s]
                dve.wait_ge(std_ready, g + 1)
                inverse_root(g)
                link(dve.tensor_tensor(t, r, r, ALU.mult))
                dve.tensor_tensor(sm[:, 9, s], sm[:, 6, s], t, ALU.mult)
                dve.tensor_tensor(sm[:, 4, s], sm[:, 0, s], r, ALU.mult).then_inc(norm_ready, 1)

            def copy_turned(n):
                dve.wait_ge(turned, n + 1)
                if n >= 2:
                    dve.wait_ge(dist_ready, n - 1)
                dve.tensor_copy(xT[:, n % 2, 1, :, :], psT[n % 2][1][:, :, :]).then_inc(xT_dve, 1)

            def squared(n):
                dve.wait_ge(dist_ready, n + 1)
                for k in range(4):
                    kk = 4 * n + k
                    ins = dve.scalar_tensor_tensor(out=cost[:, :, 1 + kk], in0=psD[n % 2][:, k, 0:CTX],
                                                   scalar=sm[:, 9, kk:kk + 1], in1=aa_row[:, :],
                                                   op0=ALU.add, op1=ALU.add)
                ins.then_inc(dist_used, 1)

            dve.wait_ge(gate_turned, 1)
            for c in range(KC):
                ins = dve.tensor_copy(gwT[:, c, :], psD[0][:, c, 0:E])
            ins.then_inc(gate_ready, 1)
            dve.wait_ge(ctx_loaded, 16)
            for b in range(B):
                ins = dve.tensor_tensor_reduce(out=ctx_rest[:, b, :], in0=ctx_sb[:, b, :], in1=ctx_sb[:, b, :],
                                               scale=1.0, scalar=0.0, op0=ALU.mult, op1=ALU.add,
                                               accum_out=aa[:, b:b + 1])
            link(ins)
            dve.wait_ge(const_ready, 2)
            for b in range(B):
                ins = dve.tensor_scalar(aa_diag[:, b, :], ident[0:CTX, 0:CTX], aa[:, b:b + 1], None, ALU.mult)
            ins.then_inc(aa_ready, 1)
            dve.tensor_copy(identb[:, :], ident[:, :]).then_inc(parts_ready, 1)
            dve.tensor_reduce(first_chunk[:, :], ident[:, 0:P:QUAD], AX.X, ALU.add)
            link(dve.tensor_reduce(last_chunk[:, :], ident[:, QUAD - 1:P:QUAD], AX.X, ALU.add))
            link(dve.memset(cost[:, :, 0:1], BIG))
            link(dve.tensor_scalar(cost[:, :, 0:1], cost[:, :, 0:1], first_chunk[:, :], None, ALU.mult))
            link(dve.memset(cost[:, 0, 0:1], 0.0))
            dve.memset(R[:, 0, :], BIG)
            dve.memset(carry[:, 0:1], BIG)
            dve.memset(A[:, NT, 0:CH], 0.0)
            link(dve.memset(A[:, :, CH:W], 1.0))
            dve.tensor_scalar(A[:, :, CH:W], A[:, :, CH:W], last_chunk[:, :], None, ALU.mult)
            link(dve.tensor_scalar(carry[:, 0:1], carry[:, 0:1], 1.0, None, ALU.mult))
            for b in range(B):
                dve.memset(carry[QUAD * b:QUAD * b + 1, 0:1], 0.0)
            dve.wait_ge(aa_spread, 1)
            link(dve.tensor_copy(aa_row[:, :], psC[0][:, 0:CTX]))

            statistics(0)
            statistics(1)
            norms(0)
            for g in range(4):
                if g + 2 < 4:
                    statistics(g + 2)
                if g + 1 < 4:
                    norms(g + 1)
                copy_turned(2 * g)
                if g:
                    squared(2 * g - 1)
                copy_turned(2 * g + 1)
                squared(2 * g)
            squared(7)
            dve.wait_ge(dist_used, 8)
            dve.tensor_scalar(cost[:, :, 1:W], cost[:, :, 1:W], 0.0, None, ALU.max).then_inc(clipped, 1)
            dve.wait_ge(clipped, 1)
            dve.wait_ge(rooted, 1)
            link(dve.tensor_scalar(half[:, :, 1:W], root[:, :, 1:W], 2.0, 1e-30, ALU.mult, ALU.max))
            link(dve.reciprocal(half[:, :, 1:W], half[:, :, 1:W]))
            link(dve.tensor_tensor(half[:, :, 1:W], half[:, :, 1:W], cost[:, :, 1:W], ALU.mult))
            dve.scalar_tensor_tensor(out=cost[:, :, 1:W], in0=root[:, :, 1:W], scalar=0.5,
                                     in1=half[:, :, 1:W], op0=ALU.mult, op1=ALU.add).then_inc(cost_ready, 1)

            dve.tensor_copy(ctx_rest[:, :, :], ctx_sb[:, :, :])
            link(dve.tensor_copy(ctx_parts[:, 0, :, :], ctx_sb[:, :, :]))
            link(dve.tensor_tensor(ctx_rest[:, :, :], ctx_rest[:, :, :], ctx_parts[:, 0, :, :], ALU.subtract))
            link(dve.tensor_copy(ctx_parts[:, 1, :, :], ctx_rest[:, :, :]))
            link(dve.tensor_tensor(ctx_rest[:, :, :], ctx_rest[:, :, :], ctx_parts[:, 1, :, :], ALU.subtract))
            dve.tensor_copy(ctx_parts[:, 2, :, :], ctx_rest[:, :, :]).then_inc(parts_ready, 2)

            dve.wait_ge(pads_zeroed, 16 * ((NT + 15) // 16))
            link(dve.memset(M[:, :, 0:1], BIG))
            dve.wait_ge(cost_in, 16)
            right = [QUAD - 1] + list(range(QUAD - 1))
            for t in range(NT):
                link(dve.tensor_tensor(M[:, t, 1:W], R[:, t, 0:CH], R[:, t, 1:W], ALU.min))
                link(dve.tensor_tensor_scan(R[:, t + 1, :], M[:, t, :], cst[:, t, :], carry[:, t:t + 1],
                                            ALU.min, ALU.add))
                if t + 1 < NT:
                    dve.stream_shuffle(carry[:, t + 1:t + 2], R[:, t + 1, CH:W], right)
                if t == 0:
                    link(dve.memset(R[:, 1, 0:1], BIG))
            link(dve.tensor_tensor(F[:, :, 1:W], R[:, 0:NT, 0:CH], R[:, 0:NT, 1:W], ALU.is_le))
            link(dve.tensor_tensor(M[:, :, 1:W], R[:, 1:NT + 1, 0:CH], M[:, :, 1:W], ALU.is_lt))
            link(dve.scalar_tensor_tensor(out=cst[:, :, 0:CH], in0=F[:, :, 1:W], scalar=0.5, in1=M[:, :, 1:W],
                                          op0=ALU.mult, op1=ALU.max))
            link(dve.memset(cst[:, :, CH:W], 1.0))
            left = list(range(1, QUAD)) + [0]
            link(dve.memset(carry[:, NT:NT + 1], 0.0))

            def rev(tns, t):
                return bass.AP(tensor=tns, offset=t * W + CH, ap=[[tns.shape[1] * W, P], [-1, W]])
            for t in range(NT - 1, -1, -1):
                link(dve.tensor_tensor_scan(rev(V, t), rev(cst, t), rev(A, t + 1), carry[:, t + 1:t + 2],
                                            ALU.mult, ALU.max))
                if t:
                    dve.stream_shuffle(carry[:, t:t + 1], V[:, t, 0:1], left)
                    link(dve.scalar_tensor_tensor(out=A[:, t, 0:CH], in0=cst[:, t, 0:CH], scalar=0.5,
                                                  in1=V[:, t, 0:CH], op0=ALU.mult, op1=ALU.is_lt))
            dve.scalar_tensor_tensor(out=mask[:, :, :], in0=V[:, 0:NT, 1:W], scalar=1.0,
                                     in1=A[:, 1:NT + 1, 0:CH], op0=ALU.is_ge,
                                     op1=ALU.subtract).then_inc(mask_ready, 1)

            for q in range(4):
                dve.wait_ge(mask_turned, q + 1)
                src = psT[q // 2][q % 2][0:CTX, :, :].rearrange("p a b -> p (a b)").bitcast(BF16)
                dve.tensor_copy(maskT[:, :, 8 * q:8 * q + 8], src.rearrange("i (k p) -> i p k", k=8)
                                ).then_inc(maskT_ready, 1)
            def statistics2(g):
                dve.wait_ge(x2_ready, 4 * g + 4)
                for T in range(8 * g, 8 * g + 8):
                    ins = dve.bn_stats(stats[:, T, :], xk[:, T, :])
                link(ins)
                moments(g, var2_ready)

            def norms2(g):
                dve.wait_ge(std2_ready, g + 1)
                inverse_root(g)
                s = slice(8 * g, 8 * g + 8)
                dve.tensor_tensor(sm[:, 4, s], sm[:, 0, s], sm[:, 1, s], ALU.mult).then_inc(norm2_ready, 1)

            def turned2(n):
                dve.wait_ge(x2_turned, n + 1)
                dst = bass.AP(tensor=x2T, offset=2 * n * P, ap=[[KC * TOK, P], [TOK, KC], [1, 2 * P]])
                dve.tensor_copy(dst, psT[0][n % 2][:, :, :].rearrange("p (c u) t -> p c (u t)", c=KC)
                                ).then_inc(x2T_ready, 1)

            dve.wait_ge(x_nat, 64)
            for n in range(TILES // 2):
                dve.wait_ge(gathered, n + 1)
                pair = xk[:, 2 * n:2 * n + 2, :].rearrange("p t d -> p (t d)")
                dve.tensor_tensor(pair, psC[n % 2][:, :], pair, ALU.add).then_inc(x2_ready, 1)
                if n % 4 == 3:
                    g = n // 4
                    statistics2(g)
                    if g:
                        norms2(g - 1)
                        for k in range(4):
                            turned2(4 * (g - 1) + k)
            norms2(3)
            for k in range(4):
                turned2(12 + k)

            def over_e(ap):
                return ap.unsqueeze(2).to_broadcast([P, TILES, E])

            dve.wait_ge(logits_ready, TILES // 2)
            dve.wait_ge(shared_small, 96)
            link(dve.tensor_reduce(r1[:, :], psL, AX.X, ALU.max))
            dve.tensor_tensor(t1[:, :, :], psL, over_e(r1[:, :]), ALU.subtract).then_inc(shifted, 1)
            dve.wait_ge(expd, 1)
            link(dve.tensor_reduce(r2[:, :], orig[:, :, :], AX.X, ALU.add))
            link(dve.reciprocal(r2[:, :], r2[:, :]))
            link(dve.tensor_tensor(orig[:, :, :], orig[:, :, :], over_e(r2[:, :]), ALU.mult))
            link(dve.tensor_tensor(score[:, :, :], orig[:, :, :],
                                   gb[:, :].unsqueeze(1).to_broadcast([P, TILES, E]), ALU.add))
            pr = score[:, :, :].rearrange("p t (h two) -> p (t h) two", two=2)
            HP = TILES * E // 2
            hi = t1[:, :, :].rearrange("p t e -> p (t e)")[:, 0:HP]
            lo = t2[:, :, :].rearrange("p t e -> p (t e)")[:, 0:HP]
            dve.tensor_tensor(hi, pr[:, :, 0], pr[:, :, 1], ALU.max)
            link(dve.tensor_tensor(lo, pr[:, :, 0], pr[:, :, 1], ALU.min))
            hi2, lo2 = (a.rearrange("p (g two) -> p g two", two=2) for a in (hi, lo))
            gsf, gkf, gpf = (a[:, :, :].rearrange("p t g -> p (t g)") for a in (gs, gk, gp))
            dve.tensor_tensor(gsf, hi2[:, :, 0], hi2[:, :, 1], ALU.max)
            dve.tensor_tensor(gkf, hi2[:, :, 0], hi2[:, :, 1], ALU.min)
            link(dve.tensor_tensor(gpf, lo2[:, :, 0], lo2[:, :, 1], ALU.max))
            link(dve.tensor_tensor(gkf, gkf, gpf, ALU.max))
            link(dve.tensor_tensor(gsf, gsf, gkf, ALU.add))
            sq = [P, TILES, G, G]
            other = gs[:, :, :].unsqueeze(2).to_broadcast(sq)
            own = gs[:, :, :].unsqueeze(3).to_broadcast(sq)
            v4 = [a[:, :, :].rearrange("p t (g h) -> p t g h", g=G) for a in (t1, t2)]
            low4 = low_e[:, :, :].unsqueeze(1).to_broadcast(sq)
            dve.wait_ge(const_ready, 8)
            dve.tensor_tensor(v4[0], other, own, ALU.is_gt)
            link(dve.tensor_tensor(v4[1], other, own, ALU.is_equal))
            link(dve.tensor_tensor(v4[1], v4[1], low4, ALU.mult))
            link(dve.tensor_tensor(v4[0], v4[0], v4[1], ALU.add))
            link(dve.tensor_reduce(gk[:, :, :], v4[0], AX.X, ALU.add))
            link(dve.tensor_scalar(gkf, gkf, 1.5, None, ALU.is_lt))
            dve.tensor_scalar(gpf, gkf, -1.0, BIG, ALU.add, ALU.mult)
            sc4, t34 = (a[:, :, :].rearrange("p t (g h) -> p (t g) h", g=G) for a in (score, t3))
            g4 = [P, TILES * G, E // G]
            link(dve.tensor_tensor(t34, sc4, gkf.unsqueeze(2).to_broadcast(g4), ALU.mult))
            link(dve.tensor_tensor(t34, t34, gpf.unsqueeze(2).to_broadcast(g4), ALU.add))
            rev = rev_e[:, :].unsqueeze(1).to_broadcast([P, TILES, E])
            for w, oh in enumerate((oh1, oh2)):
                link(dve.tensor_reduce(r1[:, :], t3[:, :, :], AX.X, ALU.max))
                link(dve.tensor_tensor(t1[:, :, :], t3[:, :, :], over_e(r1[:, :]), ALU.is_equal))
                link(dve.tensor_tensor(t1[:, :, :], t1[:, :, :], rev, ALU.mult))
                link(dve.tensor_reduce(r1[:, :], t1[:, :, :], AX.X, ALU.max))
                link(dve.tensor_tensor(oh[:, :, :], t1[:, :, :], over_e(r1[:, :]), ALU.is_equal))
                if w == 0:
                    dve.scalar_tensor_tensor(out=t3[:, :, :].rearrange("p t e -> p (t e)"),
                                             in0=oh[:, :, :].rearrange("p t e -> p (t e)"), scalar=-4.0 * BIG,
                                             in1=t3[:, :, :].rearrange("p t e -> p (t e)"),
                                             op0=ALU.mult, op1=ALU.add)
                link(dve.tensor_tensor(t2[:, :, :], orig[:, :, :], oh[:, :, :], ALU.mult))
                link(dve.tensor_reduce(wt[:, w, :], t2[:, :, :], AX.X, ALU.add))
            dve.tensor_tensor(ohb[:, :, :], oh1[:, :, :], oh2[:, :, :], ALU.add).then_inc(oh_ready, 1)

            dve.memset(keep_on[:, :, :], 1.0)
            link(dve.memset(one_e[:, :], 1.0))
            link(dve.memset(keep_on[:, :, 0:1], 0.0))
            dve.wait_ge(counted, 1)
            psn = psC[0][:, :].rearrange("p (t e) -> p e t", e=E)
            link(dve.tensor_copy(cnt[:, :, :], psn))
            link(dve.tensor_tensor_scan(upto[:, :, :].rearrange("p e t -> p (e t)"),
                                        keep_on[:, :, :].rearrange("p e t -> p (e t)"),
                                        cnt[:, :, :].rearrange("p e t -> p (e t)"), 0.0, ALU.mult, ALU.add))
            sq = [P, E, TILES]
            link(dve.tensor_tensor(keep_on[:, :, :], upto[:, :, TILES - 1:TILES].to_broadcast(sq),
                                   full[:, :].unsqueeze(1).to_broadcast(sq), ALU.is_gt))
            link(dve.tensor_reduce(te[:, :], keep_on[:, :, :], AX.X, ALU.add))
            link(dve.tensor_tensor_scan(tend[:, :], one_e[:, :], te[:, :], 0.0, ALU.mult, ALU.add))
            link(dve.tensor_tensor(tbase[:, :], tend[:, :], te[:, :], ALU.subtract))
            link(dve.tensor_scalar(tbase[:, :], tbase[:, :], float(P), None, ALU.mult))
            link(dve.tensor_tensor(cnt[:, :, :], upto[:, :, :], cnt[:, :, :], ALU.subtract))
            link(dve.tensor_tensor(cnt[:, :, :], cnt[:, :, :], tbase[:, :].unsqueeze(2).to_broadcast(sq), ALU.add))
            rank = psD[1][:, :, :].rearrange("p a b -> p (a b)").rearrange("p (t e) -> p t e", e=E)
            link(dve.tensor_tensor(t3[:, :, :], rank, cnt[:, :, :].rearrange("p e t -> p t e"), ALU.add))
            for w, oh in enumerate((oh1, oh2)):
                link(dve.tensor_tensor(t1[:, :, :], t3[:, :, :], oh[:, :, :], ALU.mult))
                link(dve.tensor_reduce(r1[:, :], t1[:, :, :], AX.X, ALU.add))
                ins = dve.tensor_copy(slot[:, w, :], r1[:, :])
                if w == 0:
                    link(ins)
            ins.then_inc(routed, 1)
            sq = [P, SLOT_TILES, E]
            link(dve.tensor_tensor(big_e[:, :, :], tend[:, :].unsqueeze(1).to_broadcast(sq),
                                   tile_no[:, :].unsqueeze(2).to_broadcast(sq), ALU.is_le))
            link(dve.tensor_reduce(lin[:, 0:SLOT_TILES], big_e[:, :, :], AX.X, ALU.add))
            dve.tensor_scalar(etab[:, :], lin[:, 0:SLOT_TILES], float(E - 1), float(D),
                              ALU.min, ALU.mult).then_inc(etab_ready, 1)

            def stage_tile(T):
                if T >= 2:
                    dve.wait_ge(scattered[T % 2], 32 * (T // 2))
                for w in range(2):
                    dve.tensor_scalar(stage[:, T % 2, w, 0:D], xk[:, T, :], sm[:, 0, T:T + 1], sm[:, 1, T:T + 1],
                                      ALU.add, ALU.mult)
                dve.tensor_copy(stage[:, T % 2, :, D:ROW].bitcast(I32), ids[:, :, T:T + 1]).then_inc(staged, 1)

            def shared_act(g):
                for m in range(MS):
                    dve.wait_ge(silu_ready, 2 * g + m + 1)
                    dve.scalar_tensor_tensor(out=silu[:, g % 2, m, :],
                                             in0=psT[m][1][:, :, :].rearrange("p a b -> p (a b)"),
                                             scalar=sb3[:, m:m + 1], in1=silu[:, g % 2, m, :],
                                             op0=ALU.add, op1=ALU.mult).then_inc(act_ready, 1)

            def shared_add(g):
                for j in range(2):
                    n = 2 * g + j
                    dve.wait_ge(z_ready, n + 1)
                    if n:
                        dve.wait_ge(z_used, n)
                    pair = xk[:, 2 * n:2 * n + 2, :]
                    link(dve.tensor_tensor(lin[:, :].rearrange("p (t d) -> p t d", t=2),
                                           psC[j][:, :].rearrange("p (t d) -> p t d", t=2),
                                           bs2b[:, :].unsqueeze(1).to_broadcast([P, 2, D]), ALU.add))
                    dve.tensor_tensor(pair.rearrange("p t d -> p (t d)"), lin[:, :],
                                      pair.rearrange("p t d -> p (t d)"), ALU.add).then_inc(z_used, 1)

            dve.wait_ge(etab_ready, 1)
            dve.wait_ge(lin_ready, 16)
            for g in range(EARLY):
                for T in range(4 * g, 4 * g + 4):
                    stage_tile(T)
                    if T % 2 == 1 and T % 4 == 1:
                        shared_act(g)
                if g:
                    shared_add(g - 1)
            for T in range(4 * EARLY, TILES):
                stage_tile(T)
            shared_add(EARLY - 1)

            dve_expert = [dve.alloc_register(f"dve_expert{u}") for u in range(4)]

            def dve_step_of(i, c):
                q = 8 * i + c
                if live(i, c - 3):
                    r = c - 3
                    e = expert(dve, dve_expert, r)
                    dve.wait_ge(y_done, q - 2)
                    if not head(i, r - 8):
                        dve.wait_ge(res_out[r % 8], 16 * (i + r // 8))
                    dve.tensor_tensor(ys[:, r % 8, :], psY[r % 2], b2f[:, bass.ds(e, D)],
                                      ALU.add).then_inc(y_read, 1)
                if live(i, c - 1):
                    r = c - 1
                    dve.wait_ge(silu_done, q)
                    if not head(i, r - 2):
                        dve.wait_ge(g_turned, q - 2)
                    dve.tensor_tensor(hg[:, r % 2, :], sg[:, r % 2, :], hb[:, r % 2, I:2 * I],
                                      ALU.mult).then_inc(gated, 1)
                if live(i, c):
                    e = expert(dve, dve_expert, c)
                    dve.wait_ge(xs_loaded[c % 4], 16 * (2 * i + c // 4 + 1))
                    if not head(i, c - 8):
                        dve.wait_ge(res_out[c % 8], 16 * (i + c // 8))
                    dve.tensor_copy(idx[:, c % 8:c % 8 + 1], xs[:, c % 4, D:ROW].bitcast(I32)).then_inc(id_copied, 1)
                    dve.wait_ge(h_done, q + 1)
                    if not head(i, c - 2):
                        dve.wait_ge(gated, q - 1)
                    dve.tensor_tensor(hb[:, c % 2, :], psH[c % 2], b13f[:, bass.ds(e, 2 * I)],
                                      ALU.add).then_inc(hb_ready, 1)
                if live(i, c + 1):
                    load_expert(dve, dve_expert, i, c + 1)

            dve.wait_ge(biases_loaded, 48)
            pipeline(dve, dve_step_of)
            for g in range(EARLY, 8):
                shared_act(g)
                if g > EARLY:
                    shared_add(g - 1)
            shared_add(7)
            for T in range(TILES):
                g = T // 4
                dve.wait_ge(tail_in[g % 2], 32 * (g // 2 + 1))
                link(dve.scalar_tensor_tensor(out=xk[:, T, :], in0=back[:, g % 2, T % 4, 0, :],
                                              scalar=wt[:, 0, T:T + 1], in1=xk[:, T, :],
                                              op0=ALU.mult, op1=ALU.add))
                dve.scalar_tensor_tensor(out=xk[:, T, :], in0=back[:, g % 2, T % 4, 1, :],
                                         scalar=wt[:, 1, T:T + 1], in1=xk[:, T, :],
                                         op0=ALU.mult, op1=ALU.add).then_inc(combined, 1)


def kernel(**inputs):
    import numpy as _np
    import concourse.bacc as _bacc
    from concourse import mybir as _mybir
    from concourse.bass_utils import run_bass_kernel_spmd as _run

    nc = _bacc.Bacc("TRN2", target_bir_lowering=False, num_devices=1)
    arrays, args = {}, []
    names = ["x", "ctx_1024"] + ["L0_ffn_" + n for n in (
        "gate_w gate_b We1 be1 We2 be2 We3 be3 ws1 bs1 ws2 bs2 ws3 bs3").split()]
    for name in names:
        a = _np.ascontiguousarray(inputs[name])
        arrays[f"in_{name}"] = a
        args.append(nc.dram_tensor(f"in_{name}", a.shape, _mybir.dt.from_np(a.dtype), kind="ExternalInput").ap())
    out = nc.dram_tensor("out_0", (4, 1024, 256), _mybir.dt.float32, kind="ExternalOutput").ap()
    build(nc, *args, out)
    r = _run(nc, [arrays], core_ids=[0])
    return r.results[0]["out_0"]
```

```python
import concourse.bass as bass
from concourse import mybir

ALU = mybir.AluOpType
ACT = mybir.ActivationFunctionType
AX = mybir.AxisListType
F32 = mybir.dt.float32
BF16 = mybir.dt.bfloat16
I32 = mybir.dt.int32

P = 128
QUAD = 32
B, S, D = 4, 1024, 256
CTX = 77
KC = D // P
CH = S // QUAD
W = CH + 1
CUT = 16
PARTS = (slice(0, CUT), slice(CUT, CTX))
NT = CTX + QUAD - 1
TILES = B * S // P
TOK = B * S
E = 16
G = 4
I = 128
MS = 2
SLOT_TILES = 80
SLOTS = SLOT_TILES * P
ROW = D + 1
DUMP = 2 * TOK
BIG = 1e30
EPS = 1e-5


def build(nc, x, ctx, gate_w, gate_b, we1, be1, we2, be2, we3, be3, ws1, bs1, ws2, bs2, ws3, bs3, out):
    def sb(name, shape, dt=F32):
        return nc.alloc_sbuf_tensor(name, shape, dt)

    def ps(name, shape, dt=F32):
        return nc.alloc_psum_tensor(name, shape, dt)

    def sem(name):
        return nc.alloc_semaphore(name)

    cost_skew = nc.dram_tensor("cost_skew", (P, NT * W), F32, kind="Internal").ap()
    mask_skew = nc.dram_tensor("mask_skew", (P, NT * CH), BF16, kind="Internal").ap()

    slot_rows = nc.dram_tensor("slot_rows", (SLOTS, ROW), F32, kind="Internal").ap()
    results = nc.dram_tensor("results", (DUMP, D), F32, kind="Internal").ap()

    top = [(nc.sbuf_base + 63) // 64 * 64]

    def size(shape, dt):
        n = 2 if dt is BF16 else 4
        for k in shape[1:]:
            n *= k
        return (n + 31) // 32 * 32

    def place(name, shape, dt=F32, at=None):
        cursor = top if at is None else at
        off = cursor[0]
        cursor[0] = off + size(shape, dt)
        assert cursor[0] <= nc.sbuf_usable_end, (name, cursor[0])
        return nc.alloc_sbuf_tensor_at(name, shape, dt, offset=off)

    ident = place("ident", [P, P])
    identb = place("identb", [P, P], BF16)
    ones = place("ones", [P, QUAD])
    stats = place("stats", [P, CH, 6])
    sm = place("sm", [P, 10, CH])
    first_chunk = place("first_chunk", [P, 1])
    last_chunk = place("last_chunk", [P, 1])
    tiny = place("tiny", [P, 1])
    xk = place("xk", [P, CH, D])
    w13_at = top[0]
    w13 = place("w13", [P, KC, E, 2 * I])
    w2 = place("w2", [P, E, D])
    sw1 = place("sw1", [P, KC, MS * I])
    sw3 = place("sw3", [P, KC, MS * I])
    sw2 = place("sw2", [P, MS, D])
    sb1 = place("sb1", [P, MS])
    sb3 = place("sb3", [P, MS])
    gwT = place("gwT", [P, KC, E])
    gb = place("gb", [P, E])
    fill = place("fill", [P, ROW])
    tri = place("tri", [P, P], BF16)
    onesb = place("onesb", [P, P], BF16)
    gw = place("gw", [E, D])
    ids = place("ids", [P, 2, TILES], I32)
    slot = place("slot", [P, 2, TILES], I32)
    wt = place("wt", [P, 2, TILES])
    etab = place("etab", [P, SLOT_TILES], I32)
    idx = place("idx", [P, 8], I32)
    low_e = place("low_e", [P, G, G])
    rev_e = place("rev_e", [P, E])
    full = place("full", [P, TILES])
    tile_no = place("tile_no", [P, SLOT_TILES])

    low = top[0]
    cost = place("cost", [P, CTX, W])
    r_at = top[0]
    R = place("R", [P, NT + 1, W])
    m_at = top[0]
    M = place("M", [P, NT, W])
    cst_at = top[0]
    cst = place("cst", [P, NT, W])
    f_at = top[0]
    F = place("F", [P, NT, W])
    v_at = top[0]
    V = place("V", [P, NT + 1, W])
    a_at = top[0]
    A = place("A", [P, NT + 1, W], BF16)
    xT = place("xT", [P, 2, KC, 4, P])
    ctx_sb = place("ctx_sb", [CTX, B, D])
    ctx_rest = place("ctx_rest", [CTX, B, D])
    ctxT = place("ctxT", [P, KC, B, CTX])
    aa_diag = place("aa_diag", [CTX, B, CTX])
    front_end = top[0]
    aa = place("aa", [CTX, B])
    aa_row = place("aa_row", [P, CTX])
    carry = place("carry", [P, NT + 1])
    ctx_parts = place("ctx_parts", [CTX, 3, B, D], BF16)
    root = place("root", [P, CTX, W], at=[v_at])
    inv = place("inv", [P, CTX, W], at=[f_at])
    rest = place("rest", [P, CTX, W], at=[cst_at])
    zeros = place("zeros", [P, W * 16], at=[m_at])
    cursor = [r_at]
    mask = place("mask", [P, NT, CH], BF16, at=cursor)
    maskU = place("maskU", [P, CTX, CH], BF16, at=cursor)
    maskT = place("maskT", [CTX, P, CH], BF16, at=[m_at])
    cursor = [low]
    orig, score, t1, t2, t3, oh1, oh2 = (place(n, [P, TILES, E], at=cursor)
                                         for n in ("orig", "score", "t1", "t2", "t3", "oh1", "oh2"))
    ohb = place("ohb", [P, TILES, E], BF16, at=cursor)
    cnt = place("cnt", [P, E, TILES], at=cursor)
    keep_on = place("keep_on", [P, E, TILES], at=cursor)
    upto = place("upto", [P, E, TILES], at=cursor)
    r1, r2, r3 = (place(n, [P, TILES], at=cursor) for n in ("r1", "r2", "r3"))
    gs, gk, gp = (place(n, [P, TILES, G], at=cursor) for n in ("gs", "gk", "gp"))
    te, tend, tbase, one_e = (place(n, [P, E], at=cursor) for n in ("te", "tend", "tbase", "one_e"))
    big_e = place("big_e", [P, SLOT_TILES, E], at=cursor)
    assert cursor[0] <= cst_at
    cursor = [low]
    b13 = place("b13", [P, E, 2 * I], at=cursor)
    b2 = place("b2", [P, E, D], at=cursor)
    hb = place("hb", [P, 2, 2 * I], at=cursor)
    sg = place("sg", [P, 2, I], at=cursor)
    hg = place("hg", [P, 2, I], at=cursor)
    hgT = place("hgT", [P, 2, P], at=cursor)
    assert cursor[0] <= cst_at
    cursor = [cst_at]
    x2T = place("x2T", [P, KC, TOK], at=cursor)
    silu = place("silu", [P, 2, MS, 512], at=cursor)
    assert cursor[0] <= a_at
    cursor = [a_at]
    x2n = place("x2n", [P, 4, D], at=cursor)
    lin = place("lin", [P, 512], at=cursor)
    bs2b = place("bs2b", [P, D], at=cursor)
    ys = place("ys", [P, 8, D], at=[cursor[0]])
    stage = place("stage", [P, 4, 2, ROW], at=cursor)
    xs = place("xs", [P, 4, ROW], at=cursor)
    xsT = place("xsT", [P, 2, KC, P], at=cursor)
    assert cursor[0] <= front_end, (cursor[0], front_end)
    back = place("back", [P, 4, 4, 2, D], at=[w13_at])

    psT = [[ps(f"psT{h}{c}", [P, 4, P]) for c in range(KC)] for h in range(2)]
    psD = [ps(f"psD{h}", [P, 4, P]) for h in range(2)]
    psC = [ps(f"psC{i}", [P, 512]) for i in range(2)]

    psL = psD[0][:, :, :].rearrange("p a b -> p (a b)").rearrange("p (t e) -> p t e", e=E)
    psX = [psD[h][:, 0:2, :].rearrange("p a b -> p (a b)") for h in range(2)]
    psG = [psC[h][:, 0:P] for h in range(2)]
    psH = [psT[0][h][:, 0:2, :].rearrange("p a b -> p (a b)") for h in range(2)]
    psY = [psT[1][h][:, 0:2, :].rearrange("p a b -> p (a b)") for h in range(2)]
    w13f = w13[:, :, :, :].rearrange("p c e i -> p (c e i)")
    w2f = w2[:, :, :].rearrange("p e d -> p (e d)")
    b13f = b13[:, :, :].rearrange("p e i -> p (e i)")
    b2f = b2[:, :, :].rearrange("p e d -> p (e d)")
    EARLY = 6

    def live(i, c):
        return not isinstance(i, int) or 0 <= 8 * i + c < SLOT_TILES

    def head(i, c):
        return isinstance(i, int) and 8 * i + c < 0

    def load_expert(eng, regs, i, c):
        eng.reg_load(regs[c % 4], etab[0:1, bass.ds(8 * i + c, 1)])

    def expert(eng, regs, c):
        return eng.snap(regs[c % 4], min_val=0, max_val=(E - 1) * D)

    def pipeline(eng, step):
        for c in range(-1, 15):
            step(0, c)
        with eng.Fori(1, SLOT_TILES // 8 - 1) as i:
            for c in range(7, 15):
                step(i, c)
        for c in range(SLOT_TILES - 1, SLOT_TILES + 3):
            step(0, c)

    x_loaded = [sem(f"x_loaded{g}") for g in range(4)]
    ctx_loaded = sem("ctx_loaded")
    pads_zeroed = sem("pads_zeroed")
    const_ready = sem("const_ready")
    pool_step = sem("pool_step")
    dve_step = sem("dve_step")
    act_step = sem("act_step")
    var_ready = sem("var_ready")
    std_ready = sem("std_ready")
    norm_ready = sem("norm_ready")
    xn_act = sem("xn_act")
    xn_pool = sem("xn_pool")
    ctx_turned = sem("ctx_turned")
    ctxT_ready = sem("ctxT_ready")
    aa_ready = sem("aa_ready")
    aa_spread = sem("aa_spread")
    aa_done = sem("aa_done")
    turned = sem("turned")
    xT_act = sem("xT_act")
    xT_dve = sem("xT_dve")
    dist_ready = sem("dist_ready")
    dist_used = sem("dist_used")
    clipped = sem("clipped")
    rooted = sem("rooted")
    logged = sem("logged")
    inverted = sem("inverted")
    cost_ready = sem("cost_ready")
    cost_out = sem("cost_out")
    cost_in = sem("cost_in")
    mask_ready = sem("mask_ready")
    mask_out = sem("mask_out")
    mask_in = sem("mask_in")
    mask_turned = sem("mask_turned")
    maskT_ready = sem("maskT_ready")
    maskT_act = sem("maskT_act")
    parts_ready = sem("parts_ready")
    x_nat = sem("x_nat")
    gathered = sem("gathered")
    x2_ready = sem("x2_ready")
    out_done = sem("out_done")
    xn_read = sem("xn_read")
    names = ("weights_loaded gate_turned gate_ready biases_loaded biases1_loaded filled fill_ready var2_ready "
             "std2_ready norm2_ready xn2_ready x2_turned x2T_ready logits_ready shifted expd oh_ready counted "
             "routed staged h_ready silu_ready act_ready z_ready z_used x_turned xT_copied h_done hb_ready "
             "silu_done gated g_turned hgT_copied y_done y_read id_copied combined etab_ready shared_small").split()
    globals_ = {n: sem(n) for n in names}
    (weights_loaded, gate_turned, gate_ready, biases_loaded, biases1_loaded, filled, fill_ready, var2_ready,
     std2_ready, norm2_ready, xn2_ready, x2_turned, x2T_ready, logits_ready, shifted, expd, oh_ready, counted,
     routed, staged, h_ready, silu_ready, act_ready, z_ready, z_used, x_turned, xT_copied, h_done, hb_ready,
     silu_done, gated, g_turned, hgT_copied, y_done, y_read, id_copied, combined, etab_ready, shared_small) = (globals_[n] for n in names)
    tail_in = [sem(f"tail_in{i}") for i in range(4)]
    scattered = [sem(f"scattered{i}") for i in range(4)]
    tagged = sem("tagged")
    xs_loaded = [sem(f"xs_loaded{i}") for i in range(4)]
    res_out = [sem(f"res_out{i}") for i in range(8)]
    zeros_ready = sem("zeros_ready")
    lin_ready = sem("lin_ready")
    passed = sem("passed")

    xk_dram = x.rearrange("b (c k) d -> (b c) k d", k=CH)
    xn_dram = x.rearrange("b (t p) d -> p (b t) d", p=P)
    out_nat = out.rearrange("b (t p) d -> p (b t) d", p=P)

    def skewed(base, row, n_rows, r0):
        return bass.AP(tensor=base.tensor, offset=r0 * row,
                       ap=[[QUAD * NT * row, B], [NT * row + row, QUAD], [1, n_rows * row]])

    with nc.Block() as block:

        @block.sync
        def _(sp):
            for g in range(4):
                sp.dma_start(xk[:, 8 * g:8 * g + 8, :], xk_dram[:, 8 * g:8 * g + 8, :]).then_inc(x_loaded[g], 16)
            sp.dma_start(gw[:, :], gate_w).then_inc(weights_loaded, 16)
            sp.wait_ge(zeros_ready, 1)
            for n in range(0, NT, 16):
                k = min(16, NT - n)
                sp.dma_start(cost_skew[:, n * W:(n + k) * W], zeros[:, 0:k * W]).then_inc(pads_zeroed, 16)
            sp.wait_ge(pads_zeroed, 16 * ((NT + 15) // 16))
            for part, (lo, hi) in enumerate(((0, CUT), (CUT, CTX))):
                sp.wait_ge(cost_ready, part + 1)
                for b in range(B):
                    dst = bass.AP(tensor=cost_skew.tensor, offset=(b * QUAD * NT + lo) * W,
                                  ap=[[(NT + 1) * W, QUAD], [1, (hi - lo) * W]])
                    sp.dma_start(dst, cost[QUAD * b:QUAD * b + QUAD, lo:hi, :].rearrange("p i w -> p (i w)")
                                 ).then_inc(cost_out, 16)
                sp.wait_ge(cost_out, 16 * B * (part + 1))
                if part == 1:
                    hi = NT
                sp.dma_start(cst[:, lo:hi, :].rearrange("p t w -> p (t w)"), cost_skew[:, lo * W:hi * W]
                             ).then_inc(cost_in, 16)
            for c in range(KC):
                for w, lo in ((we1, 0), (we3, I)):
                    sp.dma_start(w13[:, c, :, lo:lo + I], w[:, c * P:(c + 1) * P, :].rearrange("e p i -> p e i")
                                 ).then_inc(biases1_loaded, 16)
            sp.dma_start(w2[:, :, :], we2.rearrange("e p d -> p e d")).then_inc(biases1_loaded, 16)
            sp.dma_start(sw1[:, :, :], ws1.rearrange("(c p) i -> p c i", p=P)).then_inc(shared_small, 16)
            sp.dma_start(sw3[:, :, :], ws3.rearrange("(c p) i -> p c i", p=P)).then_inc(shared_small, 16)
            sp.dma_start(sw2[:, :, :], ws2.rearrange("(c p) d -> p c d", p=P)).then_inc(shared_small, 16)
            with nc.allow_non_contiguous_dma(reason="two columns of biases"):
                sp.dma_start(sb1[:, :], bs1.rearrange("(m p) -> p m", p=P)).then_inc(shared_small, 16)
                sp.dma_start(sb3[:, :], bs3.rearrange("(m p) -> p m", p=P)).then_inc(shared_small, 16)
            sp.dma_start(gb[:, :], gate_b.partition_broadcast(P)).then_inc(shared_small, 16)
            sp.wait_ge(fill_ready, 3)
            for n in range(SLOT_TILES):
                sp.dma_start(slot_rows[n * P:(n + 1) * P, :], fill[:, :]).then_inc(filled, 16)
            sp.wait_ge(turned, 8)
            for g in range(4):
                sp.dma_start(xk[:, 8 * g:8 * g + 8, :], xn_dram[:, 8 * g:8 * g + 8, :]).then_inc(x_nat, 16)
            for part, (lo, hi) in enumerate(((NT // 2, NT), (0, NT // 2))):
                sp.wait_ge(mask_ready, part + 1)
                sp.dma_start(mask_skew[:, lo * CH:hi * CH], mask[:, lo:hi, :].rearrange("p t w -> p (t w)")
                             ).then_inc(mask_out, 16)
            sp.wait_ge(mask_out, 32)
            for b in range(B):
                src = bass.AP(tensor=mask_skew.tensor, offset=b * QUAD * NT * CH,
                              ap=[[(NT + 1) * CH, QUAD], [1, CTX * CH]])
                sp.dma_start(maskU[QUAD * b:QUAD * b + QUAD, :, :].rearrange("p i w -> p (i w)"),
                             src).then_inc(mask_in, 16)
            sp.dma_start(bs2b[:, :], bs2.partition_broadcast(P)).then_inc(lin_ready, 16)
            sp.wait_ge(routed, 1)
            sp.wait_ge(etab_ready, 1)
            sp.dma_start(b13[:, :, 0:I], be1.partition_broadcast(P)).then_inc(biases_loaded, 16)
            sp.dma_start(b13[:, :, I:2 * I], be3.partition_broadcast(P)).then_inc(biases_loaded, 16)
            sp.dma_start(b2[:, :, :], be2.partition_broadcast(P)).then_inc(biases_loaded, 16)

            def load_slots(i, u):
                sp.dma_start(xs[:, u, :], slot_rows[bass.ds((4 * i + u) * P, P), :]).then_inc(xs_loaded[u], 16)

            for u in range(4):
                sp.wait_ge(scattered[u], 2 * 16 * (TILES // 4))
            for u in range(4):
                load_slots(0, u)
            with sp.Fori(1, SLOT_TILES // 4) as i:
                for u in range(4):
                    sp.wait_ge(x_turned, 4 * i + u - 3)
                    sp.wait_ge(id_copied, 4 * i + u - 3)
                    load_slots(i, u)
            for u in range(8):
                sp.wait_ge(res_out[u], 16 * (SLOT_TILES // 8))
            def load_results(g):
                for w in range(2):
                    src = results[w * TOK + g * 4 * P:w * TOK + (g + 1) * 4 * P, :].rearrange("(t p) d -> p t d", p=P)
                    sp.dma_start(back[:, g % 4, :, w, :], src).then_inc(tail_in[g % 4], 16)

            for g in range(4):
                load_results(g)
            for g in range(8):
                sp.wait_ge(combined, 4 * (g + 1))
                if g + 4 < 8:
                    load_results(g + 4)
                sp.dma_start(out_nat[:, 4 * g:4 * g + 4, :], xk[:, 4 * g:4 * g + 4, :]).then_inc(out_done, 16)
            sp.wait_ge(out_done, 16 * 8)

        @block.gpsimd
        def _(pool):
            pool.memset(zeros[:, :], 0.0).then_inc(zeros_ready, 1)
            pool.memset(ident[:, :], 0.0).then_inc(pool_step, 1)
            pool.memset(ones[:, :], 1.0).then_inc(const_ready, 1)
            pool.memset(tiny[:, :], 1e-30).then_inc(fill_ready, 1)
            pool.wait_ge(pool_step, 1)
            pool.affine_select(out=ident[:, :], in_=ident[:, :], compare_op=ALU.not_equal, fill=1.0, base=0,
                               pattern=[[-1, P]], channel_multiplier=1).then_inc(const_ready, 1)
            pool.memset(onesb[:, :], 1.0).then_inc(pool_step, 1)
            pool.memset(tri[:, :], 1.0).then_inc(pool_step, 1)
            pool.memset(low_e[:, :, :], 1.0).then_inc(pool_step, 1)
            pool.wait_ge(pool_step, 4)
            pool.affine_select(out=tri[:, :], in_=tri[:, :], compare_op=ALU.is_gt, fill=0.0, base=0,
                               pattern=[[1, P]], channel_multiplier=-1).then_inc(const_ready, 1)
            pool.affine_select(out=low_e[:, :, :], in_=low_e[:, :, :], compare_op=ALU.is_gt, fill=0.0, base=0,
                               pattern=[[1, G], [-1, G]], channel_multiplier=0).then_inc(const_ready, 1)
            pool.iota(rev_e[:, :], [[-1, E]], base=E, channel_multiplier=0,
                      allow_small_or_imprecise_dtypes=True).then_inc(const_ready, 1)
            pool.iota(full[:, :], [[P, TILES]], base=0, channel_multiplier=0,
                      allow_small_or_imprecise_dtypes=True).then_inc(const_ready, 1)
            pool.iota(tile_no[:, :], [[1, SLOT_TILES]], base=0, channel_multiplier=0,
                      allow_small_or_imprecise_dtypes=True).then_inc(const_ready, 1)
            pool.iota(ids[:, :, :], [[TOK, 2], [P, TILES]], base=0, channel_multiplier=1).then_inc(const_ready, 1)
            pool.memset(fill[:, 0:D], 0.0).then_inc(fill_ready, 1)
            pool.iota(fill[:, D:ROW].bitcast(I32), [[1, 1]], base=DUMP, channel_multiplier=1).then_inc(fill_ready, 1)
            for g in range(4):
                pool.wait_ge(norm_ready, g + 1)
                for k in range(8 * g + 5, 8 * g + 8):
                    pool.tensor_scalar(xk[:, k, :], xk[:, k, :], sm[:, 0, k:k + 1], sm[:, 1, k:k + 1],
                                       ALU.add, ALU.mult).then_inc(xn_pool, 1)
            pool.wait_ge(routed, 1)
            pool.wait_ge(filled, 16 * SLOT_TILES)
            for T in range(TILES):
                pool.wait_ge(staged, T + 1)
                pool.wait_ge(tagged, T + 1)
                for w in range(2):
                    pool.indirect_dma_start(
                        out=slot_rows, out_offset=bass.IndirectOffsetOnAxis(ap=slot[:, w, T:T + 1], axis=0),
                        in_=stage[:, T % 4, w, :], in_offset=None).then_inc(scattered[T % 4], 16)
            with pool.Fori(0, SLOT_TILES // 8) as i:
                for u in range(8):
                    pool.wait_ge(y_read, 8 * i + u + 1)
                    pool.sem_inc(passed, 1)
                    pool.indirect_dma_start(
                        out=results, out_offset=bass.IndirectOffsetOnAxis(ap=idx[:, u:u + 1], axis=0),
                        in_=ys[:, u, :], in_offset=None, bounds_check=DUMP - 1,
                        oob_is_err=False).then_inc(res_out[u], 16)

        @block.scalar
        def _(act):
            act.dma_start(ctx_sb[:, :, :], ctx.rearrange("b i d -> i b d")).then_inc(ctx_loaded, 16)
            act.wait_ge(ctx_turned, 1)
            for c in range(KC):
                act.activation(ctxT[:, c, :, :].rearrange("p b i -> p (b i)"), psC[c][:, 0:B * CTX],
                               ACT.Copy, scale=-2.0).then_inc(ctxT_ready, 1)

            def std(g):
                act.wait_ge(var_ready, g + 1)
                act.activation(sm[:, 3, 8 * g:8 * g + 8], sm[:, 2, 8 * g:8 * g + 8], ACT.Sqrt).then_inc(std_ready, 1)

            def copy_turned(n):
                act.wait_ge(turned, n + 1)
                if n >= 2:
                    act.wait_ge(dist_ready, n - 1)
                act.activation(xT[:, n % 2, 0, :, :], psT[n % 2][0][:, :, :], ACT.Copy).then_inc(xT_act, 1)

            act.wait_ge(fill_ready, 3)

            std(0)
            for g in range(4):
                if g < 3:
                    std(g + 1)
                act.wait_ge(norm_ready, g + 1)
                for k in range(8 * g, 8 * g + 5):
                    act.activation(xk[:, k, :], xk[:, k, :], ACT.Identity, scale=sm[:, 1, k:k + 1],
                                   bias=sm[:, 4, k:k + 1]).then_inc(xn_act, 1)
                copy_turned(2 * g)
                copy_turned(2 * g + 1)
            for part, rows in enumerate(PARTS):
                act.wait_ge(clipped, part + 1)
                act.activation(root[:, rows, 1:W], cost[:, rows, 1:W], ACT.Sqrt).then_inc(rooted, 1)
            for rows in PARTS:
                act.activation(inv[:, rows, 1:W], cost[:, rows, 1:W], ACT.Ln, bias=tiny[:, :]).then_inc(logged, 1)
            for part, rows in enumerate(PARTS):
                act.wait_ge(logged, part + 1)
                act.activation(inv[:, rows, 1:W], inv[:, rows, 1:W], ACT.Exp, scale=-0.5).then_inc(inverted, 1)

            for q in (1, 3):
                act.wait_ge(mask_turned, q + 1)
                src = psT[q // 2][q % 2][0:CTX, :, :].rearrange("p a b -> p (a b)").bitcast(BF16)
                act.activation(maskT[:, :, 8 * q:8 * q + 8], src.rearrange("i (k p) -> i p k", k=8),
                               ACT.Copy).then_inc(maskT_act, 1)

            def turned2(n):
                act.wait_ge(x2_turned, n + 1)
                dst = bass.AP(tensor=x2T, offset=2 * n * P, ap=[[KC * TOK, P], [TOK, KC], [1, 2 * P]])
                act.activation(dst, psT[0][n % 2][:, :, :].rearrange("p (c u) t -> p c (u t)", c=KC),
                               ACT.Copy).then_inc(x2T_ready, 1)

            for g in range(4):
                act.wait_ge(var2_ready, g + 1)
                act.activation(sm[:, 3, 8 * g:8 * g + 8], sm[:, 2, 8 * g:8 * g + 8], ACT.Sqrt).then_inc(std2_ready, 1)
                act.wait_ge(norm2_ready, g + 1)
                for n in range(4 * g, 4 * g + 4):
                    for T in (2 * n, 2 * n + 1):
                        act.activation(x2n[:, T % 4, :], xk[:, T, :], ACT.Identity, scale=sm[:, 1, T:T + 1],
                                       bias=sm[:, 4, T:T + 1]).then_inc(xn2_ready, 1)
                    if n:
                        turned2(n - 1)
            turned2(TILES // 2 - 1)
            act.wait_ge(shifted, 1)
            act.activation(orig[:, :, :], t1[:, :, :], ACT.Exp).then_inc(expd, 1)

            def shared_silu_half(g, m):
                act.wait_ge(h_ready, 2 * g + m + 1)
                if g >= 2:
                    act.wait_ge(z_ready, 2 * (g - 1))
                act.activation(silu[:, g % 2, m, :], psT[m][0][:, :, :].rearrange("p a b -> p (a b)"), ACT.Silu,
                               bias=sb1[:, m:m + 1]).then_inc(silu_ready, 1)

            def stage_tile(T):
                if T >= 4:
                    act.wait_ge(scattered[T % 4], 32 * (T // 4))
                for w in range(2):
                    ins = act.activation(stage[:, T % 4, w, 0:D], xk[:, T, :], ACT.Identity, scale=sm[:, 1, T:T + 1],
                                         bias=sm[:, 4, T:T + 1])
                ins.then_inc(staged, 1)

            act.wait_ge(shared_small, 96)
            act.wait_ge(x2_turned, TILES // 2)
            for g in range(8):
                stage_tile(4 * g)
                stage_tile(4 * g + 1)
                if g < EARLY:
                    shared_silu_half(g, 0)
                stage_tile(4 * g + 2)
                stage_tile(4 * g + 3)
                if g < EARLY:
                    shared_silu_half(g, 1)

            def act_step_of(i, c):
                q = 8 * i + c
                if live(i, c - 1):
                    act.wait_ge(hb_ready, q)
                    if not head(i, c - 3):
                        act.wait_ge(gated, q - 2)
                    act.activation(sg[:, (c - 1) % 2, :], hb[:, (c - 1) % 2, 0:I], ACT.Silu).then_inc(silu_done, 1)
                if live(i, c + 1):
                    act.wait_ge(x_turned, q + 2)
                    if not head(i, c - 1):
                        act.wait_ge(h_done, q)
                    act.activation(xsT[:, (c + 1) % 2, :, :].rearrange("p c t -> p (c t)"),
                                   psX[(c + 1) % 2], ACT.Copy).then_inc(xT_copied, 1)
                if live(i, c - 2):
                    act.wait_ge(g_turned, q - 1)
                    if not head(i, c - 4):
                        act.wait_ge(y_done, q - 3)
                    act.activation(hgT[:, c % 2, :], psG[c % 2], ACT.Copy).then_inc(hgT_copied, 1)

            pipeline(act, act_step_of)
            for g in range(EARLY, 8):
                for m in range(MS):
                    shared_silu_half(g, m)

        @block.tensor
        def _(pe):
            pe.wait_ge(const_ready, 2)
            pe.wait_ge(ctx_loaded, 16)
            for c in range(KC):
                for b in range(B):
                    mm = pe.transpose(psC[c][:, b * CTX:(b + 1) * CTX], ctx_sb[:, b, c * P:(c + 1) * P],
                                      ident[0:CTX, 0:CTX])
            mm.then_inc(ctx_turned, 1)
            pe.wait_ge(weights_loaded, 16)
            for c in range(KC):
                mm = pe.transpose(psD[0][:, c, 0:E], gw[:, c * P:(c + 1) * P], ident[0:E, 0:E])
            mm.then_inc(gate_turned, 1)
            pe.wait_ge(aa_ready, 1)
            pe.wait_ge(ctxT_ready, KC)
            for b in range(B):
                mm = pe.matmul(psC[0][QUAD * b:QUAD * b + QUAD, 0:CTX], ones[0:CTX, :], aa_diag[:, b, :],
                               start=True, stop=True)
            mm.then_inc(aa_spread, 1)

            def warm_up(n):
                for _ in range(n):
                    pe.matmul(psD[1][:, :, :].rearrange("p a b -> p (a b)"), onesb[:, :],
                              onesb[:, :].unsqueeze(1).to_broadcast([P, 4, P]), start=True, stop=True)

            def turn(n):
                g, h = n // 2, n % 2
                pe.wait_ge(xn_act, 5 * g + (4 if h == 0 else 5))
                if h == 1:
                    pe.wait_ge(xn_pool, 3 * g + 3)
                if n >= 2:
                    pe.wait_ge(xT_act, n - 1)
                    pe.wait_ge(xT_dve, n - 1)
                for c in range(KC):
                    for k in range(4):
                        mm = pe.transpose(psT[h][c][:, k, :], xk[:, 4 * n + k, c * P:(c + 1) * P], ident[:, :])
                mm.then_inc(turned, 1)

            def distances(n):
                h = n % 2
                pe.wait_ge(xT_act, n + 1)
                pe.wait_ge(xT_dve, n + 1)
                if n == 0:
                    pe.wait_ge(gate_ready, 1)
                if n >= 2:
                    pe.wait_ge(dist_used, n - 1)
                for k in range(4):
                    for b in range(B):
                        for c in range(KC):
                            mm = pe.matmul(psD[h][QUAD * b:QUAD * b + QUAD, k, 0:CTX],
                                           xT[:, h, c, k, QUAD * b:QUAD * b + QUAD], ctxT[:, c, b, :],
                                           start=(c == 0), stop=(c == KC - 1))
                mm.then_inc(dist_ready, 1)

            for n in range(8):
                turn(n)
                if n >= 1:
                    distances(n - 1)
            distances(7)

            pe.wait_ge(dist_used, 8)
            pe.wait_ge(mask_ready, 2)
            warm_up(16)
            pe.wait_ge(mask_in, 16 * B)
            pe.wait_ge(xT_act, 8)
            pe.wait_ge(xT_dve, 8)
            for q in range(4):
                dst = psT[q // 2][q % 2][0:CTX, :, :].rearrange("p a b -> p (a b)").bitcast(BF16)
                for k in range(8):
                    mm = pe.transpose(dst[:, k * P:(k + 1) * P], maskU[:, :, 8 * q + k], identb[:, :])
                mm.then_inc(mask_turned, 1)
            def gather(n):
                if n >= 2:
                    pe.wait_ge(x2_ready, n - 1)
                for u in range(2):
                    T = 2 * n + u
                    b, j = T // 8, T % 8
                    lhs = maskT[:, 32 * b + 4 * j:32 * b + 4 * j + 4, :].rearrange("i p k -> i (p k)")
                    for part in range(3):
                        mm = pe.matmul(psC[n % 2][:, u * D:(u + 1) * D], lhs, ctx_parts[:, part, b, :],
                                       start=(part == 0), stop=(part == 2))
                mm.then_inc(gathered, 1)

            def logits(n):
                pe.wait_ge(x2T_ready, n + 1)
                for T in range(2 * n, 2 * n + 2):
                    for c in range(KC):
                        mm = pe.matmul(psL[:, T, :], x2T[:, c, T * P:(T + 1) * P], gwT[:, c, :],
                                       start=(c == 0), stop=(c == KC - 1))
                mm.then_inc(logits_ready, 1)

            def turn2(n):
                pe.wait_ge(xn2_ready, 2 * n + 2)
                if n >= 2:
                    pe.wait_ge(x2T_ready, n - 1)
                for u in range(2):
                    for c in range(KC):
                        mm = pe.transpose(psT[0][n % 2][:, 2 * c + u, :], x2n[:, (2 * n + u) % 4, c * P:(c + 1) * P],
                                          ident[:, :])
                mm.then_inc(x2_turned, 1)

            pe.wait_ge(maskT_ready, 2)
            pe.wait_ge(maskT_act, 2)
            pe.wait_ge(parts_ready, 3)
            for g in range(TILES // 8 + 1):
                if g < TILES // 8:
                    for n in range(4 * g, 4 * g + 4):
                        gather(n)
                if g:
                    for n in range(4 * g - 4, 4 * g):
                        turn2(n)
                        if n:
                            logits(n - 1)
            logits(TILES // 2 - 1)
            pe.wait_ge(oh_ready, 1)
            pe.matmul(psD[1][:, :, :].rearrange("p a b -> p (a b)"), tri[:, :],
                      ohb[:, :, :].rearrange("p t e -> p (t e)"), start=True, stop=True)
            pe.matmul(psC[0][:, :], onesb[:, :], ohb[:, :, :].rearrange("p t e -> p (t e)"),
                      start=True, stop=True).then_inc(counted, 1)

            def shared_h(g):
                for m in range(MS):
                    if g >= 1:
                        pe.wait_ge(act_ready, 2 * g + m - 1)
                    for w, ps_ in ((sw1, psT[m][0]), (sw3, psT[m][1])):
                        for c in range(KC):
                            mm = pe.matmul(ps_[:, :, :].rearrange("p a b -> p (a b)"), w[:, c, m * P:(m + 1) * P],
                                           x2T[:, c, 512 * g:512 * g + 512], start=(c == 0), stop=(c == KC - 1))
                    mm.then_inc(h_ready, 1)

            def shared_z(g):
                pe.wait_ge(act_ready, 2 * g + 2)
                for j in range(2):
                    if g >= 1:
                        pe.wait_ge(z_used, 2 * (g - 1) + j + 1)
                    for u in range(2):
                        for m in range(MS):
                            mm = pe.matmul(psC[j][:, u * D:(u + 1) * D],
                                           silu[:, g % 2, m, (2 * j + u) * P:(2 * j + u + 1) * P], sw2[:, m, :],
                                           start=(m == 0), stop=(m == MS - 1))
                    mm.then_inc(z_ready, 1)

            pe.wait_ge(routed, 1)
            pe.wait_ge(shared_small, 96)
            for g in range(EARLY):
                shared_h(g)
                if g:
                    shared_z(g - 1)
            shared_z(EARLY - 1)

            pe_expert = [pe.alloc_register(f"pe_expert{u}") for u in range(4)]

            def pe_step_of(i, c):
                q = 8 * i + c
                if live(i, c + 1):
                    r = c + 1
                    pe.wait_ge(xs_loaded[r % 4], 16 * (2 * i + r // 4 + 1))
                    if not head(i, r - 2):
                        pe.wait_ge(xT_copied, q)
                    for k in range(KC):
                        mm = pe.transpose(psX[r % 2][:, k * P:(k + 1) * P], xs[:, r % 4, k * P:(k + 1) * P], ident[:, :])
                    mm.then_inc(x_turned, 1)
                if live(i, c - 2):
                    pe.wait_ge(gated, q - 1)
                    if not head(i, c - 4):
                        pe.wait_ge(hgT_copied, q - 3)
                    pe.transpose(psG[c % 2], hg[:, c % 2, :], ident[:, :]).then_inc(g_turned, 1)
                if live(i, c):
                    e = expert(pe, pe_expert, c)
                    pe.wait_ge(xT_copied, q + 1)
                    if not head(i, c - 2):
                        pe.wait_ge(hb_ready, q - 1)
                    for k in range(KC):
                        mm = pe.matmul(psH[c % 2], xsT[:, c % 2, k, :], w13f[:, bass.ds(k * E * 2 * I + e, 2 * I)],
                                       start=(k == 0), stop=(k == KC - 1))
                    mm.then_inc(h_done, 1)
                if live(i, c + 1):
                    load_expert(pe, pe_expert, i, c + 1)
                if live(i, c - 2):
                    e = expert(pe, pe_expert, c - 2)
                    pe.wait_ge(hgT_copied, q - 1)
                    if not head(i, c - 4):
                        pe.wait_ge(y_read, q - 3)
                    pe.matmul(psY[c % 2], hgT[:, c % 2, :], w2f[:, bass.ds(e, D)],
                              start=True, stop=True).then_inc(y_done, 1)

            pe.wait_ge(etab_ready, 1)
            pe.wait_ge(biases1_loaded, 80)
            pe.wait_ge(z_used, 2 * EARLY)
            pipeline(pe, pe_step_of)
            pe.wait_ge(y_read, SLOT_TILES)
            pe.wait_ge(hgT_copied, SLOT_TILES)
            for g in range(EARLY, 8):
                shared_h(g)
                if g > EARLY:
                    shared_z(g - 1)
            shared_z(7)

        @block.vector
        def _(dve):
            done = [0]

            def link(ins):
                done[0] += 1
                ins.then_inc(dve_step, 1)
                dve.wait_ge(dve_step, done[0])

            def start(ins):
                done[0] += 1
                ins.then_inc(dve_step, 1)

            def settle():
                dve.wait_ge(dve_step, done[0])

            def moments(g, ready):
                s = slice(8 * g, 8 * g + 8)
                me, m2e, mo, m2o = (stats[:, s, i] for i in (1, 2, 4, 5))
                dve.tensor_tensor(sm[:, 5, s], me, mo, ALU.subtract)
                dve.tensor_tensor(sm[:, 6, s], m2e, m2o, ALU.add)
                link(dve.tensor_tensor(sm[:, 7, s], me, mo, ALU.add))
                dve.tensor_scalar(sm[:, 0, s], sm[:, 7, s], -0.5, None, ALU.mult)
                link(dve.tensor_tensor(sm[:, 5, s], sm[:, 5, s], sm[:, 5, s], ALU.mult))
                link(dve.scalar_tensor_tensor(out=sm[:, 6, s], in0=sm[:, 5, s], scalar=D / 4.0, in1=sm[:, 6, s],
                                              op0=ALU.mult, op1=ALU.add))
                dve.tensor_scalar(sm[:, 2, s], sm[:, 6, s], 1.0 / D, EPS, ALU.mult, ALU.add).then_inc(ready, 1)

            def statistics(g):
                dve.wait_ge(x_loaded[g], 16)
                for k in range(8 * g, 8 * g + 8):
                    ins = dve.bn_stats(stats[:, k, :], xk[:, k, :])
                link(ins)
                moments(g, var_ready)

            def inverse_root(g):
                s = slice(8 * g, 8 * g + 8)
                v, sd, r, t = sm[:, 2, s], sm[:, 3, s], sm[:, 1, s], sm[:, 8, s]
                link(dve.reciprocal(r, sd))
                link(dve.tensor_tensor(t, r, r, ALU.mult))
                link(dve.tensor_tensor(t, t, v, ALU.mult))
                link(dve.tensor_scalar(t, t, -0.5, 1.5, ALU.mult, ALU.add))
                link(dve.tensor_tensor(r, r, t, ALU.mult))

            def norms(g):
                s = slice(8 * g, 8 * g + 8)
                r, t = sm[:, 1, s], sm[:, 8, s]
                dve.wait_ge(std_ready, g + 1)
                inverse_root(g)
                link(dve.tensor_tensor(t, r, r, ALU.mult))
                dve.tensor_tensor(sm[:, 9, s], sm[:, 6, s], t, ALU.mult)
                dve.tensor_tensor(sm[:, 4, s], sm[:, 0, s], r, ALU.mult).then_inc(norm_ready, 1)

            def copy_turned(n):
                dve.wait_ge(turned, n + 1)
                if n >= 2:
                    dve.wait_ge(dist_ready, n - 1)
                dve.tensor_copy(xT[:, n % 2, 1, :, :], psT[n % 2][1][:, :, :]).then_inc(xT_dve, 1)

            def squared(n):
                dve.wait_ge(dist_ready, n + 1)
                for k in range(4):
                    kk = 4 * n + k
                    ins = dve.scalar_tensor_tensor(out=cost[:, :, 1 + kk], in0=psD[n % 2][:, k, 0:CTX],
                                                   scalar=sm[:, 9, kk:kk + 1], in1=aa_row[:, :],
                                                   op0=ALU.add, op1=ALU.add)
                ins.then_inc(dist_used, 1)

            dve.wait_ge(gate_turned, 1)
            for c in range(KC):
                ins = dve.tensor_copy(gwT[:, c, :], psD[0][:, c, 0:E])
            ins.then_inc(gate_ready, 1)
            dve.wait_ge(ctx_loaded, 16)
            for b in range(B):
                ins = dve.tensor_tensor_reduce(out=ctx_rest[:, b, :], in0=ctx_sb[:, b, :], in1=ctx_sb[:, b, :],
                                               scale=1.0, scalar=0.0, op0=ALU.mult, op1=ALU.add,
                                               accum_out=aa[:, b:b + 1])
            link(ins)
            dve.wait_ge(const_ready, 2)
            for b in range(B):
                ins = dve.tensor_scalar(aa_diag[:, b, :], ident[0:CTX, 0:CTX], aa[:, b:b + 1], None, ALU.mult)
            ins.then_inc(aa_ready, 1)
            dve.tensor_copy(identb[:, :], ident[:, :]).then_inc(parts_ready, 1)
            dve.tensor_reduce(first_chunk[:, :], ident[:, 0:P:QUAD], AX.X, ALU.add)
            link(dve.tensor_reduce(last_chunk[:, :], ident[:, QUAD - 1:P:QUAD], AX.X, ALU.add))
            link(dve.memset(cost[:, :, 0:1], BIG))
            link(dve.tensor_scalar(cost[:, :, 0:1], cost[:, :, 0:1], first_chunk[:, :], None, ALU.mult))
            link(dve.memset(cost[:, 0, 0:1], 0.0))
            dve.memset(R[:, 0, :], BIG)
            dve.memset(carry[:, 0:1], BIG)
            dve.memset(A[:, NT, 0:CH], 0.0)
            link(dve.memset(A[:, :, CH:W], 1.0))
            dve.tensor_scalar(A[:, :, CH:W], A[:, :, CH:W], last_chunk[:, :], None, ALU.mult)
            link(dve.tensor_scalar(carry[:, 0:1], carry[:, 0:1], 1.0, None, ALU.mult))
            for b in range(B):
                dve.memset(carry[QUAD * b:QUAD * b + 1, 0:1], 0.0)
            dve.wait_ge(aa_spread, 1)
            link(dve.tensor_copy(aa_row[:, :], psC[0][:, 0:CTX]))

            dve.tensor_copy(ctx_rest[:, :, :], ctx_sb[:, :, :])
            link(dve.tensor_copy(ctx_parts[:, 0, :, :], ctx_sb[:, :, :]))
            link(dve.tensor_tensor(ctx_rest[:, :, :], ctx_rest[:, :, :], ctx_parts[:, 0, :, :], ALU.subtract))
            link(dve.tensor_copy(ctx_parts[:, 1, :, :], ctx_rest[:, :, :]))
            link(dve.tensor_tensor(ctx_rest[:, :, :], ctx_rest[:, :, :], ctx_parts[:, 1, :, :], ALU.subtract))
            dve.tensor_copy(ctx_parts[:, 2, :, :], ctx_rest[:, :, :]).then_inc(parts_ready, 2)

            statistics(0)
            statistics(1)
            norms(0)
            for g in range(4):
                if g + 2 < 4:
                    statistics(g + 2)
                if g + 1 < 4:
                    norms(g + 1)
                copy_turned(2 * g)
                if g:
                    squared(2 * g - 1)
                copy_turned(2 * g + 1)
                squared(2 * g)
            squared(7)
            dve.wait_ge(dist_used, 8)
            for rows in PARTS:
                dve.tensor_scalar(cost[:, rows, 1:W], cost[:, rows, 1:W], 0.0, None, ALU.max).then_inc(clipped, 1)
            for part, rows in enumerate(PARTS):
                c, r, d = (m[:, rows, 1:W] for m in (cost, root, rest))
                dve.wait_ge(rooted, part + 1)
                dve.wait_ge(clipped, part + 1)
                link(dve.tensor_tensor(d, r, r, ALU.mult))
                link(dve.tensor_tensor(d, c, d, ALU.subtract))
            for part, rows in enumerate(PARTS):
                c, r, d, i = (m[:, rows, 1:W] for m in (cost, root, rest, inv))
                dve.wait_ge(inverted, part + 1)
                link(dve.tensor_tensor(d, d, i, ALU.mult))
                dve.scalar_tensor_tensor(out=c, in0=d, scalar=0.5, in1=r, op0=ALU.mult,
                                         op1=ALU.add).then_inc(cost_ready, 1)

            dve.wait_ge(pads_zeroed, 16 * ((NT + 15) // 16))
            link(dve.memset(M[:, :, 0:1], BIG))
            def left_wins(t):
                dve.tensor_tensor(M[:, t, 1:W], R[:, t + 1, 0:CH], M[:, t, 1:W], ALU.is_lt)

            right = [QUAD - 1] + list(range(QUAD - 1))
            for t in range(NT):
                if t == 0 or t == CUT:
                    dve.wait_ge(cost_in, 16 if t == 0 else 32)
                start(dve.tensor_tensor(M[:, t, 1:W], R[:, t, 0:CH], R[:, t, 1:W], ALU.min))
                dve.tensor_tensor(F[:, t, 1:W], R[:, t, 0:CH], R[:, t, 1:W], ALU.is_le)
                settle()
                start(dve.tensor_tensor_scan(R[:, t + 1, :], M[:, t, :], cst[:, t, :], carry[:, t:t + 1],
                                             ALU.min, ALU.add))
                if t:
                    left_wins(t - 1)
                settle()
                if t + 1 < NT:
                    dve.stream_shuffle(carry[:, t + 1:t + 2], R[:, t + 1, CH:W], right)
                if t == 0:
                    link(dve.memset(R[:, 1, 0:1], BIG))
            left_wins(NT - 1)
            dve.memset(carry[:, NT:NT + 1], 0.0)
            link(dve.memset(cst[:, :, CH:W], 1.0))

            def flags(t):
                return dve.scalar_tensor_tensor(out=cst[:, t, 0:CH], in0=F[:, t, 1:W], scalar=0.5, in1=M[:, t, 1:W],
                                                op0=ALU.mult, op1=ALU.max)

            left = list(range(1, QUAD)) + [0]
            link(flags(NT - 1))

            def rev(tns, t):
                return bass.AP(tensor=tns, offset=t * W + CH, ap=[[tns.shape[1] * W, P], [-1, W]])

            def path(t):
                return dve.scalar_tensor_tensor(out=mask[:, t, :], in0=V[:, t, 1:W], scalar=1.0,
                                                in1=A[:, t + 1, 0:CH], op0=ALU.is_ge, op1=ALU.subtract)

            for t in range(NT - 1, -1, -1):
                start(dve.tensor_tensor_scan(rev(V, t), rev(cst, t), rev(A, t + 1), carry[:, t + 1:t + 2],
                                             ALU.mult, ALU.max))
                if t:
                    flags(t - 1)
                settle()
                if t:
                    dve.stream_shuffle(carry[:, t:t + 1], V[:, t, 0:1], left)
                    start(dve.scalar_tensor_tensor(out=A[:, t, 0:CH], in0=cst[:, t, 0:CH], scalar=0.5,
                                                   in1=V[:, t, 0:CH], op0=ALU.mult, op1=ALU.is_lt))
                ins = path(t)
                if t:
                    settle()
                if t in (NT // 2, 0):
                    ins.then_inc(mask_ready, 1)

            for q in (0, 2):
                dve.wait_ge(mask_turned, q + 1)
                src = psT[q // 2][q % 2][0:CTX, :, :].rearrange("p a b -> p (a b)").bitcast(BF16)
                dve.tensor_copy(maskT[:, :, 8 * q:8 * q + 8], src.rearrange("i (k p) -> i p k", k=8)
                                ).then_inc(maskT_ready, 1)
            def statistics2(g):
                dve.wait_ge(x2_ready, 4 * g + 4)
                for T in range(8 * g, 8 * g + 8):
                    ins = dve.bn_stats(stats[:, T, :], xk[:, T, :])
                link(ins)
                moments(g, var2_ready)

            def norms2(g):
                dve.wait_ge(std2_ready, g + 1)
                inverse_root(g)
                s = slice(8 * g, 8 * g + 8)
                dve.tensor_tensor(sm[:, 4, s], sm[:, 0, s], sm[:, 1, s], ALU.mult).then_inc(norm2_ready, 1)

            dve.wait_ge(x_nat, 64)
            for n in range(TILES // 2):
                g = n // 4
                dve.wait_ge(gathered, n + 1)
                pair = xk[:, 2 * n:2 * n + 2, :].rearrange("p t d -> p (t d)")
                dve.tensor_tensor(pair, psC[n % 2][:, :], pair, ALU.add).then_inc(x2_ready, 1)
                if n % 4 == 1 and g:
                    norms2(g - 1)
                if n % 4 == 3:
                    statistics2(g)
            norms2(3)

            def over_e(ap):
                return ap.unsqueeze(2).to_broadcast([P, TILES, E])

            dve.wait_ge(logits_ready, TILES // 2)
            dve.wait_ge(shared_small, 96)
            link(dve.tensor_reduce(r1[:, :], psL, AX.X, ALU.max))
            dve.tensor_tensor(t1[:, :, :], psL, over_e(r1[:, :]), ALU.subtract).then_inc(shifted, 1)
            dve.wait_ge(expd, 1)
            link(dve.tensor_reduce(r2[:, :], orig[:, :, :], AX.X, ALU.add))
            link(dve.reciprocal(r2[:, :], r2[:, :]))
            link(dve.tensor_tensor(orig[:, :, :], orig[:, :, :], over_e(r2[:, :]), ALU.mult))
            link(dve.tensor_tensor(score[:, :, :], orig[:, :, :],
                                   gb[:, :].unsqueeze(1).to_broadcast([P, TILES, E]), ALU.add))
            pr = score[:, :, :].rearrange("p t (h two) -> p (t h) two", two=2)
            HP = TILES * E // 2
            hi = t1[:, :, :].rearrange("p t e -> p (t e)")[:, 0:HP]
            lo = t2[:, :, :].rearrange("p t e -> p (t e)")[:, 0:HP]
            dve.tensor_tensor(hi, pr[:, :, 0], pr[:, :, 1], ALU.max)
            link(dve.tensor_tensor(lo, pr[:, :, 0], pr[:, :, 1], ALU.min))
            hi2, lo2 = (a.rearrange("p (g two) -> p g two", two=2) for a in (hi, lo))
            gsf, gkf, gpf = (a[:, :, :].rearrange("p t g -> p (t g)") for a in (gs, gk, gp))
            dve.tensor_tensor(gsf, hi2[:, :, 0], hi2[:, :, 1], ALU.max)
            dve.tensor_tensor(gkf, hi2[:, :, 0], hi2[:, :, 1], ALU.min)
            link(dve.tensor_tensor(gpf, lo2[:, :, 0], lo2[:, :, 1], ALU.max))
            link(dve.tensor_tensor(gkf, gkf, gpf, ALU.max))
            link(dve.tensor_tensor(gsf, gsf, gkf, ALU.add))
            sq = [P, TILES, G, G]
            other = gs[:, :, :].unsqueeze(2).to_broadcast(sq)
            own = gs[:, :, :].unsqueeze(3).to_broadcast(sq)
            v4 = [a[:, :, :].rearrange("p t (g h) -> p t g h", g=G) for a in (t1, t2)]
            low4 = low_e[:, :, :].unsqueeze(1).to_broadcast(sq)
            dve.wait_ge(const_ready, 8)
            dve.tensor_tensor(v4[0], other, own, ALU.is_gt)
            link(dve.tensor_tensor(v4[1], other, own, ALU.is_equal))
            link(dve.tensor_tensor(v4[1], v4[1], low4, ALU.mult))
            link(dve.tensor_tensor(v4[0], v4[0], v4[1], ALU.add))
            link(dve.tensor_reduce(gk[:, :, :], v4[0], AX.X, ALU.add))
            link(dve.tensor_scalar(gkf, gkf, 1.5, None, ALU.is_lt))
            dve.tensor_scalar(gpf, gkf, -1.0, BIG, ALU.add, ALU.mult)
            sc4, t34 = (a[:, :, :].rearrange("p t (g h) -> p (t g) h", g=G) for a in (score, t3))
            g4 = [P, TILES * G, E // G]
            link(dve.tensor_tensor(t34, sc4, gkf.unsqueeze(2).to_broadcast(g4), ALU.mult))
            link(dve.tensor_tensor(t34, t34, gpf.unsqueeze(2).to_broadcast(g4), ALU.add))
            rev = rev_e[:, :].unsqueeze(1).to_broadcast([P, TILES, E])
            for w, oh in enumerate((oh1, oh2)):
                link(dve.tensor_reduce(r1[:, :], t3[:, :, :], AX.X, ALU.max))
                link(dve.tensor_tensor(t1[:, :, :], t3[:, :, :], over_e(r1[:, :]), ALU.is_equal))
                link(dve.tensor_tensor(t1[:, :, :], t1[:, :, :], rev, ALU.mult))
                link(dve.tensor_reduce(r1[:, :], t1[:, :, :], AX.X, ALU.max))
                link(dve.tensor_tensor(oh[:, :, :], t1[:, :, :], over_e(r1[:, :]), ALU.is_equal))
                if w == 0:
                    dve.scalar_tensor_tensor(out=t3[:, :, :].rearrange("p t e -> p (t e)"),
                                             in0=oh[:, :, :].rearrange("p t e -> p (t e)"), scalar=-4.0 * BIG,
                                             in1=t3[:, :, :].rearrange("p t e -> p (t e)"),
                                             op0=ALU.mult, op1=ALU.add)
                link(dve.tensor_tensor(t2[:, :, :], orig[:, :, :], oh[:, :, :], ALU.mult))
                link(dve.tensor_reduce(wt[:, w, :], t2[:, :, :], AX.X, ALU.add))
            dve.tensor_tensor(ohb[:, :, :], oh1[:, :, :], oh2[:, :, :], ALU.add).then_inc(oh_ready, 1)

            dve.memset(keep_on[:, :, :], 1.0)
            link(dve.memset(one_e[:, :], 1.0))
            link(dve.memset(keep_on[:, :, 0:1], 0.0))
            dve.wait_ge(counted, 1)
            psn = psC[0][:, :].rearrange("p (t e) -> p e t", e=E)
            link(dve.tensor_copy(cnt[:, :, :], psn))
            link(dve.tensor_tensor_scan(upto[:, :, :].rearrange("p e t -> p (e t)"),
                                        keep_on[:, :, :].rearrange("p e t -> p (e t)"),
                                        cnt[:, :, :].rearrange("p e t -> p (e t)"), 0.0, ALU.mult, ALU.add))
            sq = [P, E, TILES]
            link(dve.tensor_tensor(keep_on[:, :, :], upto[:, :, TILES - 1:TILES].to_broadcast(sq),
                                   full[:, :].unsqueeze(1).to_broadcast(sq), ALU.is_gt))
            link(dve.tensor_reduce(te[:, :], keep_on[:, :, :], AX.X, ALU.add))
            link(dve.tensor_tensor_scan(tend[:, :], one_e[:, :], te[:, :], 0.0, ALU.mult, ALU.add))
            link(dve.tensor_tensor(tbase[:, :], tend[:, :], te[:, :], ALU.subtract))
            link(dve.tensor_scalar(tbase[:, :], tbase[:, :], float(P), None, ALU.mult))
            link(dve.tensor_tensor(cnt[:, :, :], upto[:, :, :], cnt[:, :, :], ALU.subtract))
            link(dve.tensor_tensor(cnt[:, :, :], cnt[:, :, :], tbase[:, :].unsqueeze(2).to_broadcast(sq), ALU.add))
            rank = psD[1][:, :, :].rearrange("p a b -> p (a b)").rearrange("p (t e) -> p t e", e=E)
            link(dve.tensor_tensor(t3[:, :, :], rank, cnt[:, :, :].rearrange("p e t -> p t e"), ALU.add))
            for w, oh in enumerate((oh1, oh2)):
                link(dve.tensor_tensor(t1[:, :, :], t3[:, :, :], oh[:, :, :], ALU.mult))
                link(dve.tensor_reduce(r1[:, :], t1[:, :, :], AX.X, ALU.add))
                ins = dve.tensor_copy(slot[:, w, :], r1[:, :])
                if w == 0:
                    link(ins)
            ins.then_inc(routed, 1)
            sq = [P, SLOT_TILES, E]
            link(dve.tensor_tensor(big_e[:, :, :], tend[:, :].unsqueeze(1).to_broadcast(sq),
                                   tile_no[:, :].unsqueeze(2).to_broadcast(sq), ALU.is_le))
            link(dve.tensor_reduce(lin[:, 0:SLOT_TILES], big_e[:, :, :], AX.X, ALU.add))
            dve.tensor_scalar(etab[:, :], lin[:, 0:SLOT_TILES], float(E - 1), float(D),
                              ALU.min, ALU.mult).then_inc(etab_ready, 1)

            def tag_tile(T):
                if T >= 4:
                    dve.wait_ge(scattered[T % 4], 32 * (T // 4))
                dve.tensor_copy(stage[:, T % 4, :, D:ROW].bitcast(I32), ids[:, :, T:T + 1]).then_inc(tagged, 1)

            def shared_act(g):
                for m in range(MS):
                    dve.wait_ge(silu_ready, 2 * g + m + 1)
                    dve.scalar_tensor_tensor(out=silu[:, g % 2, m, :],
                                             in0=psT[m][1][:, :, :].rearrange("p a b -> p (a b)"),
                                             scalar=sb3[:, m:m + 1], in1=silu[:, g % 2, m, :],
                                             op0=ALU.add, op1=ALU.mult).then_inc(act_ready, 1)

            def shared_add(g):
                dve.wait_ge(staged, 4 * g + 4)
                for j in range(2):
                    n = 2 * g + j
                    dve.wait_ge(z_ready, n + 1)
                    if n:
                        dve.wait_ge(z_used, n)
                    pair = xk[:, 2 * n:2 * n + 2, :]
                    link(dve.tensor_tensor(lin[:, :].rearrange("p (t d) -> p t d", t=2),
                                           psC[j][:, :].rearrange("p (t d) -> p t d", t=2),
                                           bs2b[:, :].unsqueeze(1).to_broadcast([P, 2, D]), ALU.add))
                    dve.tensor_tensor(pair.rearrange("p t d -> p (t d)"), lin[:, :],
                                      pair.rearrange("p t d -> p (t d)"), ALU.add).then_inc(z_used, 1)

            dve.wait_ge(etab_ready, 1)
            dve.wait_ge(lin_ready, 16)
            for g in range(8):
                for T in range(4 * g, 4 * g + 4):
                    tag_tile(T)
                    if g < EARLY and T % 4 == 1:
                        shared_act(g)
                if 1 <= g <= EARLY:
                    shared_add(g - 1)

            dve_expert = [dve.alloc_register(f"dve_expert{u}") for u in range(4)]

            def dve_step_of(i, c):
                q = 8 * i + c
                if live(i, c - 3):
                    r = c - 3
                    e = expert(dve, dve_expert, r)
                    dve.wait_ge(y_done, q - 2)
                    if not head(i, r - 8):
                        dve.wait_ge(res_out[r % 8], 16 * (i + r // 8))
                    dve.tensor_tensor(ys[:, r % 8, :], psY[r % 2], b2f[:, bass.ds(e, D)],
                                      ALU.add).then_inc(y_read, 1)
                if live(i, c - 1):
                    r = c - 1
                    dve.wait_ge(silu_done, q)
                    if not head(i, r - 2):
                        dve.wait_ge(g_turned, q - 2)
                    dve.tensor_tensor(hg[:, r % 2, :], sg[:, r % 2, :], hb[:, r % 2, I:2 * I],
                                      ALU.mult).then_inc(gated, 1)
                if live(i, c):
                    e = expert(dve, dve_expert, c)
                    dve.wait_ge(xs_loaded[c % 4], 16 * (2 * i + c // 4 + 1))
                    if not head(i, c - 8):
                        dve.wait_ge(res_out[c % 8], 16 * (i + c // 8))
                    dve.tensor_copy(idx[:, c % 8:c % 8 + 1], xs[:, c % 4, D:ROW].bitcast(I32)).then_inc(id_copied, 1)
                    dve.wait_ge(h_done, q + 1)
                    if not head(i, c - 2):
                        dve.wait_ge(gated, q - 1)
                    dve.tensor_tensor(hb[:, c % 2, :], psH[c % 2], b13f[:, bass.ds(e, 2 * I)],
                                      ALU.add).then_inc(hb_ready, 1)
                if live(i, c + 1):
                    load_expert(dve, dve_expert, i, c + 1)

            dve.wait_ge(biases_loaded, 48)
            pipeline(dve, dve_step_of)
            def combine(g):
                dve.wait_ge(tail_in[g % 4], 32 * (g // 4 + 1))
                for T in range(4 * g, 4 * g + 4):
                    link(dve.scalar_tensor_tensor(out=xk[:, T, :], in0=back[:, g % 4, T % 4, 0, :],
                                                  scalar=wt[:, 0, T:T + 1], in1=xk[:, T, :],
                                                  op0=ALU.mult, op1=ALU.add))
                    dve.scalar_tensor_tensor(out=xk[:, T, :], in0=back[:, g % 4, T % 4, 1, :],
                                             scalar=wt[:, 1, T:T + 1], in1=xk[:, T, :],
                                             op0=ALU.mult, op1=ALU.add).then_inc(combined, 1)

            shared_act(EARLY)
            for g in range(EARLY + 1, 8):
                combine(g - EARLY - 1)
                shared_act(g)
                shared_add(g - 1)
            combine(7 - EARLY)
            shared_add(7)
            for g in range(8 - EARLY, 8):
                combine(g)


def kernel(**inputs):
    import numpy as _np
    import concourse.bacc as _bacc
    from concourse import mybir as _mybir
    from concourse.bass_utils import run_bass_kernel_spmd as _run

    nc = _bacc.Bacc("TRN2", target_bir_lowering=False, num_devices=1)
    arrays, args = {}, []
    names = ["x", "ctx_1024"] + ["L0_ffn_" + n for n in (
        "gate_w gate_b We1 be1 We2 be2 We3 be3 ws1 bs1 ws2 bs2 ws3 bs3").split()]
    for name in names:
        a = _np.ascontiguousarray(inputs[name])
        arrays[f"in_{name}"] = a
        args.append(nc.dram_tensor(f"in_{name}", a.shape, _mybir.dt.from_np(a.dtype), kind="ExternalInput").ap())
    out = nc.dram_tensor("out_0", (4, 1024, 256), _mybir.dt.float32, kind="ExternalOutput").ap()
    build(nc, *args, out)
    r = _run(nc, [arrays], core_ids=[0])
    return r.results[0]["out_0"]
```

```python
import concourse.bass as bass
from concourse import mybir

ALU = mybir.AluOpType
ACT = mybir.ActivationFunctionType
AX = mybir.AxisListType
F32 = mybir.dt.float32
BF16 = mybir.dt.bfloat16
I32 = mybir.dt.int32

P = 128
QUAD = 32
B, S, D = 4, 1024, 256
CTX = 77
KC = D // P
CH = S // QUAD
W = CH + 1
CUT = 16
PARTS = (slice(0, CUT), slice(CUT, CTX))
NT = CTX + QUAD - 1
TILES = B * S // P
TOK = B * S
E = 16
G = 4
I = 128
MS = 2
SLOT_TILES = 80
SLOTS = SLOT_TILES * P
ROW = D + 1
DUMP = 2 * TOK
BIG = 1e30
EPS = 1e-5
ROUND = 1.5 * 2.0 ** 23
STAGES = 6


def build(nc, x, ctx, gate_w, gate_b, we1, be1, we2, be2, we3, be3, ws1, bs1, ws2, bs2, ws3, bs3, out):
    def sb(name, shape, dt=F32):
        return nc.alloc_sbuf_tensor(name, shape, dt)

    def ps(name, shape, dt=F32):
        return nc.alloc_psum_tensor(name, shape, dt)

    def sem(name):
        return nc.alloc_semaphore(name)

    cost_skew = nc.dram_tensor("cost_skew", (P, NT * W), F32, kind="Internal").ap()
    mask_skew = nc.dram_tensor("mask_skew", (P, NT * CH), BF16, kind="Internal").ap()

    slot_rows = nc.dram_tensor("slot_rows", (SLOTS, ROW), F32, kind="Internal").ap()
    results = nc.dram_tensor("results", (DUMP, D), F32, kind="Internal").ap()

    top = [(nc.sbuf_base + 63) // 64 * 64]

    def size(shape, dt):
        n = 2 if dt is BF16 else 4
        for k in shape[1:]:
            n *= k
        return (n + 31) // 32 * 32

    def place(name, shape, dt=F32, at=None):
        cursor = top if at is None else at
        off = cursor[0]
        cursor[0] = off + size(shape, dt)
        assert cursor[0] <= nc.sbuf_usable_end, (name, cursor[0])
        return nc.alloc_sbuf_tensor_at(name, shape, dt, offset=off)

    ident = place("ident", [P, P])
    identb = place("identb", [P, P], BF16)
    ones = place("ones", [P, QUAD])
    stats = place("stats", [P, CH, 6])
    sm = place("sm", [P, 10, CH])
    first_chunk = place("first_chunk", [P, 1])
    last_chunk = place("last_chunk", [P, 1])
    tiny = place("tiny", [P, 1])
    xk = place("xk", [P, CH, D])
    w13_at = top[0]
    w13 = place("w13", [P, KC, E, 2 * I])
    w2 = place("w2", [P, E, D])
    sw1 = place("sw1", [P, KC, MS * I])
    sw3 = place("sw3", [P, KC, MS * I])
    sw2 = place("sw2", [P, MS, D])
    sb1 = place("sb1", [P, MS])
    sb3 = place("sb3", [P, MS])
    gwT = place("gwT", [P, KC, E])
    gb = place("gb", [P, E])
    fill = place("fill", [P, ROW])
    not_before = place("not_before", [P, P], BF16)
    onesb = place("onesb", [P, P], BF16)
    gw = place("gw", [E, D])
    ids = place("ids", [P, 2, TILES])
    slot = place("slot", [P, 2, TILES], I32)
    wt = place("wt", [P, 2, TILES])
    etab = place("etab", [P, SLOT_TILES], I32)
    idx = place("idx", [P, 8], I32)
    low_e = place("low_e", [P, G, G])
    rev_e = place("rev_e", [P, E])
    tile_no = place("tile_no", [P, SLOT_TILES])

    low = top[0]
    cost = place("cost", [P, CTX, W])
    r_at = top[0]
    R = place("R", [P, NT + 1, W])
    m_at = top[0]
    M = place("M", [P, NT, W])
    cst_at = top[0]
    cst = place("cst", [P, NT, W])
    f_at = top[0]
    F = place("F", [P, NT, W])
    v_at = top[0]
    V = place("V", [P, NT + 1, W])
    a_at = top[0]
    A = place("A", [P, NT + 1, W], BF16)
    xT = place("xT", [P, 2, KC, 4, P])
    ctx_sb = place("ctx_sb", [CTX, B, D])
    ctx_rest = place("ctx_rest", [CTX, B, D])
    ctxT = place("ctxT", [P, KC, B, CTX])
    aa_diag = place("aa_diag", [CTX, B, CTX])
    front_end = top[0]
    aa = place("aa", [CTX, B])
    aa_row = place("aa_row", [P, CTX])
    carry = place("carry", [P, NT + 1])
    ctx_parts = place("ctx_parts", [CTX, 3, B, D], BF16)
    root = place("root", [P, CTX, W], at=[v_at])
    inv = place("inv", [P, CTX, W], at=[f_at])
    rest = place("rest", [P, CTX, W], at=[cst_at])
    zeros = place("zeros", [P, W * 16], at=[m_at])
    cursor = [r_at]
    mask = place("mask", [P, NT, CH], BF16, at=cursor)
    maskU = place("maskU", [P, CTX, CH], BF16, at=cursor)
    maskT = place("maskT", [CTX, P, CH], BF16, at=[m_at])
    cursor = [low]
    orig, score, t1, t2, t3, oh1, oh2 = (place(n, [P, TILES, E], at=cursor)
                                         for n in ("orig", "score", "t1", "t2", "t3", "oh1", "oh2"))
    ohb = place("ohb", [P, TILES, E], BF16, at=cursor)
    keep_on = place("keep_on", [P, E, TILES], at=cursor)
    upto = place("upto", [P, E, TILES], at=cursor)
    r1, r2 = (place(n, [P, TILES], at=cursor) for n in ("r1", "r2"))
    gs, gk, gp = (place(n, [P, TILES, G], at=cursor) for n in ("gs", "gk", "gp"))
    te, tend, tbase, one_e = (place(n, [P, E], at=cursor) for n in ("te", "tend", "tbase", "one_e"))
    big_e = place("big_e", [P, SLOT_TILES, E], at=cursor)
    assert cursor[0] <= cst_at
    cursor = [low]
    b13 = place("b13", [P, E, 2 * I], at=cursor)
    b2 = place("b2", [P, E, D], at=cursor)
    hb = place("hb", [P, 2, 2 * I], at=cursor)
    sg = place("sg", [P, 2, I], at=cursor)
    hg = place("hg", [P, 2, I], at=cursor)
    hgT = place("hgT", [P, 2, P], at=cursor)
    assert cursor[0] <= cst_at
    cursor = [cst_at]
    x2T = place("x2T", [P, KC, TOK], at=cursor)
    silu = place("silu", [P, 2, MS, 512], at=cursor)
    assert cursor[0] <= a_at
    cursor = [a_at]
    tmp = place("tmp", [P, 512], at=cursor)
    bs2b = place("bs2b", [P, D], at=cursor)
    x2n = place("x2n", [P, 4, D], at=[cursor[0]])
    ys = place("ys", [P, 8, D], at=[cursor[0]])
    stage = place("stage", [P, STAGES, 2, ROW], at=cursor)
    xs = place("xs", [P, 4, ROW], at=cursor)
    xsT = place("xsT", [P, 2, KC, P], at=cursor)
    assert cursor[0] <= front_end, (cursor[0], front_end)
    back = place("back", [P, 4, 4, 2, D], at=[w13_at])

    by_e = silu[0:E, 1, :, :]

    psT = [[ps(f"psT{h}{c}", [P, 4, P]) for c in range(KC)] for h in range(2)]
    psD = [ps(f"psD{h}", [P, 4, P]) for h in range(2)]
    psC = [ps(f"psC{i}", [P, 512]) for i in range(2)]

    HT = TILES // 2
    psL = [psD[h][:, 0:2, :].rearrange("p a b -> p (a b)").rearrange("p (t e) -> p t e", e=E) for h in range(2)]
    psE = [psT[1][h][0:E, :, :].rearrange("p a b -> p (a b)") for h in range(2)]
    psX = [psD[h][:, 0:2, :].rearrange("p a b -> p (a b)") for h in range(2)]
    psG = [psC[h][:, 0:P] for h in range(2)]
    psH = [psT[0][h][:, 0:2, :].rearrange("p a b -> p (a b)") for h in range(2)]
    psY = [psT[1][h][:, 0:2, :].rearrange("p a b -> p (a b)") for h in range(2)]
    w13f = w13[:, :, :, :].rearrange("p c e i -> p (c e i)")
    w2f = w2[:, :, :].rearrange("p e d -> p (e d)")
    b13f = b13[:, :, :].rearrange("p e i -> p (e i)")
    b2f = b2[:, :, :].rearrange("p e d -> p (e d)")
    EARLY = 8

    def staged_by(n):
        k = 2 * EARLY - 4
        return range(STAGES + (TILES - STAGES) * (n - 4) // k, STAGES + (TILES - STAGES) * (n - 3) // k)

    def live(i, c):
        return not isinstance(i, int) or 0 <= 8 * i + c < SLOT_TILES

    def head(i, c):
        return isinstance(i, int) and 8 * i + c < 0

    def load_expert(eng, regs, i, c):
        eng.reg_load(regs[c % 4], etab[0:1, bass.ds(8 * i + c, 1)])

    def expert(eng, regs, c):
        return eng.snap(regs[c % 4], min_val=0, max_val=(E - 1) * D)

    def pipeline(eng, step):
        for c in range(-1, 15):
            step(0, c)
        with eng.Fori(1, SLOT_TILES // 8 - 1) as i:
            for c in range(7, 15):
                step(i, c)
        for c in range(SLOT_TILES - 1, SLOT_TILES + 3):
            step(0, c)

    x_loaded = [sem(f"x_loaded{g}") for g in range(4)]
    ctx_loaded = sem("ctx_loaded")
    pads_zeroed = sem("pads_zeroed")
    const_ready = sem("const_ready")
    pool_step = sem("pool_step")
    dve_step = sem("dve_step")
    var_ready = sem("var_ready")
    std_ready = sem("std_ready")
    norm_ready = sem("norm_ready")
    xn_act = sem("xn_act")
    xn_pool = sem("xn_pool")
    ctx_turned = sem("ctx_turned")
    ctxT_ready = sem("ctxT_ready")
    aa_ready = sem("aa_ready")
    aa_spread = sem("aa_spread")
    turned = sem("turned")
    xT_act = sem("xT_act")
    xT_dve = sem("xT_dve")
    dist_ready = sem("dist_ready")
    dist_used = sem("dist_used")
    clipped = sem("clipped")
    rooted = sem("rooted")
    logged = sem("logged")
    inverted = sem("inverted")
    cost_ready = sem("cost_ready")
    cost_out = sem("cost_out")
    cost_in = sem("cost_in")
    mask_ready = sem("mask_ready")
    mask_out = sem("mask_out")
    mask_in = sem("mask_in")
    mask_turned = sem("mask_turned")
    maskT_ready = sem("maskT_ready")
    maskT_act = sem("maskT_act")
    parts_ready = sem("parts_ready")
    x_nat = sem("x_nat")
    gathered = sem("gathered")
    x2_ready = sem("x2_ready")
    out_done = sem("out_done")
    weights_loaded = sem("weights_loaded")
    gate_turned = sem("gate_turned")
    gate_ready = sem("gate_ready")
    biases_loaded = sem("biases_loaded")
    expert_weights_loaded = sem("expert_weights_loaded")
    filled = sem("filled")
    fill_ready = sem("fill_ready")
    var2_ready = sem("var2_ready")
    std2_ready = sem("std2_ready")
    norm2_ready = sem("norm2_ready")
    xn2_act = sem("xn2_act")
    x2_turned = sem("x2_turned")
    x2T_ready = sem("x2T_ready")
    logits_ready = sem("logits_ready")
    shifted = sem("shifted")
    expd = sem("expd")
    oh_ready = sem("oh_ready")
    counted = sem("counted")
    routed = sem("routed")
    staged = sem("staged")
    h_ready = sem("h_ready")
    silu_ready = sem("silu_ready")
    act_ready = sem("act_ready")
    z_ready = sem("z_ready")
    z_used = sem("z_used")
    x_turned = sem("x_turned")
    xT_copied = sem("xT_copied")
    h_done = sem("h_done")
    hb_ready = sem("hb_ready")
    silu_done = sem("silu_done")
    gated = sem("gated")
    g_turned = sem("g_turned")
    hgT_copied = sem("hgT_copied")
    y_done = sem("y_done")
    y_read = sem("y_read")
    id_copied = sem("id_copied")
    combined = sem("combined")
    etab_ready = sem("etab_ready")
    shared_small = sem("shared_small")
    tail_in = [sem(f"tail_in{i}") for i in range(4)]
    scattered = [sem(f"scattered{i}") for i in range(STAGES)]
    split_step = sem("split_step")
    counts_read = sem("counts_read")
    xn2_pool = sem("xn2_pool")
    gate_done = sem("gate_done")
    gate_copied = sem("gate_copied")
    xs_loaded = [sem(f"xs_loaded{i}") for i in range(4)]
    res_out = [sem(f"res_out{i}") for i in range(8)]
    zeros_ready = sem("zeros_ready")
    bs2_loaded = sem("bs2_loaded")
    passed = sem("passed")

    xk_dram = x.rearrange("b (c k) d -> (b c) k d", k=CH)
    xn_dram = x.rearrange("b (t p) d -> p (b t) d", p=P)
    results_in = results.rearrange("(p t w) d -> p t w d", t=TILES, w=2)
    out_nat = out.rearrange("b (t p) d -> p (b t) d", p=P)

    with nc.Block() as block:

        @block.sync
        def _(sp):
            for g in range(4):
                sp.dma_start(xk[:, 8 * g:8 * g + 8, :], xk_dram[:, 8 * g:8 * g + 8, :]).then_inc(x_loaded[g], 16)
            sp.wait_ge(zeros_ready, 1)
            for n in range(0, NT, 16):
                k = min(16, NT - n)
                sp.dma_start(cost_skew[:, n * W:(n + k) * W], zeros[:, 0:k * W]).then_inc(pads_zeroed, 16)
            sp.wait_ge(pads_zeroed, 16 * ((NT + 15) // 16))
            for part, (lo, hi) in enumerate(((0, CUT), (CUT, CTX))):
                sp.wait_ge(cost_ready, part + 1)
                for b in range(B):
                    dst = bass.AP(tensor=cost_skew.tensor, offset=(b * QUAD * NT + lo) * W,
                                  ap=[[(NT + 1) * W, QUAD], [1, (hi - lo) * W]])
                    sp.dma_start(dst, cost[QUAD * b:QUAD * b + QUAD, lo:hi, :].rearrange("p i w -> p (i w)")
                                 ).then_inc(cost_out, 16)
                sp.wait_ge(cost_out, 16 * B * (part + 1))
                if part == 1:
                    hi = NT
                sp.dma_start(cst[:, lo:hi, :].rearrange("p t w -> p (t w)"), cost_skew[:, lo * W:hi * W]
                             ).then_inc(cost_in, 16)
            for c in range(KC):
                for w, lo in ((we1, 0), (we3, I)):
                    sp.dma_start(w13[:, c, :, lo:lo + I], w[:, c * P:(c + 1) * P, :].rearrange("e p i -> p e i")
                                 ).then_inc(expert_weights_loaded, 16)
            sp.dma_start(w2[:, :, :], we2.rearrange("e p d -> p e d")).then_inc(expert_weights_loaded, 16)
            sp.dma_start(sw1[:, :, :], ws1.rearrange("(c p) i -> p c i", p=P)).then_inc(shared_small, 16)
            sp.dma_start(sw3[:, :, :], ws3.rearrange("(c p) i -> p c i", p=P)).then_inc(shared_small, 16)
            sp.dma_start(sw2[:, :, :], ws2.rearrange("(c p) d -> p c d", p=P)).then_inc(shared_small, 16)
            with nc.allow_non_contiguous_dma(reason="two columns of biases"):
                sp.dma_start(sb1[:, :], bs1.rearrange("(m p) -> p m", p=P)).then_inc(shared_small, 16)
                sp.dma_start(sb3[:, :], bs3.rearrange("(m p) -> p m", p=P)).then_inc(shared_small, 16)
            sp.dma_start(gb[:, :], gate_b.partition_broadcast(P)).then_inc(shared_small, 16)
            sp.wait_ge(fill_ready, 3)
            for n in range(SLOT_TILES):
                sp.dma_start(slot_rows[n * P:(n + 1) * P, :], fill[:, :]).then_inc(filled, 16)
            sp.wait_ge(turned, 8)
            for g in range(4):
                sp.dma_start(xk[:, 8 * g:8 * g + 8, :], xn_dram[:, 8 * g:8 * g + 8, :]).then_inc(x_nat, 16)
            for part, (lo, hi) in enumerate(((NT // 2, NT), (0, NT // 2))):
                sp.wait_ge(mask_ready, part + 1)
                sp.dma_start(mask_skew[:, lo * CH:hi * CH], mask[:, lo:hi, :].rearrange("p t w -> p (t w)")
                             ).then_inc(mask_out, 16)
            sp.wait_ge(mask_out, 32)
            for b in range(B):
                src = bass.AP(tensor=mask_skew.tensor, offset=b * QUAD * NT * CH,
                              ap=[[(NT + 1) * CH, QUAD], [1, CTX * CH]])
                sp.dma_start(maskU[QUAD * b:QUAD * b + QUAD, :, :].rearrange("p i w -> p (i w)"),
                             src).then_inc(mask_in, 16)
            sp.dma_start(bs2b[:, :], bs2.partition_broadcast(P)).then_inc(bs2_loaded, 16)
            sp.wait_ge(routed, 2)
            sp.wait_ge(etab_ready, 1)
            sp.dma_start(b13[:, :, 0:I], be1.partition_broadcast(P)).then_inc(biases_loaded, 16)
            sp.dma_start(b13[:, :, I:2 * I], be3.partition_broadcast(P)).then_inc(biases_loaded, 16)
            sp.dma_start(b2[:, :, :], be2.partition_broadcast(P)).then_inc(biases_loaded, 16)

            def load_slots(i, u):
                sp.dma_start(xs[:, u, :], slot_rows[bass.ds((4 * i + u) * P, P), :]).then_inc(xs_loaded[u], 16)

            for u in range(STAGES):
                sp.wait_ge(scattered[u], 2 * 16 * len(range(u, TILES, STAGES)))
            for u in range(4):
                load_slots(0, u)
            with sp.Fori(1, SLOT_TILES // 4) as i:
                for u in range(4):
                    sp.wait_ge(x_turned, 4 * i + u - 3)
                    sp.wait_ge(id_copied, 4 * i + u - 3)
                    load_slots(i, u)
            for u in range(8):
                sp.wait_ge(res_out[u], 16 * (SLOT_TILES // 8))
            def load_results(g):
                sp.dma_start(back[:, g % 4, :, :, :], results_in[:, 4 * g:4 * g + 4, :, :]).then_inc(tail_in[g % 4], 16)

            for g in range(4):
                load_results(g)
            for g in range(8):
                sp.wait_ge(combined, g + 1)
                if g + 4 < 8:
                    load_results(g + 4)
                sp.dma_start(out_nat[:, 4 * g:4 * g + 4, :], xk[:, 4 * g:4 * g + 4, :]).then_inc(out_done, 16)
            sp.wait_ge(out_done, 16 * 8)

        @block.gpsimd
        def _(pool):
            pool.memset(zeros[:, :], 0.0).then_inc(zeros_ready, 1)
            pool.memset(ident[:, :], 0.0).then_inc(pool_step, 1)
            pool.memset(ones[:, :], 1.0).then_inc(const_ready, 1)
            pool.memset(tiny[:, :], 1e-30).then_inc(fill_ready, 1)
            pool.wait_ge(pool_step, 1)
            pool.affine_select(out=ident[:, :], in_=ident[:, :], compare_op=ALU.not_equal, fill=1.0, base=0,
                               pattern=[[-1, P]], channel_multiplier=1).then_inc(const_ready, 1)
            pool.memset(onesb[:, :], 1.0).then_inc(pool_step, 1)
            pool.memset(not_before[:, :], -1.0).then_inc(pool_step, 1)
            pool.memset(low_e[:, :, :], 1.0).then_inc(pool_step, 1)
            pool.wait_ge(pool_step, 4)
            pool.affine_select(out=not_before[:, :], in_=not_before[:, :], compare_op=ALU.is_ge, fill=0.0, base=0,
                               pattern=[[-1, P]], channel_multiplier=1).then_inc(const_ready, 1)
            pool.affine_select(out=low_e[:, :, :], in_=low_e[:, :, :], compare_op=ALU.is_gt, fill=0.0, base=0,
                               pattern=[[1, G], [-1, G]], channel_multiplier=0).then_inc(const_ready, 1)
            pool.iota(rev_e[:, :], [[-1, E]], base=E, channel_multiplier=0,
                      allow_small_or_imprecise_dtypes=True).then_inc(const_ready, 1)
            pool.iota(tile_no[:, :], [[1, SLOT_TILES]], base=0, channel_multiplier=0,
                      allow_small_or_imprecise_dtypes=True).then_inc(const_ready, 1)
            pool.iota(ids[:, :, :], [[1, 2], [2, TILES]], base=0, channel_multiplier=2 * TILES,
                      allow_small_or_imprecise_dtypes=True).then_inc(const_ready, 1)
            pool.memset(fill[:, 0:D], 0.0).then_inc(fill_ready, 1)
            pool.iota(fill[:, D:ROW], [[1, 1]], base=DUMP, channel_multiplier=1,
                      allow_small_or_imprecise_dtypes=True).then_inc(fill_ready, 1)
            for g in range(4):
                pool.wait_ge(norm_ready, g + 1)
                for k in range(8 * g + 5, 8 * g + 8):
                    pool.tensor_scalar(xk[:, k, :], xk[:, k, :], sm[:, 0, k:k + 1], sm[:, 1, k:k + 1],
                                       ALU.add, ALU.mult).then_inc(xn_pool, 1)
            pool.wait_ge(ctx_loaded, 16)
            pool.tensor_copy(ctx_rest[:, :, :], ctx_sb[:, :, :])
            pool.tensor_copy(ctx_parts[:, 0, :, :], ctx_sb[:, :, :]).then_inc(split_step, 1)
            pool.wait_ge(split_step, 1)
            pool.tensor_tensor(ctx_rest[:, :, :], ctx_rest[:, :, :], ctx_parts[:, 0, :, :],
                               ALU.subtract).then_inc(split_step, 1)
            pool.wait_ge(split_step, 2)
            pool.tensor_copy(ctx_parts[:, 1, :, :], ctx_rest[:, :, :]).then_inc(split_step, 1)
            pool.wait_ge(split_step, 3)
            pool.tensor_tensor(ctx_rest[:, :, :], ctx_rest[:, :, :], ctx_parts[:, 1, :, :],
                               ALU.subtract).then_inc(split_step, 1)
            pool.wait_ge(split_step, 4)
            pool.tensor_copy(ctx_parts[:, 2, :, :], ctx_rest[:, :, :]).then_inc(parts_ready, 2)
            for T in range(1, TILES, 2):
                pool.wait_ge(norm2_ready, T // 8 + 1)
                if T >= 4:
                    pool.wait_ge(x2_turned, T // 2 - 1)
                pool.tensor_scalar(x2n[:, T % 4, :], xk[:, T, :], sm[:, 0, T:T + 1], sm[:, 1, T:T + 1],
                                   ALU.add, ALU.mult).then_inc(xn2_pool, 1)
            pool.wait_ge(filled, 16 * SLOT_TILES)
            for T in range(TILES):
                if T % HT == 0:
                    pool.wait_ge(routed, T // HT + 1)
                pool.wait_ge(staged, T + 1)
                for w in range(2):
                    pool.indirect_dma_start(
                        out=slot_rows, out_offset=bass.IndirectOffsetOnAxis(ap=slot[:, w, T:T + 1], axis=0),
                        in_=stage[:, T % STAGES, w, :], in_offset=None).then_inc(scattered[T % STAGES], 16)
            with pool.Fori(0, SLOT_TILES // 8) as i:
                for u in range(8):
                    pool.wait_ge(y_read, 8 * i + u + 1)
                    pool.sem_inc(passed, 1)
                    pool.indirect_dma_start(
                        out=results, out_offset=bass.IndirectOffsetOnAxis(ap=idx[:, u:u + 1], axis=0),
                        in_=ys[:, u, :], in_offset=None, bounds_check=DUMP - 1,
                        oob_is_err=False).then_inc(res_out[u], 16)

        @block.scalar
        def _(act):
            act.dma_start(ctx_sb[:, :, :], ctx.rearrange("b i d -> i b d")).then_inc(ctx_loaded, 16)
            act.dma_start(gw[:, :], gate_w).then_inc(weights_loaded, 16)
            act.wait_ge(ctx_turned, 1)
            for c in range(KC):
                act.activation(ctxT[:, c, :, :].rearrange("p b i -> p (b i)"), psC[c][:, 0:B * CTX],
                               ACT.Copy, scale=-2.0).then_inc(ctxT_ready, 1)

            def std(g):
                act.wait_ge(var_ready, g + 1)
                act.activation(sm[:, 3, 8 * g:8 * g + 8], sm[:, 2, 8 * g:8 * g + 8], ACT.Sqrt).then_inc(std_ready, 1)

            def copy_turned(n):
                act.wait_ge(turned, n + 1)
                if n >= 2:
                    act.wait_ge(dist_ready, n - 1)
                act.activation(xT[:, n % 2, 0, :, :], psT[n % 2][0][:, :, :], ACT.Copy).then_inc(xT_act, 1)

            act.wait_ge(fill_ready, 3)

            std(0)
            for g in range(4):
                if g < 3:
                    std(g + 1)
                act.wait_ge(norm_ready, g + 1)
                for k in range(8 * g, 8 * g + 5):
                    act.activation(xk[:, k, :], xk[:, k, :], ACT.Identity, scale=sm[:, 1, k:k + 1],
                                   bias=sm[:, 4, k:k + 1]).then_inc(xn_act, 1)
                copy_turned(2 * g)
                copy_turned(2 * g + 1)
            for part, rows in enumerate(PARTS):
                act.wait_ge(clipped, part + 1)
                act.activation(root[:, rows, 1:W], cost[:, rows, 1:W], ACT.Sqrt).then_inc(rooted, 1)
            for rows in PARTS:
                act.activation(inv[:, rows, 1:W], cost[:, rows, 1:W], ACT.Ln, bias=tiny[:, :]).then_inc(logged, 1)
            for part, rows in enumerate(PARTS):
                act.wait_ge(logged, part + 1)
                act.activation(inv[:, rows, 1:W], inv[:, rows, 1:W], ACT.Exp, scale=-0.5).then_inc(inverted, 1)

            for q in (1, 3):
                act.wait_ge(mask_turned, q + 1)
                src = psT[q // 2][q % 2][0:CTX, :, :].rearrange("p a b -> p (a b)").bitcast(BF16)
                act.activation(maskT[:, :, 8 * q:8 * q + 8], src.rearrange("i (k p) -> i p k", k=8),
                               ACT.Copy).then_inc(maskT_act, 1)

            def turned2(n):
                act.wait_ge(x2_turned, n + 1)
                dst = bass.AP(tensor=x2T, offset=2 * n * P, ap=[[KC * TOK, P], [TOK, KC], [1, 2 * P]])
                act.activation(dst, psT[0][n % 2][:, :, :].rearrange("p (c u) t -> p c (u t)", c=KC),
                               ACT.Copy).then_inc(x2T_ready, 1)

            def stage_tile(T):
                if T >= STAGES:
                    act.wait_ge(scattered[T % STAGES], 32 * (T // STAGES))
                act.activation(stage[:, T % STAGES, :, D:ROW], ids[:, :, T:T + 1], ACT.Copy)
                for w in range(2):
                    ins = act.activation(stage[:, T % STAGES, w, 0:D], xk[:, T, :], ACT.Identity, scale=sm[:, 1, T:T + 1],
                                         bias=sm[:, 4, T:T + 1])
                ins.then_inc(staged, 1)

            def copy_gate(k):
                act.wait_ge(gate_done, k + 1)
                if k >= 2:
                    act.wait_ge(logits_ready, k - 1)
                act.activation(by_e[:, k % 2, :], psE[k % 2], ACT.Copy).then_inc(gate_copied, 1)

            def exponentials(h):
                hs = slice(h * HT, (h + 1) * HT)
                act.wait_ge(shifted, h + 1)
                act.activation(orig[:, hs, :], t1[:, hs, :], ACT.Exp).then_inc(expd, 1)

            for g in range(4):
                act.wait_ge(var2_ready, g + 1)
                act.activation(sm[:, 3, 8 * g:8 * g + 8], sm[:, 2, 8 * g:8 * g + 8], ACT.Sqrt).then_inc(std2_ready, 1)
                act.wait_ge(norm2_ready, g + 1)
                for n in range(4 * g, 4 * g + 4):
                    T = 2 * n
                    act.activation(x2n[:, T % 4, :], xk[:, T, :], ACT.Identity, scale=sm[:, 1, T:T + 1],
                                   bias=sm[:, 4, T:T + 1]).then_inc(xn2_act, 1)
                    if n:
                        turned2(n - 1)
                    if n % 2 == 0 and n >= 4:
                        copy_gate(n // 2 - 2)
                    if n == 12:
                        exponentials(0)
            turned2(TILES // 2 - 1)
            copy_gate(6)
            copy_gate(7)
            act.wait_ge(const_ready, 7)
            act.wait_ge(x2_turned, TILES // 2)
            for T in range(STAGES):
                if T == 2:
                    exponentials(1)
                stage_tile(T)
            def shared_silu_half(g, m):
                act.wait_ge(h_ready, 2 * g + m + 1)
                if g >= 2:
                    act.wait_ge(z_ready, 2 * (g - 1))
                act.activation(silu[:, g % 2, m, :], psT[m][0][:, :, :].rearrange("p a b -> p (a b)"), ACT.Silu,
                               bias=sb1[:, m:m + 1]).then_inc(silu_ready, 1)

            act.wait_ge(shared_small, 96)
            for g in range(2):
                for m in range(MS):
                    shared_silu_half(g, m)
            for g in range(2, EARLY):
                for m in range(MS):
                    for T in staged_by(2 * g + m):
                        stage_tile(T)
                    shared_silu_half(g, m)

            def act_step_of(i, c):
                q = 8 * i + c
                if live(i, c - 1):
                    act.wait_ge(hb_ready, q)
                    if not head(i, c - 3):
                        act.wait_ge(gated, q - 2)
                    act.activation(sg[:, (c - 1) % 2, :], hb[:, (c - 1) % 2, 0:I], ACT.Silu).then_inc(silu_done, 1)
                if live(i, c + 1):
                    act.wait_ge(x_turned, q + 2)
                    if not head(i, c - 1):
                        act.wait_ge(h_done, q)
                    act.activation(xsT[:, (c + 1) % 2, :, :].rearrange("p c t -> p (c t)"),
                                   psX[(c + 1) % 2], ACT.Copy).then_inc(xT_copied, 1)
                if live(i, c - 2):
                    act.wait_ge(g_turned, q - 1)
                    if not head(i, c - 4):
                        act.wait_ge(y_done, q - 3)
                    act.activation(hgT[:, c % 2, :], psG[c % 2], ACT.Copy).then_inc(hgT_copied, 1)

            pipeline(act, act_step_of)
            for g in range(EARLY, 8):
                for m in range(MS):
                    shared_silu_half(g, m)

        @block.tensor
        def _(pe):
            pe.wait_ge(const_ready, 2)
            pe.wait_ge(ctx_loaded, 16)
            for c in range(KC):
                for b in range(B):
                    mm = pe.transpose(psC[c][:, b * CTX:(b + 1) * CTX], ctx_sb[:, b, c * P:(c + 1) * P],
                                      ident[0:CTX, 0:CTX])
            mm.then_inc(ctx_turned, 1)
            pe.wait_ge(weights_loaded, 16)
            for c in range(KC):
                mm = pe.transpose(psD[0][:, c, 0:E], gw[:, c * P:(c + 1) * P], ident[0:E, 0:E])
            mm.then_inc(gate_turned, 1)
            pe.wait_ge(aa_ready, 1)
            pe.wait_ge(ctxT_ready, KC)
            for b in range(B):
                mm = pe.matmul(psC[0][QUAD * b:QUAD * b + QUAD, 0:CTX], ones[0:CTX, :], aa_diag[:, b, :],
                               start=True, stop=True)
            mm.then_inc(aa_spread, 1)

            def warm_up(n):
                for _ in range(n):
                    pe.matmul(psT[1][1][:, :, :].rearrange("p a b -> p (a b)"), onesb[:, :],
                              onesb[:, :].unsqueeze(1).to_broadcast([P, 4, P]), start=True, stop=True)

            def turn(n):
                g, h = n // 2, n % 2
                pe.wait_ge(xn_act, 5 * g + (4 if h == 0 else 5))
                if h == 1:
                    pe.wait_ge(xn_pool, 3 * g + 3)
                if n >= 2:
                    pe.wait_ge(xT_act, n - 1)
                    pe.wait_ge(xT_dve, n - 1)
                for c in range(KC):
                    for k in range(4):
                        mm = pe.transpose(psT[h][c][:, k, :], xk[:, 4 * n + k, c * P:(c + 1) * P], ident[:, :])
                mm.then_inc(turned, 1)

            def distances(n):
                h = n % 2
                pe.wait_ge(xT_act, n + 1)
                pe.wait_ge(xT_dve, n + 1)
                if n == 0:
                    pe.wait_ge(gate_ready, 1)
                if n >= 2:
                    pe.wait_ge(dist_used, n - 1)
                for k in range(4):
                    for b in range(B):
                        for c in range(KC):
                            mm = pe.matmul(psD[h][QUAD * b:QUAD * b + QUAD, k, 0:CTX],
                                           xT[:, h, c, k, QUAD * b:QUAD * b + QUAD], ctxT[:, c, b, :],
                                           start=(c == 0), stop=(c == KC - 1))
                mm.then_inc(dist_ready, 1)

            for n in range(8):
                turn(n)
                if n >= 1:
                    distances(n - 1)
            distances(7)

            pe.wait_ge(dist_used, 8)
            pe.wait_ge(mask_ready, 2)
            warm_up(16)
            pe.wait_ge(mask_in, 16 * B)
            pe.wait_ge(xT_act, 8)
            pe.wait_ge(xT_dve, 8)
            for q in range(4):
                dst = psT[q // 2][q % 2][0:CTX, :, :].rearrange("p a b -> p (a b)").bitcast(BF16)
                for k in range(8):
                    mm = pe.transpose(dst[:, k * P:(k + 1) * P], maskU[:, :, 8 * q + k], identb[:, :])
                mm.then_inc(mask_turned, 1)
            def gather(n):
                if n >= 2:
                    pe.wait_ge(x2_ready, n - 1)
                for u in range(2):
                    T = 2 * n + u
                    b, j = T // 8, T % 8
                    lhs = maskT[:, 32 * b + 4 * j:32 * b + 4 * j + 4, :].rearrange("i p k -> i (p k)")
                    for part in range(3):
                        mm = pe.matmul(psC[n % 2][:, u * D:(u + 1) * D], lhs, ctx_parts[:, part, b, :],
                                       start=(part == 0), stop=(part == 2))
                mm.then_inc(gathered, 1)

            def gate(k):
                pe.wait_ge(x2T_ready, 2 * k + 2)
                if k >= 2:
                    pe.wait_ge(gate_copied, k - 1)
                for c in range(KC):
                    mm = pe.matmul(psE[k % 2], gwT[:, c, :], x2T[:, c, 512 * k:512 * k + 512],
                                   start=(c == 0), stop=(c == KC - 1))
                mm.then_inc(gate_done, 1)

            def logits(k):
                pe.wait_ge(gate_copied, k + 1)
                for T in range(4 * k, 4 * k + 4):
                    mm = pe.transpose(psL[T // HT][:, T % HT, :], by_e[:, k % 2, (T % 4) * P:(T % 4 + 1) * P],
                                      ident[0:E, 0:E])
                mm.then_inc(logits_ready, 1)

            def turn2(n):
                pe.wait_ge(xn2_act, n + 1)
                pe.wait_ge(xn2_pool, n + 1)
                if n >= 2:
                    pe.wait_ge(x2T_ready, n - 1)
                for u in range(2):
                    for c in range(KC):
                        mm = pe.transpose(psT[0][n % 2][:, 2 * c + u, :], x2n[:, (2 * n + u) % 4, c * P:(c + 1) * P],
                                          ident[:, :])
                mm.then_inc(x2_turned, 1)

            pe.wait_ge(maskT_ready, 2)
            pe.wait_ge(maskT_act, 2)
            pe.wait_ge(parts_ready, 3)
            for n in range(4):
                gather(n)
            warm_up(8)
            for n in range(4, 8):
                gather(n)
            for n in range(TILES // 2):
                turn2(n)
                if n + 8 < TILES // 2:
                    gather(n + 8)
                if n % 2 and n >= 3:
                    gate(n // 2 - 1)
                    if n >= 5:
                        logits(n // 2 - 2)
            gate(7)
            for k in (6, 7):
                logits(k)
            def shared_h(g, ms=range(MS)):
                for m in ms:
                    if g >= 1:
                        pe.wait_ge(act_ready, 2 * g + m - 1)
                    for w, ps_ in ((sw1, psT[m][0]), (sw3, psT[m][1])):
                        for c in range(KC):
                            mm = pe.matmul(ps_[:, :, :].rearrange("p a b -> p (a b)"), w[:, c, m * P:(m + 1) * P],
                                           x2T[:, c, 512 * g:512 * g + 512], start=(c == 0), stop=(c == KC - 1))
                    mm.then_inc(h_ready, 1)

            def shared_z(g):
                pe.wait_ge(act_ready, 2 * g + 2)
                for j in range(2):
                    if g >= 1:
                        pe.wait_ge(z_used, 2 * (g - 1) + j + 1)
                    for u in range(2):
                        for m in range(MS):
                            mm = pe.matmul(psC[j][:, u * D:(u + 1) * D],
                                           silu[:, g % 2, m, (2 * j + u) * P:(2 * j + u + 1) * P], sw2[:, m, :],
                                           start=(m == 0), stop=(m == MS - 1))
                    mm.then_inc(z_ready, 1)

            pe.wait_ge(shared_small, 96)
            shared_h(0)
            shared_h(1, [0])
            pe.wait_ge(oh_ready, 2)
            pe.matmul(psD[1][:, :, :].rearrange("p a b -> p (a b)"), not_before[:, :],
                      ohb[:, :, :].rearrange("p t e -> p (t e)"), start=True, stop=True)
            pe.matmul(psC[0][:, :].rearrange("p (e t) -> p e t", e=E), onesb[:, :],
                      ohb[:, :, :].rearrange("p t e -> p e t"),
                      start=True, stop=True).then_inc(counted, 1)
            for g in range(1, EARLY):
                shared_h(g, [1] if g == 1 else range(MS))
                if g == 1:
                    pe.wait_ge(counts_read, 1)
                shared_z(g - 1)
            shared_z(EARLY - 1)

            pe_expert = [pe.alloc_register(f"pe_expert{u}") for u in range(4)]

            def pe_step_of(i, c):
                q = 8 * i + c
                if live(i, c + 1):
                    r = c + 1
                    pe.wait_ge(xs_loaded[r % 4], 16 * (2 * i + r // 4 + 1))
                    if not head(i, r - 2):
                        pe.wait_ge(xT_copied, q)
                    for k in range(KC):
                        mm = pe.transpose(psX[r % 2][:, k * P:(k + 1) * P], xs[:, r % 4, k * P:(k + 1) * P], ident[:, :])
                    mm.then_inc(x_turned, 1)
                if live(i, c - 2):
                    pe.wait_ge(gated, q - 1)
                    if not head(i, c - 4):
                        pe.wait_ge(hgT_copied, q - 3)
                    pe.transpose(psG[c % 2], hg[:, c % 2, :], ident[:, :]).then_inc(g_turned, 1)
                if live(i, c):
                    e = expert(pe, pe_expert, c)
                    pe.wait_ge(xT_copied, q + 1)
                    if not head(i, c - 2):
                        pe.wait_ge(hb_ready, q - 1)
                    for k in range(KC):
                        mm = pe.matmul(psH[c % 2], xsT[:, c % 2, k, :], w13f[:, bass.ds(k * E * 2 * I + e, 2 * I)],
                                       start=(k == 0), stop=(k == KC - 1))
                    mm.then_inc(h_done, 1)
                if live(i, c + 1):
                    load_expert(pe, pe_expert, i, c + 1)
                if live(i, c - 2):
                    e = expert(pe, pe_expert, c - 2)
                    pe.wait_ge(hgT_copied, q - 1)
                    if not head(i, c - 4):
                        pe.wait_ge(y_read, q - 3)
                    pe.matmul(psY[c % 2], hgT[:, c % 2, :], w2f[:, bass.ds(e, D)],
                              start=True, stop=True).then_inc(y_done, 1)

            pe.wait_ge(etab_ready, 1)
            pe.wait_ge(expert_weights_loaded, 80)
            pe.wait_ge(z_used, 2 * EARLY)
            pipeline(pe, pe_step_of)
            pe.wait_ge(y_read, SLOT_TILES)
            pe.wait_ge(hgT_copied, SLOT_TILES)
            for g in range(EARLY, 8):
                shared_h(g)
                shared_z(g)

        @block.vector
        def _(dve):
            done = [0]

            def link(ins):
                done[0] += 1
                ins.then_inc(dve_step, 1)
                dve.wait_ge(dve_step, done[0])

            def start(ins):
                done[0] += 1
                ins.then_inc(dve_step, 1)

            def settle():
                dve.wait_ge(dve_step, done[0])

            def moments(g, ready):
                s = slice(8 * g, 8 * g + 8)
                me, m2e, mo, m2o = (stats[:, s, i] for i in (1, 2, 4, 5))
                dve.tensor_tensor(sm[:, 5, s], me, mo, ALU.subtract)
                dve.tensor_tensor(sm[:, 6, s], m2e, m2o, ALU.add)
                link(dve.tensor_tensor(sm[:, 7, s], me, mo, ALU.add))
                dve.tensor_scalar(sm[:, 0, s], sm[:, 7, s], -0.5, None, ALU.mult)
                link(dve.tensor_tensor(sm[:, 5, s], sm[:, 5, s], sm[:, 5, s], ALU.mult))
                link(dve.scalar_tensor_tensor(out=sm[:, 6, s], in0=sm[:, 5, s], scalar=D / 4.0, in1=sm[:, 6, s],
                                              op0=ALU.mult, op1=ALU.add))
                dve.tensor_scalar(sm[:, 2, s], sm[:, 6, s], 1.0 / D, EPS, ALU.mult, ALU.add).then_inc(ready, 1)

            def statistics(g):
                dve.wait_ge(x_loaded[g], 16)
                for k in range(8 * g, 8 * g + 8):
                    ins = dve.bn_stats(stats[:, k, :], xk[:, k, :])
                link(ins)
                moments(g, var_ready)

            def inverse_root(g):
                s = slice(8 * g, 8 * g + 8)
                v, sd, r, t = sm[:, 2, s], sm[:, 3, s], sm[:, 1, s], sm[:, 8, s]
                link(dve.reciprocal(r, sd))
                link(dve.tensor_tensor(t, r, r, ALU.mult))
                link(dve.tensor_tensor(t, t, v, ALU.mult))
                link(dve.tensor_scalar(t, t, -0.5, 1.5, ALU.mult, ALU.add))
                link(dve.tensor_tensor(r, r, t, ALU.mult))

            def norms(g):
                s = slice(8 * g, 8 * g + 8)
                r, t = sm[:, 1, s], sm[:, 8, s]
                dve.wait_ge(std_ready, g + 1)
                inverse_root(g)
                link(dve.tensor_tensor(t, r, r, ALU.mult))
                dve.tensor_tensor(sm[:, 9, s], sm[:, 6, s], t, ALU.mult)
                dve.tensor_tensor(sm[:, 4, s], sm[:, 0, s], r, ALU.mult).then_inc(norm_ready, 1)

            def copy_turned(n):
                dve.wait_ge(turned, n + 1)
                if n >= 2:
                    dve.wait_ge(dist_ready, n - 1)
                dve.tensor_copy(xT[:, n % 2, 1, :, :], psT[n % 2][1][:, :, :]).then_inc(xT_dve, 1)

            def squared(n):
                dve.wait_ge(dist_ready, n + 1)
                for k in range(4):
                    kk = 4 * n + k
                    ins = dve.scalar_tensor_tensor(out=cost[:, :, 1 + kk], in0=psD[n % 2][:, k, 0:CTX],
                                                   scalar=sm[:, 9, kk:kk + 1], in1=aa_row[:, :],
                                                   op0=ALU.add, op1=ALU.add)
                ins.then_inc(dist_used, 1)

            dve.wait_ge(const_ready, 2)
            dve.tensor_copy(identb[:, :], ident[:, :]).then_inc(parts_ready, 1)
            dve.tensor_reduce(first_chunk[:, :], ident[:, 0:P:QUAD], AX.X, ALU.add)
            link(dve.tensor_reduce(last_chunk[:, :], ident[:, QUAD - 1:P:QUAD], AX.X, ALU.add))
            link(dve.memset(cost[:, :, 0:1], BIG))
            link(dve.tensor_scalar(cost[:, :, 0:1], cost[:, :, 0:1], first_chunk[:, :], None, ALU.mult))
            link(dve.memset(cost[:, 0, 0:1], 0.0))
            dve.memset(R[:, 0, :], BIG)
            dve.memset(carry[:, 0:1], BIG)
            dve.memset(A[:, NT, 0:CH], 0.0)
            link(dve.memset(A[:, :, CH:W], 1.0))
            dve.tensor_scalar(A[:, :, CH:W], A[:, :, CH:W], last_chunk[:, :], None, ALU.mult)
            link(dve.tensor_scalar(carry[:, 0:1], carry[:, 0:1], 1.0, None, ALU.mult))
            for b in range(B):
                dve.memset(carry[QUAD * b:QUAD * b + 1, 0:1], 0.0)
            dve.wait_ge(ctx_loaded, 16)
            for b in range(B):
                ins = dve.tensor_tensor_reduce(out=ctx_rest[:, b, :], in0=ctx_sb[:, b, :], in1=ctx_sb[:, b, :],
                                               scale=1.0, scalar=0.0, op0=ALU.mult, op1=ALU.add,
                                               accum_out=aa[:, b:b + 1])
            link(ins)
            for b in range(B):
                ins = dve.tensor_scalar(aa_diag[:, b, :], ident[0:CTX, 0:CTX], aa[:, b:b + 1], None, ALU.mult)
            ins.then_inc(aa_ready, 1)
            statistics(0)
            dve.wait_ge(gate_turned, 1)
            for c in range(KC):
                ins = dve.tensor_copy(gwT[:, c, :], psD[0][:, c, 0:E])
            ins.then_inc(gate_ready, 1)
            dve.wait_ge(aa_spread, 1)
            link(dve.tensor_copy(aa_row[:, :], psC[0][:, 0:CTX]))

            norms(0)
            statistics(1)
            for g in range(4):
                if g + 1 < 4:
                    norms(g + 1)
                if g + 2 < 4:
                    statistics(g + 2)
                copy_turned(2 * g)
                if g:
                    squared(2 * g - 1)
                copy_turned(2 * g + 1)
                squared(2 * g)
            squared(7)
            dve.wait_ge(dist_used, 8)
            for rows in PARTS:
                dve.tensor_scalar(cost[:, rows, 1:W], cost[:, rows, 1:W], 0.0, None, ALU.max).then_inc(clipped, 1)
            for part, rows in enumerate(PARTS):
                c, r, d = (m[:, rows, 1:W] for m in (cost, root, rest))
                dve.wait_ge(rooted, part + 1)
                dve.wait_ge(clipped, part + 1)
                link(dve.tensor_tensor(d, r, r, ALU.mult))
                link(dve.tensor_tensor(d, c, d, ALU.subtract))
            for part, rows in enumerate(PARTS):
                c, r, d, i = (m[:, rows, 1:W] for m in (cost, root, rest, inv))
                dve.wait_ge(inverted, part + 1)
                link(dve.tensor_tensor(d, d, i, ALU.mult))
                dve.scalar_tensor_tensor(out=c, in0=d, scalar=0.5, in1=r, op0=ALU.mult,
                                         op1=ALU.add).then_inc(cost_ready, 1)

            dve.wait_ge(pads_zeroed, 16 * ((NT + 15) // 16))
            link(dve.memset(M[:, :, 0:1], BIG))
            def left_wins(t):
                dve.tensor_tensor(M[:, t, 1:W], R[:, t + 1, 0:CH], M[:, t, 1:W], ALU.is_lt)

            right = [QUAD - 1] + list(range(QUAD - 1))
            for t in range(NT):
                if t == 0 or t == CUT:
                    dve.wait_ge(cost_in, 16 if t == 0 else 32)
                start(dve.tensor_tensor(M[:, t, 1:W], R[:, t, 0:CH], R[:, t, 1:W], ALU.min))
                dve.tensor_tensor(F[:, t, 1:W], R[:, t, 0:CH], R[:, t, 1:W], ALU.is_le)
                settle()
                start(dve.tensor_tensor_scan(R[:, t + 1, :], M[:, t, :], cst[:, t, :], carry[:, t:t + 1],
                                             ALU.min, ALU.add))
                if t:
                    left_wins(t - 1)
                settle()
                if t + 1 < NT:
                    dve.stream_shuffle(carry[:, t + 1:t + 2], R[:, t + 1, CH:W], right)
                if t == 0:
                    link(dve.memset(R[:, 1, 0:1], BIG))
            left_wins(NT - 1)
            dve.memset(carry[:, NT:NT + 1], 0.0)
            link(dve.memset(cst[:, :, CH:W], 1.0))

            def flags(t):
                return dve.scalar_tensor_tensor(out=cst[:, t, 0:CH], in0=F[:, t, 1:W], scalar=0.5, in1=M[:, t, 1:W],
                                                op0=ALU.mult, op1=ALU.max)

            left = list(range(1, QUAD)) + [0]
            link(flags(NT - 1))

            def rev(tns, t):
                return bass.AP(tensor=tns, offset=t * W + CH, ap=[[tns.shape[1] * W, P], [-1, W]])

            def path(t):
                return dve.scalar_tensor_tensor(out=mask[:, t, :], in0=V[:, t, 1:W], scalar=1.0,
                                                in1=A[:, t + 1, 0:CH], op0=ALU.is_ge, op1=ALU.subtract)

            for t in range(NT - 1, -1, -1):
                start(dve.tensor_tensor_scan(rev(V, t), rev(cst, t), rev(A, t + 1), carry[:, t + 1:t + 2],
                                             ALU.mult, ALU.max))
                if t:
                    flags(t - 1)
                settle()
                if t:
                    dve.stream_shuffle(carry[:, t:t + 1], V[:, t, 0:1], left)
                    start(dve.scalar_tensor_tensor(out=A[:, t, 0:CH], in0=cst[:, t, 0:CH], scalar=0.5,
                                                   in1=V[:, t, 0:CH], op0=ALU.mult, op1=ALU.is_lt))
                ins = path(t)
                if t:
                    settle()
                if t in (NT // 2, 0):
                    ins.then_inc(mask_ready, 1)

            for q in (0, 2):
                dve.wait_ge(mask_turned, q + 1)
                src = psT[q // 2][q % 2][0:CTX, :, :].rearrange("p a b -> p (a b)").bitcast(BF16)
                dve.tensor_copy(maskT[:, :, 8 * q:8 * q + 8], src.rearrange("i (k p) -> i p k", k=8)
                                ).then_inc(maskT_ready, 1)
            def statistics2(g):
                dve.wait_ge(x2_ready, 4 * g + 4)
                for T in range(8 * g, 8 * g + 8):
                    ins = dve.bn_stats(stats[:, T, :], xk[:, T, :])
                link(ins)
                moments(g, var2_ready)

            def norms2(g):
                dve.wait_ge(std2_ready, g + 1)
                inverse_root(g)
                s = slice(8 * g, 8 * g + 8)
                dve.tensor_tensor(sm[:, 4, s], sm[:, 0, s], sm[:, 1, s], ALU.mult).then_inc(norm2_ready, 1)

            dve.wait_ge(x_nat, 64)
            for n in range(TILES // 2):
                g = n // 4
                dve.wait_ge(gathered, n + 1)
                pair = xk[:, 2 * n:2 * n + 2, :].rearrange("p t d -> p (t d)")
                dve.tensor_tensor(pair, psC[n % 2][:, :], pair, ALU.add).then_inc(x2_ready, 1)
                if n % 4 == 1 and g:
                    norms2(g - 1)
                if n % 4 == 3:
                    statistics2(g)
            norms2(3)

            def shared_act(g):
                for m in range(MS):
                    dve.wait_ge(silu_ready, 2 * g + m + 1)
                    dve.scalar_tensor_tensor(out=silu[:, g % 2, m, :],
                                             in0=psT[m][1][:, :, :].rearrange("p a b -> p (a b)"),
                                             scalar=sb3[:, m:m + 1], in1=silu[:, g % 2, m, :],
                                             op0=ALU.add, op1=ALU.mult).then_inc(act_ready, 1)

            def choose(h):
                hs = slice(h * HT, (h + 1) * HT)
                HE = HT * E
                flat = slice(h * HE, (h + 1) * HE)

                def over_e(ap):
                    return ap.unsqueeze(2).to_broadcast([P, HT, E])

                def line(a):
                    return a[:, hs, :].rearrange("p t e -> p (t e)")

                a1, a2, a3, po, sc = (a[:, hs, :] for a in (t1, t2, t3, orig, score))
                top_, sum_ = r1[:, hs], r2[:, hs]
                dve.wait_ge(logits_ready, (h + 1) * HT // 4)
                link(dve.tensor_reduce(top_, psL[h], AX.X, ALU.max))
                dve.tensor_tensor(a1, psL[h], over_e(top_), ALU.subtract).then_inc(shifted, 1)
                dve.wait_ge(expd, h + 1)
                link(dve.tensor_reduce(sum_, po, AX.X, ALU.add))
                link(dve.reciprocal(sum_, sum_))
                link(dve.tensor_tensor(po, po, over_e(sum_), ALU.mult))
                link(dve.tensor_tensor(sc, po, gb[:, :].unsqueeze(1).to_broadcast([P, HT, E]), ALU.add))
                pr = sc.rearrange("p t (h two) -> p (t h) two", two=2)
                hi, lo = (line(a)[:, 0:HE // 2] for a in (t1, t2))
                dve.tensor_tensor(hi, pr[:, :, 0], pr[:, :, 1], ALU.max)
                link(dve.tensor_tensor(lo, pr[:, :, 0], pr[:, :, 1], ALU.min))
                hi2, lo2 = (a.rearrange("p (g two) -> p g two", two=2) for a in (hi, lo))
                gsf, gkf, gpf = (line(a) for a in (gs, gk, gp))
                dve.tensor_tensor(gsf, hi2[:, :, 0], hi2[:, :, 1], ALU.max)
                dve.tensor_tensor(gkf, hi2[:, :, 0], hi2[:, :, 1], ALU.min)
                link(dve.tensor_tensor(gpf, lo2[:, :, 0], lo2[:, :, 1], ALU.max))
                link(dve.tensor_tensor(gkf, gkf, gpf, ALU.max))
                link(dve.tensor_tensor(gsf, gsf, gkf, ALU.add))
                sq = [P, HT, G, G]
                other = gs[:, hs, :].unsqueeze(2).to_broadcast(sq)
                own = gs[:, hs, :].unsqueeze(3).to_broadcast(sq)
                v4 = [a.rearrange("p t (g h) -> p t g h", g=G) for a in (a1, a2)]
                low4 = low_e[:, :, :].unsqueeze(1).to_broadcast(sq)
                dve.tensor_tensor(v4[0], other, own, ALU.is_gt)
                link(dve.tensor_tensor(v4[1], other, own, ALU.is_equal))
                link(dve.tensor_tensor(v4[1], v4[1], low4, ALU.mult))
                link(dve.tensor_tensor(v4[0], v4[0], v4[1], ALU.add))
                link(dve.tensor_reduce(gk[:, hs, :], v4[0], AX.X, ALU.add))
                link(dve.tensor_scalar(gkf, gkf, 1.5, None, ALU.is_lt))
                dve.tensor_scalar(gpf, gkf, -1.0, BIG, ALU.add, ALU.mult)
                sc4, t34 = (a.rearrange("p t (g h) -> p (t g) h", g=G) for a in (sc, a3))
                g4 = [P, HT * G, E // G]
                link(dve.tensor_tensor(t34, sc4, gkf.unsqueeze(2).to_broadcast(g4), ALU.mult))
                link(dve.tensor_tensor(t34, t34, gpf.unsqueeze(2).to_broadcast(g4), ALU.add))
                rev = rev_e[:, :].unsqueeze(1).to_broadcast([P, HT, E])
                for w, oh in enumerate((oh1, oh2)):
                    if h == 1 and w == 1:
                        shared_act(0)
                    link(dve.tensor_reduce(top_, a3, AX.X, ALU.max))
                    link(dve.tensor_tensor(a1, a3, over_e(top_), ALU.is_equal))
                    link(dve.tensor_tensor(a1, a1, rev, ALU.mult))
                    link(dve.tensor_reduce(top_, a1, AX.X, ALU.max))
                    link(dve.tensor_tensor(oh[:, hs, :], a1, over_e(top_), ALU.is_equal))
                    if w == 0:
                        link(dve.scalar_tensor_tensor(out=line(t3), in0=line(oh), scalar=-4.0 * BIG, in1=line(t3),
                                                      op0=ALU.mult, op1=ALU.add))
                dve.tensor_tensor(ohb[:, hs, :], oh1[:, hs, :], oh2[:, hs, :], ALU.add).then_inc(oh_ready, 1)

            dve.wait_ge(shared_small, 96)
            dve.wait_ge(const_ready, 7)
            choose(0)
            choose(1)

            dve.memset(keep_on[:, :, :], 1.0)
            link(dve.memset(one_e[:, :], 1.0))
            link(dve.memset(keep_on[:, :, 0:1], 0.0))
            dve.wait_ge(counted, 1)
            dve.tensor_tensor_scan(upto[:, :, :].rearrange("p e t -> p (e t)"),
                                   keep_on[:, :, :].rearrange("p e t -> p (e t)"), psC[0][:, :], 0.0,
                                   ALU.mult, ALU.add).then_inc(counts_read, 1)
            dve.wait_ge(counts_read, 1)
            link(dve.tensor_scalar(te[:, :], upto[:, :, TILES - 1:TILES].rearrange("p e t -> p (e t)"),
                                   (P - 1) / 2.0, 1.0 / P, ALU.add, ALU.mult))
            link(dve.tensor_scalar(te[:, :], te[:, :], ROUND, None, ALU.add))
            link(dve.tensor_scalar(te[:, :], te[:, :], -ROUND, None, ALU.add))
            link(dve.tensor_tensor_scan(tend[:, :], one_e[:, :], te[:, :], 0.0, ALU.mult, ALU.add))
            link(dve.tensor_tensor(tbase[:, :], tend[:, :], te[:, :], ALU.subtract))
            link(dve.tensor_scalar(tbase[:, :], tbase[:, :], float(P), None, ALU.mult))
            link(dve.tensor_tensor(upto[:, :, :], upto[:, :, :],
                                   tbase[:, :].unsqueeze(2).to_broadcast([P, E, TILES]), ALU.add))
            rank = psD[1][:, :, :].rearrange("p a b -> p (a b)").rearrange("p (t e) -> p t e", e=E)
            for h in range(2):
                hs = slice(h * HT, (h + 1) * HT)
                link(dve.tensor_tensor(t3[:, hs, :], rank[:, hs, :], upto[:, :, hs].rearrange("p e t -> p t e"),
                                       ALU.add))
                for w, oh in enumerate((oh1, oh2)):
                    a, r = (t1, t2)[w], (r1, r2)[w]
                    link(dve.tensor_tensor(a[:, hs, :], t3[:, hs, :], oh[:, hs, :], ALU.mult))
                    link(dve.tensor_reduce(r[:, hs], a[:, hs, :], AX.X, ALU.add))
                    ins = dve.tensor_copy(slot[:, w, hs], r[:, hs])
                ins.then_inc(routed, 1)
            shared_act(1)
            for w, oh in enumerate((oh1, oh2)):
                link(dve.tensor_tensor(t2[:, :, :], orig[:, :, :], oh[:, :, :], ALU.mult))
                link(dve.tensor_reduce(wt[:, w, :], t2[:, :, :], AX.X, ALU.add))
            sq = [P, SLOT_TILES, E]
            link(dve.tensor_tensor(big_e[:, :, :], tend[:, :].unsqueeze(1).to_broadcast(sq),
                                   tile_no[:, :].unsqueeze(2).to_broadcast(sq), ALU.is_le))
            link(dve.tensor_reduce(tmp[:, 0:SLOT_TILES], big_e[:, :, :], AX.X, ALU.add))
            dve.tensor_scalar(etab[:, :], tmp[:, 0:SLOT_TILES], float(E - 1), float(D),
                              ALU.min, ALU.mult).then_inc(etab_ready, 1)

            def shared_add(g):
                dve.wait_ge(staged, 4 * g + 4)
                for j in range(2):
                    n = 2 * g + j
                    dve.wait_ge(z_ready, n + 1)
                    if n:
                        dve.wait_ge(z_used, n)
                    pair = xk[:, 2 * n:2 * n + 2, :]
                    link(dve.tensor_tensor(tmp[:, :].rearrange("p (t d) -> p t d", t=2),
                                           psC[j][:, :].rearrange("p (t d) -> p t d", t=2),
                                           bs2b[:, :].unsqueeze(1).to_broadcast([P, 2, D]), ALU.add))
                    dve.tensor_tensor(pair.rearrange("p t d -> p (t d)"), tmp[:, :],
                                      pair.rearrange("p t d -> p (t d)"), ALU.add).then_inc(z_used, 1)

            dve.wait_ge(etab_ready, 1)
            dve.wait_ge(bs2_loaded, 16)
            for g in range(2, EARLY):
                shared_add(g - 2)
                shared_act(g)
            shared_add(EARLY - 2)
            shared_add(EARLY - 1)

            dve_expert = [dve.alloc_register(f"dve_expert{u}") for u in range(4)]

            def dve_step_of(i, c):
                q = 8 * i + c
                if live(i, c - 3):
                    r = c - 3
                    e = expert(dve, dve_expert, r)
                    dve.wait_ge(y_done, q - 2)
                    if not head(i, r - 8):
                        dve.wait_ge(res_out[r % 8], 16 * (i + r // 8))
                    dve.tensor_tensor(ys[:, r % 8, :], psY[r % 2], b2f[:, bass.ds(e, D)],
                                      ALU.add).then_inc(y_read, 1)
                if live(i, c - 1):
                    r = c - 1
                    dve.wait_ge(silu_done, q)
                    if not head(i, r - 2):
                        dve.wait_ge(g_turned, q - 2)
                    dve.tensor_tensor(hg[:, r % 2, :], sg[:, r % 2, :], hb[:, r % 2, I:2 * I],
                                      ALU.mult).then_inc(gated, 1)
                if live(i, c):
                    e = expert(dve, dve_expert, c)
                    dve.wait_ge(xs_loaded[c % 4], 16 * (2 * i + c // 4 + 1))
                    if not head(i, c - 8):
                        dve.wait_ge(res_out[c % 8], 16 * (i + c // 8))
                    dve.tensor_copy(idx[:, c % 8:c % 8 + 1], xs[:, c % 4, D:ROW]).then_inc(id_copied, 1)
                    dve.wait_ge(h_done, q + 1)
                    if not head(i, c - 2):
                        dve.wait_ge(gated, q - 1)
                    dve.tensor_tensor(hb[:, c % 2, :], psH[c % 2], b13f[:, bass.ds(e, 2 * I)],
                                      ALU.add).then_inc(hb_ready, 1)
                if live(i, c + 1):
                    load_expert(dve, dve_expert, i, c + 1)

            dve.wait_ge(biases_loaded, 48)
            pipeline(dve, dve_step_of)
            def combine(g):
                dve.wait_ge(tail_in[g % 4], 16 * (g // 4 + 1))
                for w in range(2):
                    for T in range(4 * g, 4 * g + 4):
                        ins = dve.scalar_tensor_tensor(out=xk[:, T, :], in0=back[:, g % 4, T % 4, w, :],
                                                       scalar=wt[:, w, T:T + 1], in1=xk[:, T, :],
                                                       op0=ALU.mult, op1=ALU.add)
                    if w == 0:
                        link(ins)
                ins.then_inc(combined, 1)

            for g in range(EARLY, 8):
                shared_act(g)
                combine(g - EARLY)
                shared_add(g)
            for g in range(8 - EARLY, 8):
                combine(g)


def kernel(**inputs):
    import numpy as _np
    import concourse.bacc as _bacc
    from concourse import mybir as _mybir
    from concourse.bass_utils import run_bass_kernel_spmd as _run

    nc = _bacc.Bacc("TRN2", target_bir_lowering=False, num_devices=1)
    arrays, args = {}, []
    names = ["x", "ctx_1024"] + ["L0_ffn_" + n for n in (
        "gate_w gate_b We1 be1 We2 be2 We3 be3 ws1 bs1 ws2 bs2 ws3 bs3").split()]
    for name in names:
        a = _np.ascontiguousarray(inputs[name])
        arrays[f"in_{name}"] = a
        args.append(nc.dram_tensor(f"in_{name}", a.shape, _mybir.dt.from_np(a.dtype), kind="ExternalInput").ap())
    out = nc.dram_tensor("out_0", (4, 1024, 256), _mybir.dt.float32, kind="ExternalOutput").ap()
    build(nc, *args, out)
    r = _run(nc, [arrays], core_ids=[0])
    return r.results[0]["out_0"]
```
